# Optimizing a Trainium2 kernel written in Bass

```python
import numpy as np
import jax
import jax.numpy as jnp

def _softmax(x, axis=-1):
    return jax.nn.softmax(x, axis=axis)

def _gelu(x):
    return jax.nn.gelu(x, approximate=True)

def _silu(x):
    return jax.nn.silu(x)

def _sigmoid(x):
    return jax.nn.sigmoid(x)

def _layernorm(x, axis=-1, eps=1e-05):
    m = jnp.mean(x, axis=axis, keepdims=True)
    v = jnp.var(x, axis=axis, keepdims=True)
    return (x - m) / jnp.sqrt(v + eps)

def _scatter_add(tgt, idx, src, axis=0):
    return tgt.at[idx].add(src)

def _segment_sum(src, seg, n):
    return jax.ops.segment_sum(src, seg, n)
kernel_name = 'mk_decoder_preln_d1_seqx_r4_17bcbd'

def setup_inputs(seed: int=0):
    np.random.seed(seed)
    _w = jnp.asarray

    def _rec_inputs():
        import jax
        import jax.numpy as jnp
        _rk = jax.random.key(seed)
        x = -0.0002928 + 1 * jax.random.normal(jax.random.fold_in(_rk, 1), (4, 1024, 256), jnp.float32)
        _lenS = 1024 - jax.random.randint(jax.random.fold_in(_rk, 7), (4,), 0, max(1, 1024 // 4) + 1, jnp.int32)
        _lenS2 = 77 - jax.random.randint(jax.random.fold_in(_rk, 8), (4,), 0, max(1, 77 // 4) + 1, jnp.int32)
        _ctx_1024P = jax.random.normal(jax.random.fold_in(_rk, 11), (4, 16, 256), jnp.float32)
        _ctx_1024c = jax.random.dirichlet(jax.random.fold_in(_rk, 511), 0.3 * jnp.ones((16,), jnp.float32), (4, 77))
        _ctx_1024t = jnp.einsum('bsk,bkd->bsd', _ctx_1024c, _ctx_1024P)
        _ctx_1024t = _ctx_1024t * jax.lax.rsqrt(jnp.mean(jnp.square(_ctx_1024t)) + 1e-12) * 0.953939
        ctx_1024 = -0.000191848 + 0.999787 * (_ctx_1024t + 0.3 * jax.random.normal(jax.random.fold_in(_rk, 611), (4, 77, 256), jnp.float32))
        _validS = jnp.arange(1024)[None, :] < _lenS[:, None]
        _validS2 = jnp.arange(77)[None, :] < _lenS2[:, None]
        _causal = jnp.tril(jnp.ones((1024, 1024), dtype=bool))
        mask_BxS2_bk0 = jnp.logical_not(jnp.broadcast_to(_validS2[:, :], (4, 77)))
        return (x, ctx_1024, mask_BxS2_bk0)
    x, ctx_1024, mask_BxS2_bk0 = _rec_inputs()

    def _L0_attn_setup():
        import jax, jax.numpy as jnp
        import numpy as np
        import math
        D_MODEL = 256
        NUM_HEADS = 16
        D_HEAD = D_MODEL // NUM_HEADS
        B, T = (8, 256)

        def rel_pos_encoding(seq_len, d, dtype=jnp.float32):
            pos = jnp.arange(seq_len, dtype=jnp.float32)[:, None]
            div = jnp.exp(jnp.arange(0, d, 2, dtype=jnp.float32) * (-math.log(10000.0) / d))
            ang = pos * div
            pe_pos = jnp.stack([jnp.sin(ang), jnp.cos(ang)], axis=-1).reshape(seq_len, d)
            pe_neg = jnp.stack([jnp.sin(-ang), jnp.cos(-ang)], axis=-1).reshape(seq_len, d)
            pe = jnp.concatenate([pe_pos[::-1], pe_neg[1:]], axis=0)
            return pe.astype(dtype)

        def _rel_shift(pos_score):
            b, h, t1, t2 = pos_score.shape
            padded = jnp.pad(pos_score, ((0, 0), (0, 0), (0, 0), (1, 0)))
            padded = padded.reshape(b, h, t2 + 1, t1)
            return padded[:, :, 1:].reshape(b, h, t1, t2)[:, :, :, :t1]
        key = jax.random.key(seed)
        ks = jax.random.split(key, 9)
        D = D_MODEL
        s = 1.0 / math.sqrt(D)
        return {'x': jax.random.normal(ks[0], (B, T, D), jnp.float32), 'Wq': jax.random.normal(ks[1], (D, D), jnp.float32) * s, 'bq': jnp.zeros((D,), jnp.float32), 'Wk': jax.random.normal(ks[2], (D, D), jnp.float32) * s, 'bk': jnp.zeros((D,), jnp.float32), 'Wv': jax.random.normal(ks[3], (D, D), jnp.float32) * s, 'bv': jnp.zeros((D,), jnp.float32), 'Wpos': jax.random.normal(ks[4], (D, D), jnp.float32) * s, 'Wout': jax.random.normal(ks[5], (D, D), jnp.float32) * s, 'bout': jnp.zeros((D,), jnp.float32), 'u_bias': jax.random.normal(ks[6], (NUM_HEADS, D_HEAD), jnp.float32) * 0.1, 'v_bias': jax.random.normal(ks[7], (NUM_HEADS, D_HEAD), jnp.float32) * 0.1, 'ln_gamma': jnp.ones((D,), jnp.float32), 'ln_beta': jnp.zeros((D,), jnp.float32)}
    _L0_attn_all = _L0_attn_setup()
    _L0_attn_in = {k: v for k, v in _L0_attn_all.items() if k in ('Wq', 'bq', 'Wk', 'bk', 'Wv', 'bv', 'Wpos', 'Wout', 'bout', 'u_bias', 'v_bias', 'ln_gamma', 'ln_beta')}
    del _L0_attn_all

    def _L0_xattn_setup():
        import jax, jax.numpy as jnp
        import numpy as np
        NUM_HEADS = 16
        EPS = 1e-06

        def _ln(t, w, b):
            mu = jnp.mean(t, axis=-1, keepdims=True)
            var = jnp.mean(jnp.square(t - mu), axis=-1, keepdims=True)
            return (t - mu) * jax.lax.rsqrt(var + EPS) * w + b
        key = jax.random.key(seed)
        ks = jax.random.split(key, 10)
        b, s1, s2, qdim, kdim = (2, 512, 768, 256, 256)
        d = qdim // NUM_HEADS
        x = jax.random.normal(ks[0], (b, s1, qdim), dtype=jnp.float32)
        y = jax.random.normal(ks[1], (b, s2, kdim), dtype=jnp.float32)
        padding_mask = jax.random.randint(ks[2], (b, s2), 0, 2) > 0
        padding_mask = padding_mask.at[:, 0].set(True)
        w = 0.02
        Wq = jax.random.normal(ks[3], (qdim, qdim), dtype=jnp.float32) * w
        bq = jnp.zeros((qdim,), jnp.float32)
        Wkv = jax.random.normal(ks[4], (2 * qdim, kdim), dtype=jnp.float32) * w
        bkv = jnp.zeros((2 * qdim,), jnp.float32)
        qn_w = jnp.ones((d,), jnp.float32)
        qn_b = jnp.zeros((d,), jnp.float32)
        kn_w = jnp.ones((d,), jnp.float32)
        kn_b = jnp.zeros((d,), jnp.float32)
        Wo = jax.random.normal(ks[5], (qdim, qdim), dtype=jnp.float32) * w
        bo = jnp.zeros((qdim,), jnp.float32)
        return {'x': x, 'y': y, 'padding_mask': padding_mask, 'Wq': Wq, 'bq': bq, 'Wkv': Wkv, 'bkv': bkv, 'qn_w': qn_w, 'qn_b': qn_b, 'kn_w': kn_w, 'kn_b': kn_b, 'Wo': Wo, 'bo': bo}
    _L0_xattn_all = _L0_xattn_setup()
    _L0_xattn_in = {k: v for k, v in _L0_xattn_all.items() if k in ('Wq', 'bq', 'Wkv', 'bkv', 'qn_w', 'qn_b', 'kn_w', 'kn_b', 'Wo', 'bo')}
    del _L0_xattn_all

    def _L0_ffn_setup():
        import jax, jax.numpy as jnp
        import numpy as np
        EPS = 1e-05
        HEADS = 8
        DIM_KEY = 128
        K = 16
        NUM_KEYS = 64
        key = jax.random.key(seed)
        ks = jax.random.split(key, 5)
        B, T, D = (1, 256, 256)
        x = jax.random.normal(ks[0], (B, T, D), dtype=jnp.float32)
        norm_w = jnp.ones((D,), dtype=jnp.float32)
        wq = jax.random.normal(ks[1], (D, DIM_KEY * HEADS * 2), dtype=jnp.float32) * 0.02
        keys = jax.random.normal(ks[2], (HEADS, NUM_KEYS, 2, DIM_KEY), dtype=jnp.float32) * 0.02
        expert_down = jax.random.normal(ks[3], (NUM_KEYS * NUM_KEYS, D), dtype=jnp.float32) * 0.02
        expert_up = jax.random.normal(ks[4], (NUM_KEYS * NUM_KEYS, D), dtype=jnp.float32) * 0.02
        return {'x': x, 'norm_w': norm_w, 'wq': wq, 'keys': keys, 'expert_down': expert_down, 'expert_up': expert_up}
    _L0_ffn_all = _L0_ffn_setup()
    _L0_ffn_in = {k: v for k, v in _L0_ffn_all.items() if k in ('norm_w', 'wq', 'keys', 'expert_down', 'expert_up')}
    del _L0_ffn_all
    return {'x': x, 'ctx_1024': ctx_1024, 'mask_BxS2_bk0': mask_BxS2_bk0, 'L0_attn_Wq': _L0_attn_in['Wq'], 'L0_attn_bq': _L0_attn_in['bq'], 'L0_attn_Wk': _L0_attn_in['Wk'], 'L0_attn_bk': _L0_attn_in['bk'], 'L0_attn_Wv': _L0_attn_in['Wv'], 'L0_attn_bv': _L0_attn_in['bv'], 'L0_attn_Wpos': _L0_attn_in['Wpos'], 'L0_attn_Wout': _L0_attn_in['Wout'], 'L0_attn_bout': _L0_attn_in['bout'], 'L0_attn_u_bias': _L0_attn_in['u_bias'], 'L0_attn_v_bias': _L0_attn_in['v_bias'], 'L0_attn_ln_gamma': _L0_attn_in['ln_gamma'], 'L0_attn_ln_beta': _L0_attn_in['ln_beta'], 'L0_xattn_Wq': _L0_xattn_in['Wq'], 'L0_xattn_bq': _L0_xattn_in['bq'], 'L0_xattn_Wkv': _L0_xattn_in['Wkv'], 'L0_xattn_bkv': _L0_xattn_in['bkv'], 'L0_xattn_qn_w': _L0_xattn_in['qn_w'], 'L0_xattn_qn_b': _L0_xattn_in['qn_b'], 'L0_xattn_kn_w': _L0_xattn_in['kn_w'], 'L0_xattn_kn_b': _L0_xattn_in['kn_b'], 'L0_xattn_Wo': _L0_xattn_in['Wo'], 'L0_xattn_bo': _L0_xattn_in['bo'], 'L0_ffn_norm_w': _L0_ffn_in['norm_w'], 'L0_ffn_wq': _L0_ffn_in['wq'], 'L0_ffn_keys': _L0_ffn_in['keys'], 'L0_ffn_expert_down': _L0_ffn_in['expert_down'], 'L0_ffn_expert_up': _L0_ffn_in['expert_up']}

def reference(x, ctx_1024, mask_BxS2_bk0, L0_attn_Wq, L0_attn_bq, L0_attn_Wk, L0_attn_bk, L0_attn_Wv, L0_attn_bv, L0_attn_Wpos, L0_attn_Wout, L0_attn_bout, L0_attn_u_bias, L0_attn_v_bias, L0_attn_ln_gamma, L0_attn_ln_beta, L0_xattn_Wq, L0_xattn_bq, L0_xattn_Wkv, L0_xattn_bkv, L0_xattn_qn_w, L0_xattn_qn_b, L0_xattn_kn_w, L0_xattn_kn_b, L0_xattn_Wo, L0_xattn_bo, L0_ffn_norm_w, L0_ffn_wq, L0_ffn_keys, L0_ffn_expert_down, L0_ffn_expert_up):
    import jax
    import jax.numpy as jnp

    def _L0_attn_ref(x, Wq, bq, Wk, bk, Wv, bv, Wpos, Wout, bout, u_bias, v_bias, ln_gamma, ln_beta):
        import jax, jax.numpy as jnp
        import numpy as np
        import math
        D_MODEL = 256
        NUM_HEADS = 16
        D_HEAD = D_MODEL // NUM_HEADS
        B, T = (8, 256)

        def rel_pos_encoding(seq_len, d, dtype=jnp.float32):
            pos = jnp.arange(seq_len, dtype=jnp.float32)[:, None]
            div = jnp.exp(jnp.arange(0, d, 2, dtype=jnp.float32) * (-math.log(10000.0) / d))
            ang = pos * div
            pe_pos = jnp.stack([jnp.sin(ang), jnp.cos(ang)], axis=-1).reshape(seq_len, d)
            pe_neg = jnp.stack([jnp.sin(-ang), jnp.cos(-ang)], axis=-1).reshape(seq_len, d)
            pe = jnp.concatenate([pe_pos[::-1], pe_neg[1:]], axis=0)
            return pe.astype(dtype)

        def _rel_shift(pos_score):
            b, h, t1, t2 = pos_score.shape
            padded = jnp.pad(pos_score, ((0, 0), (0, 0), (0, 0), (1, 0)))
            padded = padded.reshape(b, h, t2 + 1, t1)
            return padded[:, :, 1:].reshape(b, h, t1, t2)[:, :, :, :t1]
        b, t, d = x.shape
        h, dh = (NUM_HEADS, D_HEAD)
        mu = jnp.mean(x, axis=-1, keepdims=True)
        var = jnp.mean((x - mu) ** 2, axis=-1, keepdims=True)
        xn = (x - mu) * jax.lax.rsqrt(var + 1e-05) * ln_gamma + ln_beta
        pos_emb = rel_pos_encoding(t, d, x.dtype)
        q = (xn @ Wq.T + bq).reshape(b, t, h, dh)
        k = (xn @ Wk.T + bk).reshape(b, t, h, dh)
        v = (xn @ Wv.T + bv).reshape(b, t, h, dh)
        p = (pos_emb @ Wpos.T).reshape(2 * t - 1, h, dh)
        content_score = jnp.einsum('bthd,bshd->bhts', q + u_bias, k)
        pos_score = jnp.einsum('bthd,phd->bhtp', q + v_bias, p)
        pos_score = _rel_shift(pos_score)
        score = (content_score + pos_score) / math.sqrt(dh)
        attn = jax.nn.softmax(score, axis=-1)
        ctx = jnp.einsum('bhts,bshd->bthd', attn, v).reshape(b, t, d)
        return ctx @ Wout.T + bout

    def _L0_xattn_ref(x, y, padding_mask, Wq, bq, Wkv, bkv, qn_w, qn_b, kn_w, kn_b, Wo, bo):
        import jax, jax.numpy as jnp
        import numpy as np
        NUM_HEADS = 16
        EPS = 1e-06

        def _ln(t, w, b):
            mu = jnp.mean(t, axis=-1, keepdims=True)
            var = jnp.mean(jnp.square(t - mu), axis=-1, keepdims=True)
            return (t - mu) * jax.lax.rsqrt(var + EPS) * w + b
        b, s1, c = x.shape
        s2 = y.shape[1]
        h, d = (NUM_HEADS, c // NUM_HEADS)
        scale = d ** (-0.5)
        q = (x @ Wq.T + bq).reshape(b, s1, h, d)
        kv = (y @ Wkv.T + bkv).reshape(b, s2, 2, h, d)
        k, v = (kv[:, :, 0], kv[:, :, 1])
        q = _ln(q, qn_w, qn_b) * scale
        k = _ln(k, kn_w, kn_b)
        attn = jnp.einsum('bihd,bjhd->bhij', q, k)
        attn = jnp.where(padding_mask[:, None, None, :], attn, -jnp.inf)
        p = jax.nn.softmax(attn, axis=-1)
        ctx = jnp.einsum('bhij,bjhd->bihd', p, v).reshape(b, s1, c)
        out = ctx @ Wo.T + bo
        return out

    def _L0_ffn_ref(x, norm_w, wq, keys, expert_down, expert_up):
        import jax, jax.numpy as jnp
        import numpy as np
        EPS = 1e-05
        HEADS = 8
        DIM_KEY = 128
        K = 16
        NUM_KEYS = 64
        B, T, D = x.shape
        inv = jax.lax.rsqrt(jnp.mean(x * x, axis=-1, keepdims=True) + EPS)
        x_norm = x * inv * norm_w
        q = (x_norm @ wq).reshape(B, T, HEADS, 2, DIM_KEY)
        sim = jnp.einsum('bthpd,hkpd->pbthk', q, keys)
        s1, i1 = jax.lax.top_k(sim[0], K)
        s2, i2 = jax.lax.top_k(sim[1], K)
        all_idx = (i1[..., :, None] * NUM_KEYS + i2[..., None, :]).reshape(B, T, HEADS, K * K)
        all_scores = (s1[..., :, None] + s2[..., None, :]).reshape(B, T, HEADS, K * K)
        final_scores, pk = jax.lax.top_k(all_scores, K)
        final_idx = jnp.take_along_axis(all_idx, pk, axis=-1)
        wd = expert_down[final_idx]
        wu = expert_up[final_idx]
        hidden = jnp.einsum('btd,bthkd->bthk', x_norm, wd)
        hidden = jax.nn.gelu(hidden, approximate=False)
        hidden = hidden * jax.nn.relu(final_scores)
        out = jnp.einsum('bthk,bthkd->btd', hidden, wu)
        return out
    x = x + _L0_attn_ref(_layernorm(x, axis=-1), L0_attn_Wq, L0_attn_bq, L0_attn_Wk, L0_attn_bk, L0_attn_Wv, L0_attn_bv, L0_attn_Wpos, L0_attn_Wout, L0_attn_bout, L0_attn_u_bias, L0_attn_v_bias, L0_attn_ln_gamma, L0_attn_ln_beta)
    x = x + _L0_xattn_ref(_layernorm(x, axis=-1), ctx_1024, mask_BxS2_bk0, L0_xattn_Wq, L0_xattn_bq, L0_xattn_Wkv, L0_xattn_bkv, L0_xattn_qn_w, L0_xattn_qn_b, L0_xattn_kn_w, L0_xattn_kn_b, L0_xattn_Wo, L0_xattn_bo)
    x = x + _L0_ffn_ref(_layernorm(x, axis=-1), L0_ffn_norm_w, L0_ffn_wq, L0_ffn_keys, L0_ffn_expert_down, L0_ffn_expert_up)
    return x

_drawn_inputs = setup_inputs


def setup_inputs(seed=0):
    import zlib

    import numpy as np

    out = dict(_drawn_inputs(seed))
    spreads = {'L0_attn_bq': (0.0, 0.757),
     'L0_attn_bk': (0.0, 0.8),
     'L0_attn_bv': (0.0, 0.1),
     'L0_attn_bout': (0.0, 0.1),
     'L0_attn_ln_gamma': (1.0, 0.2),
     'L0_attn_ln_beta': (0.0, 0.1),
     'L0_xattn_bq': (0.0, 0.8),
     'L0_xattn_bkv': (0.0, 0.1),
     'L0_xattn_qn_w': (1.0, 0.6),
     'L0_xattn_qn_b': (0.0, 0.8),
     'L0_xattn_kn_w': (1.0, 0.6),
     'L0_xattn_kn_b': (0.0, 0.8),
     'L0_xattn_bo': (0.0, 0.1),
     'L0_ffn_norm_w': (1.0, 0.6)}
    factors = {'L0_attn_u_bias': 5.278,
     'L0_attn_v_bias': 8.0,
     'L0_ffn_wq': 4.593,
     'L0_ffn_keys': 4.6,
     'L0_ffn_expert_down': 4.64,
     'L0_ffn_expert_up': 4.517}
    for name, (base, spread) in spreads.items():
        noise = np.random.default_rng([zlib.crc32(name.encode()), seed]).standard_normal(out[name].shape)
        drawn = base * np.exp(spread * noise) if base else spread * noise
        out[name] = jnp.asarray(drawn.astype(out[name].dtype))
    for name, factor in factors.items():
        out[name] = (out[name] * factor).astype(out[name].dtype)
    return out
```

```python
from contextlib import ExitStack
import math

import numpy as np
import concourse.bass as bass
from concourse import mybir

ALU = mybir.AluOpType
ACT = mybir.ActivationFunctionType
AX_X = mybir.AxisListType.X
F32 = mybir.dt.float32
BF16 = mybir.dt.bfloat16
U32 = mybir.dt.uint32

P = 128
B, T, D = 4, 1024, 256
N = B * T
S2 = 77
KC = D // P
H, DH = 16, 16
NT = T // P
TILES = N // P
HALF = 512
SCALE = 1.0 / math.sqrt(DH)

PARTS_Q = (0, 0, 0, 1, 1, 1, 2, 2)
PARTS_K = (0, 1, 2, 0, 1, 2, 0, 1)


AHEAD = 1
DMA_AHEAD = 16


def project_qkv(nc, x, wT, vecs, bv_rows, ident_in, eps_in, wpos, qu_s, qv_s, k_s, v_s, wp_s):
    xf = x.rearrange("b (i p) d -> b p i d", p=P)
    with ExitStack() as ctx:
        def sb(name, shape, dt=F32):
            return ctx.enter_context(nc.sbuf_tensor(name, shape, dt))

        def sem(name):
            return ctx.enter_context(nc.semaphore(name))

        ident = sb("a_ident", [P, P])
        w_sb = sb("a_w", [P, 3, KC, D])
        vec = sb("a_vec", [P, 7, KC])
        bias = sb("a_bias", [P, 3, KC])
        bv_b = sb("a_bv", [P, D])
        wp_f = sb("a_wp", [P, KC, D])
        wp_r = sb("a_wp_r", [P, KC, D])
        wp_parts = sb("a_wp_parts", [P, 3, KC, D], BF16)
        xt = sb("a_x", [P, NT, D])
        st = sb("a_st", [P, NT, 6])
        mv = sb("a_mv", [P, NT, 2])
        sd = sb("a_sd", [P, NT])
        eps = sb("a_eps", [P, 1])
        spare = sb("a_spare", [P, 1])
        xnT = sb("a_xnT", [P, KC, T])
        parts = sb("a_parts", [P, 2, 3, HALF], BF16)
        resid = sb("a_resid", [P, 2, HALF])
        v_sb = sb("a_v", [P, NT, D])
        v_parts = sb("a_v_parts", [P, NT, H, 3, DH], BF16)
        ps_t = ctx.enter_context(nc.psum_tensor("a_ps_t", [P, 2, HALF], F32))
        ps_p = ctx.enter_context(nc.psum_tensor("a_ps_p", [P, 2, HALF], F32))
        ps_v = ctx.enter_context(nc.psum_tensor("a_ps_v", [P, 2, HALF], F32))

        consts = sem("a_consts")
        x_in = sem("a_x_in")
        wp_out = sem("a_wp_out")
        parts_out = [sem(f"a_parts_out{u}") for u in range(2)]
        v_out = sem("a_v_out")
        wp_steps = sem("a_wp_steps")
        dve_steps = sem("a_dve_steps")
        var_ready = sem("a_var_ready")
        sd_ready = sem("a_sd_ready")
        z_ready = sem("a_z_ready")
        tr_ready = sem("a_tr_ready")
        tr_used = sem("a_tr_used")
        proj_ready = sem("a_proj_ready")
        high_ready = sem("a_high_ready")
        resid_ready = sem("a_resid_ready")
        mid_ready = sem("a_mid_ready")
        low_ready = sem("a_low_ready")
        vproj_ready = sem("a_vproj_ready")
        v_ready = sem("a_v_ready")
        v_high = sem("a_v_high")
        v_resid = sem("a_v_resid")
        v_mid = sem("a_v_mid")
        v_low = sem("a_v_low")
        unit_free = sem("a_unit_free")
        block = ctx.enter_context(nc.Block())

        UNITS = [(w, c, hf) for hf in range(2) for w in range(3) for c in range(KC)]
        NU = len(UNITS)
        W_OF = (0, 0, 1)
        NCONST = 6 * 16

        def v_part(n):
            return v_parts[:, :, :, n, :].rearrange("p i h d -> p (i h) d")

        v_rows = v_sb[:, :, :].rearrange("p i (h d) -> p (i h) d", d=DH)

        @block.sync
        def _(sp):
            sp.dma_start(ident[:, :], ident_in).then_inc(consts, 16)
            sp.dma_start(w_sb[:, :, :, :], wT.rearrange("w (c p) n -> p w c n", p=P)).then_inc(consts, 16)
            with nc.allow_non_contiguous_dma(reason="short per-channel vectors"):
                sp.dma_start(vec[:, 0:6, :], vecs.rearrange("v (c p) -> p v c", p=P)).then_inc(consts, 16)
            sp.dma_start(bv_b[:, :], bv_rows).then_inc(consts, 16)
            sp.dma_start(wp_f[:, :, :], wpos.rearrange("(c p) n -> p c n", p=P)).then_inc(consts, 16)
            sp.dma_start(eps[:, :], eps_in).then_inc(consts, 16)
            for s in (*parts_out, v_out):
                sp.sem_inc(s, DMA_AHEAD)
            sp.wait_ge(wp_steps, 5)
            for part in range(3):
                sp.dma_start(wp_s[part].rearrange("(c p) n -> p c n", p=P), wp_parts[:, part, :, :]).then_inc(wp_out, 16)
            with sp.Fori(0, B) as b:
                sp.wait_ge(tr_ready, b * (2 * NT) + AHEAD)
                sp.dma_start(xt[:, :, :], xf[b, :, :, :]).then_inc(x_in, 16)
                for n, (w, c, hf) in enumerate(UNITS):
                    sp.wait_ge(low_ready, b * NU + (n + 1))
                    dst = (qu_s, qv_s, k_s)[w]
                    for part in range(3):
                        sp.dma_start(dst[part, c * P:(c + 1) * P, bass.ds(b * T + hf * HALF, HALF)],
                                     parts[:, n % 2, part, :]).then_inc(parts_out[n % 2], 16)
                sp.wait_ge(v_low, b + (1 + AHEAD))
                sp.dma_start(v_s[bass.ds(b * T, T), :].rearrange("(i p) n -> p i n", p=P),
                             v_parts[:, :, :, :, :].rearrange("p i h n d -> p i (h n d)")).then_inc(v_out, 16)
            sp.wait_ge(wp_out, 3 * 16)
            for u in range(2):
                sp.wait_ge(parts_out[u], B * (NU // 2) * 3 * 16 + DMA_AHEAD)
            sp.wait_ge(v_out, B * 16 + DMA_AHEAD)

        @block.vector
        def _(dve):
            dve.wait_ge(consts, NCONST)
            nc.vector.tensor_copy(wp_parts[:, 0], wp_f[:, :, :]).then_inc(wp_steps, 1)
            dve.wait_ge(wp_steps, 1)
            nc.vector.tensor_tensor(wp_r[:, :, :], wp_f[:, :, :], wp_parts[:, 0], ALU.subtract).then_inc(wp_steps, 1)
            dve.wait_ge(wp_steps, 2)
            nc.vector.tensor_copy(wp_parts[:, 1], wp_r[:, :, :]).then_inc(wp_steps, 1)
            dve.wait_ge(wp_steps, 3)
            nc.vector.tensor_tensor(wp_parts[:, 2], wp_r[:, :, :], wp_parts[:, 1], ALU.subtract).then_inc(wp_steps, 1)
            nc.vector.tensor_tensor(bias[:, 0, :], vec[:, 0, :], vec[:, 2, :], ALU.add)
            nc.vector.tensor_tensor(bias[:, 1, :], vec[:, 0, :], vec[:, 3, :], ALU.add)
            nc.vector.tensor_copy(bias[:, 2, :], vec[:, 1, :]).then_inc(wp_steps, 1)
            def carry(spare):
                nc.vector.memset(spare, 0.0)

            with dve.Fori(0, B) as b:
                def stats(rnd):
                    for i in range(NT):
                        last = nc.vector.bn_stats(st[:, i, :], xt[:, i, :])
                    last.then_inc(dve_steps, 1)
                    dve.wait_ge(dve_steps, b * 5 + (3 * rnd + 1))
                    carry(spare[:, :])
                    for i in range(NT):
                        last = nc.vector.bn_aggr(mv[:, i, :], st[:, i, :])
                    last.then_inc(var_ready, 1)
                    dve.wait_ge(sd_ready, b * 2 + (rnd + 1))
                    nc.vector.reciprocal(sd[:, :], sd[:, :]).then_inc(dve_steps, 1)
                    dve.wait_ge(dve_steps, b * 5 + (3 * rnd + 2))
                    for i in range(NT):
                        last = nc.vector.tensor_scalar(xt[:, i, :], xt[:, i, :], mv[:, i, 0:1], sd[:, i:i + 1],
                                                       ALU.subtract, ALU.mult)
                    last.then_inc(dve_steps if rnd == 0 else z_ready, 1)

                dve.wait_ge(x_in, b * 16 + 16)
                stats(0)
                dve.wait_ge(dve_steps, b * 5 + 3)
                stats(1)
                for g in range(2 * NT // 4):
                    c, i0 = g // 2, 4 * (g % 2)
                    dve.wait_ge(tr_ready, b * (2 * NT) + (4 * g + 4 + AHEAD))
                    nc.vector.tensor_scalar(xnT[:, c, i0 * P:(i0 + 4) * P], ps_t[:, g % 2, :],
                                            vec[:, 4, c:c + 1], vec[:, 5, c:c + 1], ALU.mult, ALU.add).then_inc(tr_used, 1)
                for n, (w, c, hf) in enumerate(UNITS):
                    dve.wait_ge(high_ready, b * NU + (n + 1))
                    nc.vector.scalar_tensor_tensor(out=resid[:, n % 2, :], in0=ps_p[:, n % 2, :], scalar=bias[:, w, c:c + 1],
                                                   in1=parts[:, n % 2, 0, :], op0=ALU.add, op1=ALU.subtract).then_inc(resid_ready, 1)
                    dve.wait_ge(mid_ready, b * NU + (n + 1))
                    nc.vector.tensor_tensor(parts[:, n % 2, 2, :], resid[:, n % 2, :], parts[:, n % 2, 1, :],
                                            ALU.subtract).then_inc(low_ready, 1)
                for i in range(NT):
                    if i == 0:
                        dve.wait_ge(v_low, b + AHEAD)
                    dve.wait_ge(vproj_ready, b * NT + (i + 1))
                    nc.vector.tensor_tensor(v_sb[:, i, :], ps_v[:, i % 2, 0:D], bv_b[:, :], ALU.add).then_inc(v_ready, 1)

        @block.scalar
        def _(act):
            act.wait_ge(wp_steps, 5)
            with act.Fori(0, B) as b:
                for rnd in range(2):
                    act.wait_ge(var_ready, b * 2 + (rnd + 1))
                    nc.scalar.activation(sd[:, :], mv[:, :, 1], ACT.Sqrt, bias=eps[:, 0:1]).then_inc(sd_ready, 1)
                for n, (w, c, hf) in enumerate(UNITS):
                    act.wait_ge(parts_out[n % 2], b * (NU // 2 * 48) + (n // 2 * 48 + DMA_AHEAD))
                    act.wait_ge(proj_ready, b * NU + (n + 1))
                    nc.scalar.activation(parts[:, n % 2, 0, :], ps_p[:, n % 2, :], ACT.Identity,
                                         bias=bias[:, w, c:c + 1]).then_inc(high_ready, 1)
                    act.wait_ge(resid_ready, b * NU + (n + 1))
                    nc.scalar.copy(parts[:, n % 2, 1, :], resid[:, n % 2, :]).then_inc(mid_ready, 1)
                act.wait_ge(v_out, b * 16 + DMA_AHEAD)
                act.wait_ge(v_ready, b * NT + NT)
                nc.scalar.copy(v_part(0), v_rows).then_inc(v_high, 1)
                act.wait_ge(v_resid, b + 1)
                nc.scalar.copy(v_part(1), v_rows).then_inc(v_mid, 1)

        @block.gpsimd
        def _(pool):
            pool.sem_inc(v_low, AHEAD)
            with pool.Fori(0, B) as b:
                pool.wait_ge(v_high, b + 1)
                nc.gpsimd.tensor_tensor(v_rows, v_rows, v_part(0), ALU.subtract).then_inc(v_resid, 1)
                pool.wait_ge(v_mid, b + 1)
                nc.gpsimd.tensor_tensor(v_part(2), v_rows, v_part(1), ALU.subtract).then_inc(v_low, 1)

        @block.tensor
        def _(pe):
            pe.wait_ge(consts, NCONST)
            pe.sem_inc(tr_ready, AHEAD)
            with pe.Fori(0, B) as b:
                for g in range(2 * NT // 4):
                    c, i0 = g // 2, 4 * (g % 2)
                    if g == 0:
                        pe.wait_ge(z_ready, b + 1)
                    if g >= 2:
                        pe.wait_ge(tr_used, b * 4 + (g - 1))
                    for i in range(4):
                        nc.tensor.transpose(ps_t[:, g % 2, i * P:(i + 1) * P], xt[:, i0 + i, c * P:(c + 1) * P],
                                            ident[:, :]).then_inc(tr_ready, 1)
                pe.wait_ge(tr_used, b * 4 + 4)
                for n, (w, c, hf) in enumerate(UNITS):
                    if n >= 2:
                        pe.wait_ge(resid_ready, b * NU + (n - 1))
                    for k in range(KC):
                        mm = nc.tensor.matmul(ps_p[:, n % 2, :], w_sb[:, W_OF[w], k, c * P:(c + 1) * P],
                                              xnT[:, k, hf * HALF:(hf + 1) * HALF], start=(k == 0), stop=(k == KC - 1))
                    mm.then_inc(proj_ready, 1)
                for i in range(NT):
                    if i >= 2:
                        pe.wait_ge(v_ready, b * NT + (i - 1))
                    for k in range(KC):
                        mm = nc.tensor.matmul(ps_v[:, i % 2, 0:D], xnT[:, k, i * P:(i + 1) * P], w_sb[:, 2, k, :],
                                              start=(k == 0), stop=(k == KC - 1))
                    mm.then_inc(vproj_ready, 1)


def self_attention(nc, trig_in, ident_in, qu_s, qv_s, k_s, v_s, wp_s, ctx_s):
    with ExitStack() as ctx:
        def sb(name, shape, dt=F32):
            return ctx.enter_context(nc.sbuf_tensor(name, shape, dt))

        def pb(name, shape):
            return ctx.enter_context(nc.psum_tensor(name, shape, F32))

        def sem(name):
            return ctx.enter_context(nc.semaphore(name))

        ident = sb("b_ident", [P, P])
        trig = sb("b_trig", [P, 3, T])
        qu = sb("b_qu", [P, 2, T], BF16)
        ks = sb("b_ks", [P, 2, T], BF16)
        qv = sb("b_qv", [P, 2, T], BF16)
        wp = sb("b_wp", [P, 2, D], BF16)
        vh = sb("b_vh", [P, 2, NT, 3 * DH], BF16)
        r1 = sb("b_r1", [P, 2, HALF])
        r2 = sb("b_r2", [P, 2, HALF])
        uv = sb("b_uv", [P, 2, 2, T])
        nmax = sb("b_nmax", [P, 2])
        rmax = sb("b_rmax", [P, 2])
        probs = sb("b_probs", [P, 2, T])
        rsum = sb("b_rsum", [P, 2, NT])
        rinv = sb("b_rinv", [P, NT])
        pT = sb("b_pT", [P, 2, 3, NT, P], BF16)
        pr = sb("b_pr", [P, 2, HALF])
        ctx_sum = sb("b_ctx_sum", [P, NT, DH])
        ctx_sb = sb("b_ctx", [P, 2, NT, DH])
        zero = sb("b_zero", [P, 2])
        ps_a = pb("b_ps_a", [P, 2, HALF])
        ps_s = pb("b_ps_s", [P, 2, 2, HALF])
        ps_t = pb("b_ps_t", [P, HALF])
        ps_o = pb("b_ps_o", [P, HALF])

        consts = sem("b_consts")
        qv_in = [sem(f"b_qv_in{u}") for u in range(2)]
        qk_in = [sem(f"b_qk_in{u}") for u in range(2)]
        ctx_out = [sem(f"b_ctx_out{u}") for u in range(2)]
        sc_ready = sem("b_sc_ready")
        max_ready = sem("b_max_ready")
        nmax_ready = sem("b_nmax_ready")
        exp_done = sem("b_exp_done")
        tr_ready = sem("b_tr_ready")
        hi_done = sem("b_hi_done")
        rest_done = sem("b_rest_done")
        mid_done = sem("b_mid_done")
        lo_done = sem("b_lo_done")
        sum_ready = sem("b_sum_ready")
        av_done = sem("b_av_done")
        a_ready = sem("b_a_ready")
        rot_done = sem("b_rot_done")
        uv_ready = sem("b_uv_ready")
        inv_ready = sem("b_inv_ready")
        ctx_ready = sem("b_ctx_ready")
        block = ctx.enter_context(nc.Block())

        TPH = B * NT
        NCONST = 2 * 16
        QV_DMAS, QK_DMAS = 16, 17


        @block.sync
        def _(sp):
            sp.dma_start(ident[:, :], ident_in).then_inc(consts, 16)
            sp.dma_start(trig[:, :, :], trig_in).then_inc(consts, 16)

            def load_qv(h, b, first):
                if not first:
                    sp.wait_ge(a_ready, (h * B + b) * 2 - 2)
                for n in range(8):
                    sp.dma_start(qv[n * DH:(n + 1) * DH, b % 2, :],
                                 qv_s[PARTS_K[n], bass.ds(h * DH, DH), b * T:(b + 1) * T]).then_inc(qv_in[b % 2], 16)
                    sp.dma_start(wp[n * DH:(n + 1) * DH, b % 2, :],
                                 wp_s[PARTS_Q[n], bass.ds(h * DH, DH), :]).then_inc(qv_in[b % 2], 16)

            def load_qk(h, b, first):
                if not first:
                    sp.wait_ge(av_done, (h * B + b) * NT - (NT - AHEAD))
                for n in range(8):
                    sp.dma_start(qu[n * DH:(n + 1) * DH, b % 2, :],
                                 qu_s[PARTS_Q[n], bass.ds(h * DH, DH), b * T:(b + 1) * T]).then_inc(qk_in[b % 2], 16)
                    sp.dma_start(ks[n * DH:(n + 1) * DH, b % 2, :],
                                 k_s[PARTS_K[n], bass.ds(h * DH, DH), b * T:(b + 1) * T]).then_inc(qk_in[b % 2], 16)
                sp.dma_start(vh[:, b % 2, :, :],
                             v_s[b * T:(b + 1) * T, bass.ds(h * (3 * DH), 3 * DH)].rearrange("(i p) d -> p i d", p=P)).then_inc(qk_in[b % 2], 16)

            for s in ctx_out:
                sp.sem_inc(s, DMA_AHEAD)
            load_qv(0, 0, True)
            load_qk(0, 0, True)
            load_qv(0, 1, True)
            load_qk(0, 1, True)

            def job(h, b, ahead):
                if ahead:
                    load_qv(h + (b + 2) // B, (b + 2) % B, False)
                    load_qk(h + (b + 2) // B, (b + 2) % B, False)

            with sp.Fori(0, H - 1) as h:
                for b in range(B):
                    job(h, b, True)
            for b in range(2):
                job(H - 1, b, True)
            for u in range(2):
                sp.wait_ge(ctx_out[u], H * (B // 2) * 16 + DMA_AHEAD)

        @block.tensor
        def _(pe):
            def sc_chunk(h, hf, b, job_off):
                if hf == 0:
                    pe.wait_ge(qv_in[b], h * (B // 2 * QV_DMAS * 16) + (job_off // 2 + 1) * (QV_DMAS * 16))
                pe.wait_ge(rot_done, (h * B + job_off) * 4 + 2 * hf)
                for c in range(2):
                    mm = nc.tensor.matmul(ps_a[:, c, :], wp[:, b, c * P:(c + 1) * P], qv[:, b, hf * HALF:(hf + 1) * HALF],
                                          start=True, stop=True)
                mm.then_inc(a_ready, 1)

            def scores(h, s, hf):
                b, i = s // NT, s % NT
                slot = b % 2
                if hf == 0:
                    pe.wait_ge(exp_done, h * TPH + (s + 1))
                    if i == 0:
                        pe.wait_ge(qk_in[slot], h * (B // 2 * QK_DMAS * 16) + (b // 2 + 1) * (QK_DMAS * 16))
                    if i == 0 or i == NT // 2:
                        pe.wait_ge(uv_ready, h * (B * 4) + (4 * b + (2 if i == 0 else 4)))
                q = slice(i * P, (i + 1) * P)
                k = slice(hf * HALF, (hf + 1) * HALF)
                nc.tensor.matmul(ps_s[:, s % 2, hf, :], uv[:, slot, 0, q], trig[:, 1, k], start=True, stop=False)
                nc.tensor.matmul(ps_s[:, s % 2, hf, :], uv[:, slot, 1, q], trig[:, 0, k], start=False, stop=False)
                mm = nc.tensor.matmul(ps_s[:, s % 2, hf, :], qu[:, slot, q], ks[:, slot, k], start=False, stop=True)
                if hf == 1:
                    mm.then_inc(sc_ready, 1)

            def transposes(h, s, g):
                if g == 0:
                    pe.wait_ge(exp_done, h * TPH + (s + 3))
                pe.wait_ge(rest_done, h * (2 * TPH) + (2 * s + g))
                for j in range(4):
                    mm = nc.tensor.transpose(ps_t[:, j * P:(j + 1) * P], probs[:, s % 2, (4 * g + j) * P:(4 * g + j + 1) * P],
                                             ident[:, :])
                mm.then_inc(tr_ready, 1)

            def context(h, s):
                b, i = (s // NT) % B, s % NT
                pe.wait_ge(lo_done, h * (2 * TPH) + (2 * s + 2))
                if i == 0:
                    pe.wait_ge(ctx_ready, h * B + (s // NT + AHEAD))
                for j in range(NT):
                    for part in range(3):
                        w = (3 - part) * DH
                        mm = nc.tensor.matmul(ps_o[:, i * 3 * DH:i * 3 * DH + w], pT[:, s % 2, part, j, :], vh[:, b % 2, j, 0:w],
                                              start=(j == 0 and part == 0), stop=(j == NT - 1 and part == 2), skip_group_check=True)
                mm.then_inc(av_done, 1)

            def step(h, s, behind=3, ahead=True):
                hh, ss = (h + 1, s - TPH) if s >= TPH else (h, s)
                scores(hh, ss, 0)
                if behind >= 2:
                    transposes(h, s - 2, 1)
                scores(hh, ss, 1)
                if behind >= 3:
                    context(h, s - 3)
                if behind >= 1:
                    transposes(h, s - 1, 0)
                if ahead and s % NT in (3, 5):
                    sc_chunk(h, (s % NT) // 5, (s // NT + 1) % 2, s // NT + 1)

            pe.wait_ge(consts, NCONST)
            pe.sem_inc(av_done, AHEAD)
            for hf in range(2):
                sc_chunk(0, hf, 0, 0)
            for s in range(3):
                step(0, s, behind=s)
            with pe.Fori(0, H - 1) as h:
                for s in range(3, TPH + 3):
                    step(h, s)
            for s in range(3, TPH):
                step(H - 1, s, ahead=(s < TPH - NT))
            transposes(H - 1, TPH - 2, 1)
            context(H - 1, TPH - 3)
            transposes(H - 1, TPH - 1, 0)
            transposes(H - 1, TPH - 1, 1)
            context(H - 1, TPH - 2)
            context(H - 1, TPH - 1)

        @block.scalar
        def _(act):
            act.wait_ge(consts, NCONST)
            nc.scalar.copy(zero[:, 0:1], ident[:, 0:1]).then_inc(exp_done, 1)
            nc.scalar.copy(zero[:, 1:2], ident[:, 1:2]).then_inc(exp_done, 1)

            def exp(h, s, first=False):
                b = s // NT
                act.wait_ge(nmax_ready, h * TPH + (s + 1))
                if s % NT == 0 and not first:
                    act.wait_ge(ctx_ready, h * B + (b - 1 + AHEAD))
                nc.scalar.activation(probs[:, s % 2, :], ps_s[:, s % 2, :, :].rearrange("p a n -> p (a n)"), ACT.Exp,
                                     bias=nmax[:, s % 2:s % 2 + 1], scale=SCALE,
                                     accum_out=rsum[:, b % 2, s % NT:s % NT + 1]).then_inc(exp_done, 1)

            def high(h, s, g):
                if g == 0 and s >= 2:
                    act.wait_ge(av_done, h * TPH + (s - 1 + AHEAD))
                act.wait_ge(tr_ready, h * (2 * TPH) + (2 * s + g + 1))
                nc.scalar.copy(pT[:, s % 2, 0, 4 * g:4 * g + 4, :].rearrange("p a n -> p (a n)"), ps_t[:, :]).then_inc(hi_done, 1)

            def middle(h, s, g):
                act.wait_ge(rest_done, h * (2 * TPH) + (2 * s + g + 1))
                nc.scalar.copy(pT[:, s % 2, 1, 4 * g:4 * g + 4, :].rearrange("p a n -> p (a n)"), pr[:, g, :]).then_inc(mid_done, 1)

            def store_ctx(h, b):
                act.wait_ge(ctx_ready, h * B + (b + 1 + AHEAD))
                act.dma_start(ctx_s[b * T:(b + 1) * T, bass.ds(h * DH, DH)].rearrange("(i p) d -> p i d", p=P),
                              ctx_sb[:, b % 2, :, :]).then_inc(ctx_out[b % 2], 16)

            def step(h, s, behind=2):
                hh, ss = (h + 1, s - TPH) if s >= TPH else (h, s)
                if behind >= 2:
                    high(h, s - 2, 1)
                    middle(h, s - 2, 1)
                if behind >= 1:
                    high(h, s - 1, 0)
                exp(hh, ss, first=(behind == 0))
                if behind >= 1:
                    middle(h, s - 1, 0)

            for s in range(3):
                step(0, s, behind=s)
            with act.Fori(0, H - 1) as h:
                for s in range(3, TPH + 3):
                    step(h, s)
                    if s % NT == 4 and s > NT:
                        store_ctx(h, s // NT - 1)
                store_ctx(h, B - 1)
            for s in range(3, TPH):
                step(H - 1, s)
                if s % NT == 4 and s > NT:
                    store_ctx(H - 1, s // NT - 1)
            high(H - 1, TPH - 2, 1)
            middle(H - 1, TPH - 2, 1)
            for g in range(2):
                high(H - 1, TPH - 1, g)
                middle(H - 1, TPH - 1, g)
            store_ctx(H - 1, B - 1)

        @block.vector
        def _(dve):
            def row_max(h, s):
                dve.wait_ge(sc_ready, h * TPH + (s + 1))
                nc.vector.tensor_reduce(rmax[:, s % 2:s % 2 + 1], ps_s[:, s % 2, :, :].rearrange("p a n -> p (a n)"),
                                        AX_X, ALU.max).then_inc(max_ready, 1)
                dve.wait_ge(max_ready, h * TPH + (s + 1))
                nc.vector.tensor_scalar(nmax[:, s % 2:s % 2 + 1], rmax[:, s % 2:s % 2 + 1], -SCALE, None,
                                        ALU.mult).then_inc(nmax_ready, 1)

            def products(h, job_off, hf):
                cols = slice(hf * HALF, (hf + 1) * HALF)
                dve.wait_ge(a_ready, (h * B + job_off) * 2 + (hf + 1))
                dve.wait_ge(uv_ready, (h * B + job_off) * 4 + 2 * hf)
                nc.vector.tensor_tensor(r1[:, :, :], ps_a[:, :, :], trig[:, 0:2, cols], ALU.mult).then_inc(rot_done, 1)
                nc.vector.tensor_tensor(r2[:, :, :], ps_a[:, :, :], trig[:, 1:3, cols], ALU.mult).then_inc(rot_done, 1)

            def normalise(h, b):
                dve.wait_ge(av_done, h * TPH + ((b + 1) * NT + AHEAD))
                nc.vector.reciprocal(rinv[:, :], rsum[:, b % 2, :]).then_inc(inv_ready, 1)
                dve.wait_ge(ctx_out[b % 2], h * (B // 2 * 16) + (b // 2 * 16 + DMA_AHEAD))
                nc.vector.tensor_reduce(ctx_sum[:, :, :], ps_o[:, 0:NT * 3 * DH].rearrange("p (i n d) -> p i d n", n=3, d=DH),
                                        AX_X, ALU.add).then_inc(sum_ready, 1)
                dve.wait_ge(inv_ready, h * B + (b + 1))
                dve.wait_ge(sum_ready, h * B + (b + 1))
                nc.vector.tensor_tensor(ctx_sb[:, b % 2, :, :], ctx_sum[:, :, :],
                                        rinv[:, :].unsqueeze(2).to_broadcast([P, NT, DH]), ALU.mult).then_inc(ctx_ready, 1)

            def rest(h, s, g):
                if s >= 1:
                    dve.wait_ge(lo_done, h * (2 * TPH) + (2 * s + g - 1))
                dve.wait_ge(hi_done, h * (2 * TPH) + (2 * s + g + 1))
                nc.vector.tensor_tensor(pr[:, g, :], ps_t[:, :], pT[:, s % 2, 0, 4 * g:4 * g + 4, :].rearrange("p a n -> p (a n)"),
                                        ALU.subtract).then_inc(rest_done, 1)

            def step(h, s, behind=2, ahead=True):
                hh, ss = (h + 1, s - TPH) if s >= TPH else (h, s)
                if behind >= 2:
                    rest(h, s - 2, 1)
                row_max(hh, ss)
                if behind >= 1:
                    rest(h, s - 1, 0)
                if s > NT and s % NT == 2:
                    normalise(h, s // NT - 1)
                if ahead and s % NT in (3, 5):
                    products(h, s // NT + 1, (s % NT) // 5)

            dve.wait_ge(consts, NCONST)
            dve.sem_inc(ctx_ready, AHEAD)
            for hf in range(2):
                products(0, 0, hf)
            for s in range(3):
                step(0, s, behind=s)
            with dve.Fori(0, H - 1) as h:
                for s in range(3, TPH + 3):
                    step(h, s)
            for s in range(3, TPH):
                step(H - 1, s, ahead=(s < TPH - NT))
            rest(H - 1, TPH - 2, 1)
            rest(H - 1, TPH - 1, 0)
            rest(H - 1, TPH - 1, 1)
            normalise(H - 1, B - 1)

        @block.gpsimd
        def _(pool):
            def combine(h, job_off, slot, hf):
                cols = slice(hf * HALF, (hf + 1) * HALF)
                pool.wait_ge(rot_done, (h * B + job_off) * 4 + (2 * hf + 1))
                nc.gpsimd.tensor_tensor(uv[:, slot, 0, cols], r1[:, 0, :], r1[:, 1, :], ALU.add).then_inc(uv_ready, 1)
                pool.wait_ge(rot_done, (h * B + job_off) * 4 + (2 * hf + 2))
                nc.gpsimd.tensor_tensor(uv[:, slot, 1, cols], r2[:, 1, :], r2[:, 0, :], ALU.subtract).then_inc(uv_ready, 1)

            def low(h, s, g):
                pool.wait_ge(mid_done, h * (2 * TPH) + (2 * s + g + 1))
                cols = slice(4 * g, 4 * g + 4)
                nc.gpsimd.tensor_tensor(pT[:, s % 2, 2, cols, :].rearrange("p a n -> p (a n)"), pr[:, g, :],
                                        pT[:, s % 2, 1, cols, :].rearrange("p a n -> p (a n)"), ALU.subtract).then_inc(lo_done, 1)

            def step(h, s, behind=2, ahead=True):
                if behind >= 2:
                    low(h, s - 2, 1)
                if behind >= 1:
                    low(h, s - 1, 0)
                if ahead and s % NT in (3, 5):
                    combine(h, s // NT + 1, (s // NT + 1) % 2, (s % NT) // 5)

            for hf in range(2):
                combine(0, 0, 0, hf)
            for s in range(3):
                step(0, s, behind=s)
            with pool.Fori(0, H - 1) as h:
                for s in range(3, TPH + 3):
                    step(h, s)
            for s in range(3, TPH):
                step(H - 1, s, ahead=(s < TPH - NT))
            low(H - 1, TPH - 2, 1)
            low(H - 1, TPH - 1, 0)
            low(H - 1, TPH - 1, 1)


def project_out(nc, x, ident_in, woT, bo_rows, ctx_s, x1):
    xf = x.rearrange("b t d -> (b t) d")
    with ExitStack() as ctx:
        def sb(name, shape, dt=F32):
            return ctx.enter_context(nc.sbuf_tensor(name, shape, dt))

        def sem(name):
            return ctx.enter_context(nc.semaphore(name))

        ident = sb("c_ident", [P, P])
        wo = sb("c_wo", [P, KC, D])
        bo = sb("c_bo", [P, D])
        NS = 2
        ct = sb("c_ct", [P, NS, D])
        xt = sb("c_xt", [P, NS, D])
        cT = sb("c_cT", [P, NS, KC, P])
        y = sb("c_y", [P, NS, D])
        ps_t = ctx.enter_context(nc.psum_tensor("c_ps_t", [P, NS, HALF], F32))
        ps_y = ctx.enter_context(nc.psum_tensor("c_ps_y", [P, NS, HALF], F32))
        consts = sem("c_consts")
        ctx_in = [sem(f"c_ctx_in{u}") for u in range(NS)]
        y_out = sem("c_y_out")
        tr_ready = sem("c_tr_ready")
        tr_copied = sem("c_tr_copied")
        y_ready = sem("c_y_ready")
        xb_ready = sem("c_xb_ready")
        y_done = sem("c_y_done")
        block = ctx.enter_context(nc.Block())

        @block.sync
        def _(sp):
            sp.dma_start(ident[:, :], ident_in).then_inc(consts, 16)
            sp.dma_start(wo[:, :, :], woT.rearrange("(c p) n -> p c n", p=P)).then_inc(consts, 16)
            sp.dma_start(bo[:, :], bo_rows).then_inc(consts, 16)
            sp.sem_inc(y_out, DMA_AHEAD)
            with sp.Fori(0, TILES // NS) as r:
                for u in range(NS):
                    sp.wait_ge(y_done, r * NS + AHEAD)
                    sp.dma_start(ct[:, u, :], ctx_s[bass.ds(r * (NS * P) + u * P, P), :]).then_inc(ctx_in[u], 16)
                    sp.dma_start(xt[:, u, :], xf[bass.ds(r * (NS * P) + u * P, P), :]).then_inc(ctx_in[u], 16)
                for u in range(NS):
                    sp.wait_ge(y_done, r * NS + (u + 1 + AHEAD))
                    sp.dma_start(x1[bass.ds(r * (NS * P) + u * P, P), :], y[:, u, :]).then_inc(y_out, 16)
            sp.wait_ge(y_out, TILES * 16 + DMA_AHEAD)

        @block.tensor
        def _(pe):
            pe.wait_ge(consts, 48)
            with pe.Fori(0, TILES // NS) as r:
                for u in range(NS):
                    pe.wait_ge(ctx_in[u], r * 32 + 32)
                    for k in range(KC):
                        mm = nc.tensor.transpose(ps_t[:, u, k * P:(k + 1) * P], ct[:, u, k * P:(k + 1) * P], ident[:, :])
                    mm.then_inc(tr_ready, 1)
                for u in range(NS):
                    pe.wait_ge(tr_copied, r * NS + (u + 1))
                    for k in range(KC):
                        mm = nc.tensor.matmul(ps_y[:, u, 0:D], cT[:, u, k, :], wo[:, k, :], start=(k == 0), stop=(k == KC - 1))
                    mm.then_inc(y_ready, 1)

        @block.scalar
        def _(act):
            with act.Fori(0, TILES // NS) as r:
                for u in range(NS):
                    act.wait_ge(tr_ready, r * NS + (u + 1))
                    nc.scalar.copy(cT[:, u, :, :].rearrange("p k n -> p (k n)"), ps_t[:, u, 0:D]).then_inc(tr_copied, 1)

        @block.vector
        def _(dve):
            dve.wait_ge(consts, 48)
            dve.sem_inc(y_done, AHEAD)
            with dve.Fori(0, TILES // NS) as r:
                for u in range(NS):
                    dve.wait_ge(ctx_in[u], r * 32 + 32)
                    nc.vector.tensor_tensor(xt[:, u, :], xt[:, u, :], bo[:, :], ALU.add).then_inc(xb_ready, 1)
                for u in range(NS):
                    dve.wait_ge(y_out, r * (NS * 16) + DMA_AHEAD)
                    dve.wait_ge(xb_ready, r * NS + (u + 1))
                    dve.wait_ge(y_ready, r * NS + (u + 1))
                    nc.vector.tensor_tensor(y[:, u, :], ps_y[:, u, 0:D], xt[:, u, :], ALU.add).then_inc(y_done, 1)


def cross_attention(nc, a, x1, x2):
    x1f = x1.rearrange("(b i p) d -> b p i d", p=P, b=B)
    x2f = x2.rearrange("(b i p) d -> b i p d", p=P, b=B)
    with ExitStack() as ctx:
        def sb(name, shape, dt=F32):
            return ctx.enter_context(nc.sbuf_tensor(name, shape, dt))

        def sem(name):
            return ctx.enter_context(nc.semaphore(name))

        G = 4
        NG = H // G
        HC = H // KC
        ident = sb("d_ident", [P, P])
        wq = sb("d_wq", [P, KC, D])
        wkv = sb("d_wkv", [P, KC, 2 * D])
        wo = sb("d_wo", [P, KC, D])
        rows = sb("d_rows", [P, 4, D])
        lnw = sb("d_lnw", [P, 4])
        eps = sb("d_eps", [P, 2])
        yT = sb("d_yT", [P, KC, S2])
        diag = sb("d_diag", [P, HC])
        mask8 = sb("d_mask8", [P, B, S2], mybir.dt.uint8)
        bias = sb("d_bias", [P, B, S2])
        kx = sb("d_kx", [P, D])
        k_sq = sb("d_k_sq", [P, D])
        k_st = sb("d_k_st", [P, 3, H])
        kbd = sb("d_kbd", [P, KC, HC, S2])
        kT = sb("d_kT", [P, KC, S2])
        v_sb = sb("d_v", [P, D])
        xt = sb("d_x", [P, NT, D])
        z = sb("d_z", [P, NT, D])
        st = sb("d_st", [P, NT, 6])
        mv = sb("d_mv", [P, NT, 2])
        sd = sb("d_sd", [P, NT])
        xnT = sb("d_xnT", [P, KC, T])
        q = z
        q_sq = sb("d_q_sq", [P, NT, D])
        q_st = sb("d_q_st", [P, 3, NT * H])
        qT = xnT
        sc = sb("d_sc", [P, 2, H, S2])
        pm = sb("d_pm", [P, 2, H])
        rs = sb("d_rs", [P, 2, H])
        ri = sb("d_ri", [P, 2, H])
        pT = sb("d_pT", [P, 2, H, P])
        cx = sb("d_cx", [P, 2, D])
        cT = sb("d_cT", [P, 2, KC, P])
        xb = sb("d_xb", [P, 2, D])
        y = sb("d_y", [P, 2, D])
        spare = sb("d_spare", [P, 1])
        ps_s = ctx.enter_context(nc.psum_tensor("d_ps_s", [P, NG, HALF], F32))
        ps_t = ctx.enter_context(nc.psum_tensor("d_ps_t", [P, 2, HALF], F32))
        ps_o = ctx.enter_context(nc.psum_tensor("d_ps_o", [P, HALF], F32))
        ps_y = ctx.enter_context(nc.psum_tensor("d_ps_y", [P, HALF], F32))

        consts = sem("d_consts")
        x_in = sem("d_x_in")
        yT_in = sem("d_yT_in")
        y_out = [sem(f"d_y_out{u}") for u in range(2)]
        setup = sem("d_setup")
        chain = sem("d_chain")
        sd_ready = sem("d_sd_ready")
        dev_in = sem("d_dev_in")
        z_ready = sem("d_z_ready")
        tr_ready = sem("d_tr_ready")
        tr_copied = sem("d_tr_copied")
        mm_ready = sem("d_mm_ready")
        mm_used = sem("d_mm_used")
        kbd_ready = sem("d_kbd_ready")
        kT_ready = sem("d_kT_ready")
        sc_ready = sem("d_sc_ready")
        sc_used = sem("d_sc_used")
        sm_max = sem("d_sm_max")
        sm_sum = sem("d_sm_sum")
        sm_inv = sem("d_sm_inv")
        xb_ready = sem("d_xb_ready")
        sub_ready = sem("d_sub_ready")
        exp_done = sem("d_exp_done")
        pT_copied = sem("d_pT_copied")
        pT_ready = sem("d_pT_ready")
        av_ready = sem("d_av_ready")
        cx_ready = sem("d_cx_ready")
        cT_ready = sem("d_cT_ready")
        cT_copied = sem("d_cT_copied")
        y_ready = sem("d_y_ready")
        y_done = sem("d_y_done")
        block = ctx.enter_context(nc.Block())

        NCONST = 9 * 16
        CH = 12
        TRB = 2 * NT // 4 * 2 + 1
        MMB = NT + 2
        HB = HC * DH

        @block.sync
        def _(sp):
            for dst, src in ((ident[:, :], a["ident"]), (wq[:, :, :], a["x_wqT"].rearrange("(c p) n -> p c n", p=P)),
                             (wkv[:, :, :], a["x_wkvT"].rearrange("(c p) n -> p c n", p=P)),
                             (wo[:, :, :], a["x_woT"].rearrange("(c p) n -> p c n", p=P)),
                             (rows[:, :, :], a["x_rows"]), (lnw[:, :], a["x_lnw"]), (eps[:, :], a["eps2"]),
                             (diag[:, :], a["x_diag"]),
                             (mask8[:, :, :], a["mask"])):
                sp.dma_start(dst, src).then_inc(consts, 16)
            for s in y_out:
                sp.sem_inc(s, DMA_AHEAD)
            with sp.Fori(0, B) as b:
                sp.wait_ge(y_done, b * NT + AHEAD)
                sp.dma_start(yT[:, :, :], a["ctxT"].rearrange("b (c p) s -> b p c s", p=P)[b, :, :, :]).then_inc(yT_in, 16)
                sp.dma_start(xt[:, :, :], x1f[b, :, :, :]).then_inc(x_in, 16)
                for i in range(NT):
                    sp.wait_ge(y_done, b * NT + (i + 1 + AHEAD))
                    sp.dma_start(x2f[b, i, :, :], y[:, i % 2, :]).then_inc(y_out[i % 2], 16)
            for s in y_out:
                sp.wait_ge(s, TILES // 2 * 16 + DMA_AHEAD)

        @block.vector
        def _(dve):
            def bc(v, n, w):
                return v.unsqueeze(2).to_broadcast([P, n, w])

            dve.wait_ge(consts, NCONST)
            nc.vector.tensor_scalar(bias[:, :, :], mask8[:, :, :], 1.0, 1e30, ALU.subtract, ALU.mult).then_inc(setup, 1)
            dve.wait_ge(setup, 1)
            dve.sem_inc(y_done, AHEAD)
            dve.sem_inc(sc_used, AHEAD)
            with dve.Fori(0, B) as b:
                steps = [0]

                def then(ins):
                    steps[0] += 1
                    ins.then_inc(chain, 1)
                    dve.wait_ge(chain, b * CH + steps[0])

                dve.wait_ge(x_in, b * 16 + 16)
                for i in range(NT):
                    last = nc.vector.bn_stats(st[:, i, :], xt[:, i, :])
                then(last)
                nc.vector.memset(spare[:, :], 0.0)
                for i in range(NT):
                    last = nc.vector.bn_aggr(mv[:, i, :], st[:, i, :])
                last.then_inc(dev_in, 1)
                dve.wait_ge(sd_ready, b * 3 + 1)
                then(nc.vector.reciprocal(sd[:, :], sd[:, :]))
                for i in range(NT):
                    last = nc.vector.tensor_scalar(z[:, i, :], xt[:, i, :], mv[:, i, 0:1], sd[:, i:i + 1],
                                                   ALU.subtract, ALU.mult)
                last.then_inc(z_ready, 1)

                def head_norm(v, sq, stat, n, p, dev):
                    v3 = v[0:p].rearrange("p (h d) -> p h d", d=DH)
                    q3 = sq[0:p].rearrange("p (h d) -> p h d", d=DH)
                    wide = [p, n, DH]
                    then(nc.vector.tensor_reduce(stat[0:p, 0, :], v3, AX_X, ALU.add))
                    then(nc.vector.tensor_scalar(stat[0:p, 0, :], stat[0:p, 0, :], 1.0 / DH, None, ALU.mult))
                    then(nc.vector.tensor_tensor(v3, v3, stat[0:p, 0, :].unsqueeze(2).to_broadcast(wide), ALU.subtract))
                    then(nc.vector.tensor_tensor(q3, v3, v3, ALU.mult))
                    nc.vector.tensor_reduce(stat[0:p, 1, :], q3, AX_X, ALU.add).then_inc(dev_in, 1)
                    dve.wait_ge(sd_ready, b * 3 + dev)
                    then(nc.vector.reciprocal(stat[0:p, 2, :], stat[0:p, 2, :]))
                    return nc.vector.tensor_tensor(v3, v3, stat[0:p, 2, :].unsqueeze(2).to_broadcast(wide), ALU.mult)

                dve.wait_ge(mm_ready, b * MMB + 1)
                nc.vector.tensor_tensor(kx[0:S2, :], ps_y[0:S2, 0:D], rows[0:S2, 1, :], ALU.add).then_inc(mm_used, 1)
                dve.wait_ge(mm_ready, b * MMB + 2)
                nc.vector.tensor_tensor(v_sb[0:S2, :], ps_o[0:S2, 0:D], rows[0:S2, 2, :], ALU.add).then_inc(mm_used, 1)
                dve.wait_ge(mm_used, b * MMB + 2)
                head_norm(kx[:, :], k_sq[:, :], k_st, H, S2, 2).then_inc(z_ready, 1)
                for g in range(2 * NT // 4):
                    dve.wait_ge(tr_ready, b * TRB + (g + 1))
                    nc.vector.tensor_copy(xnT[:, g // 2, (g % 2) * HALF:(g % 2 + 1) * HALF], ps_t[:, g % 2, :]).then_inc(tr_copied, 1)
                dve.wait_ge(tr_ready, b * TRB + 5)
                nc.vector.tensor_scalar(kT[:, :, :], ps_t[:, 0, 0:KC * S2].rearrange("p (c s) -> p c s", c=KC),
                                        lnw[:, 2:3], lnw[:, 3:4], ALU.mult, ALU.add).then_inc(kT_ready, 1)
                dve.wait_ge(kT_ready, b + 1)
                for c in range(KC):
                    last = nc.vector.tensor_tensor(kbd[:, c, :, :], kT[:, c:c + 1, :].to_broadcast([P, HC, S2]),
                                                   bc(diag[:, :], HC, S2), ALU.mult)
                last.then_inc(kbd_ready, 1)
                for i in range(NT):
                    dve.wait_ge(mm_ready, b * MMB + (i + 3))
                    bank = ps_y if i % 2 == 0 else ps_o
                    nc.vector.tensor_tensor(q[:, i, :], bank[:, 0:D], rows[:, 0, :], ALU.add).then_inc(mm_used, 1)
                dve.wait_ge(mm_used, b * MMB + MMB)
                head_norm(q[:, :, :].rearrange("p i n -> p (i n)"), q_sq[:, :, :].rearrange("p i n -> p (i n)"),
                          q_st, NT * H, P, 3).then_inc(z_ready, 1)
                for g in range(2 * NT // 4):
                    dve.wait_ge(tr_ready, b * TRB + (g + 6))
                    nc.vector.tensor_scalar(qT[:, g // 2, (g % 2) * HALF:(g % 2 + 1) * HALF], ps_t[:, (g + 1) % 2, :],
                                            lnw[:, 0:1], lnw[:, 1:2], ALU.mult, ALU.add).then_inc(tr_copied, 1)
                assert steps[0] == CH, steps

                def soft_a(i):
                    u = i % 2
                    dve.wait_ge(sc_ready, b * NT + (i + 1))
                    for g in range(NG):
                        last = nc.vector.tensor_tensor(sc[:, u, g * G:(g + 1) * G, :],
                                                       ps_s[:, g, 0:G * S2].rearrange("p (h s) -> p h s", s=S2),
                                                       bias[:, bass.ds(b, 1), :].to_broadcast([P, G, S2]), ALU.add)
                    last.then_inc(sc_used, 1)
                    dve.wait_ge(sc_used, b * NT + (i + 1 + AHEAD))
                    nc.vector.tensor_reduce(pm[:, u, :], sc[:, u, :, :], AX_X, ALU.max).then_inc(sm_max, 1)
                    dve.wait_ge(sm_max, b * NT + (i + 1))
                    nc.vector.tensor_tensor(sc[:, u, :, :], sc[:, u, :, :], bc(pm[:, u, :], H, S2), ALU.subtract).then_inc(sub_ready, 1)

                def soft_b(i):
                    u = i % 2
                    dve.wait_ge(exp_done, b * NT + (i + 1))
                    nc.vector.tensor_reduce(rs[:, u, :], sc[:, u, :, :], AX_X, ALU.add).then_inc(sm_sum, 1)
                    dve.wait_ge(sm_sum, b * NT + (i + 1))
                    nc.vector.reciprocal(ri[:, u, :], rs[:, u, :]).then_inc(sm_inv, 1)

                def context(i):
                    u = i % 2
                    dve.wait_ge(sm_inv, b * NT + (i + 1))
                    dve.wait_ge(av_ready, b * NT + (i + 1))
                    nc.vector.tensor_tensor(cx[:, u, :].rearrange("p (h d) -> p h d", d=DH),
                                            ps_o[:, 0:D].rearrange("p (h d) -> p h d", d=DH), bc(ri[:, u, :], H, DH),
                                            ALU.mult).then_inc(cx_ready, 1)

                def result(i):
                    u = i % 2
                    dve.wait_ge(y_out[u], b * (NT // 2 * 16) + (i // 2 * 16 + DMA_AHEAD))
                    nc.vector.tensor_tensor(xb[:, u, :], xt[:, i, :], rows[:, 3, :], ALU.add).then_inc(xb_ready, 1)
                    dve.wait_ge(xb_ready, b * NT + (i + 1))
                    dve.wait_ge(y_ready, b * NT + (i + 1))
                    nc.vector.tensor_tensor(y[:, u, :], ps_y[:, 0:D], xb[:, u, :], ALU.add).then_inc(y_done, 1)

                for i in range(NT + 2):
                    if i < NT:
                        soft_a(i)
                    if 1 <= i <= NT:
                        soft_b(i - 1)
                        context(i - 1)
                    if i >= 2:
                        result(i - 2)

        @block.scalar
        def _(act):
            act.wait_ge(consts, NCONST)
            act.sem_inc(pT_copied, AHEAD)
            with act.Fori(0, B) as b:
                act.wait_ge(dev_in, b * 3 + 1)
                nc.scalar.activation(sd[:, :], mv[:, :, 1], ACT.Sqrt, bias=eps[:, 0:1]).then_inc(sd_ready, 1)
                act.wait_ge(dev_in, b * 3 + 2)
                nc.scalar.activation(k_st[0:S2, 2, :], k_st[0:S2, 1, :], ACT.Sqrt, bias=eps[0:S2, 1:2], scale=1.0 / DH).then_inc(sd_ready, 1)
                act.wait_ge(dev_in, b * 3 + 3)
                nc.scalar.activation(q_st[:, 2, :], q_st[:, 1, :], ACT.Sqrt, bias=eps[:, 1:2], scale=1.0 / DH).then_inc(sd_ready, 1)

                def exp(i):
                    u = i % 2
                    act.wait_ge(sub_ready, b * NT + (i + 1))
                    nc.scalar.activation(sc[:, u, :, :], sc[:, u, :, :], ACT.Exp, scale=SCALE).then_inc(exp_done, 1)

                def copy_pT(i):
                    u = i % 2
                    for g in range(NG):
                        act.wait_ge(pT_ready, b * (NT * NG) + (i * NG + g + 1))
                        nc.scalar.copy(pT[0:S2, u, g * G:(g + 1) * G, :].rearrange("p g n -> p (g n)"),
                                       ps_t[0:S2, g % 2, :]).then_inc(pT_copied, 1)

                def copy_cT(i):
                    u = i % 2
                    act.wait_ge(cT_ready, b * NT + (i + 1))
                    nc.scalar.copy(cT[:, u, :, :].rearrange("p c n -> p (c n)"), ps_y[:, D:2 * D]).then_inc(cT_copied, 1)

                for i in range(NT + 2):
                    if i >= 2:
                        copy_cT(i - 2)
                    if i < NT:
                        exp(i)
                    if 1 <= i <= NT:
                        copy_pT(i - 1)

        @block.tensor
        def _(pe):
            pe.wait_ge(consts, NCONST)
            with pe.Fori(0, B) as b:
                pe.wait_ge(y_done, b * NT + AHEAD)
                pe.wait_ge(yT_in, b * 16 + 16)
                for w, bank in ((0, ps_y), (1, ps_o)):
                    for k in range(KC):
                        mm = nc.tensor.matmul(bank[0:S2, 0:D], yT[:, k, :], wkv[:, k, w * D:(w + 1) * D],
                                              start=(k == 0), stop=(k == KC - 1))
                    mm.then_inc(mm_ready, 1)
                pe.wait_ge(z_ready, b * 3 + 1)
                for g in range(2 * NT // 4):
                    c, i0 = g // 2, 4 * (g % 2)
                    if g >= 2:
                        pe.wait_ge(tr_copied, b * 8 + (g - 1))
                    for i in range(4):
                        mm = nc.tensor.transpose(ps_t[:, g % 2, i * P:(i + 1) * P], z[:, i0 + i, c * P:(c + 1) * P], ident[:, :])
                    mm.then_inc(tr_ready, 1)
                pe.wait_ge(z_ready, b * 3 + 2)
                pe.wait_ge(tr_copied, b * 8 + 4)
                for c in range(KC):
                    mm = nc.tensor.transpose(ps_t[:, 0, c * S2:(c + 1) * S2], kx[0:S2, c * P:(c + 1) * P], ident[0:S2, 0:S2])
                mm.then_inc(tr_ready, 1)
                for i in range(NT):
                    pe.wait_ge(mm_used, b * MMB + (i + 1))
                    bank = ps_y if i % 2 == 0 else ps_o
                    for k in range(KC):
                        mm = nc.tensor.matmul(bank[:, 0:D], xnT[:, k, i * P:(i + 1) * P], wq[:, k, :], start=(k == 0), stop=(k == KC - 1))
                    mm.then_inc(mm_ready, 1)
                pe.wait_ge(z_ready, b * 3 + 3)
                pe.wait_ge(kT_ready, b + 1)
                for g in range(2 * NT // 4):
                    c, i0 = g // 2, 4 * (g % 2)
                    if g >= 2:
                        pe.wait_ge(tr_copied, b * 8 + (4 + g - 1))
                    for i in range(4):
                        mm = nc.tensor.transpose(ps_t[:, (g + 1) % 2, i * P:(i + 1) * P], q[:, i0 + i, c * P:(c + 1) * P], ident[:, :])
                    mm.then_inc(tr_ready, 1)
                pe.wait_ge(tr_copied, b * 8 + 8)
                pe.wait_ge(kbd_ready, b + 1)

                def scores(i):
                    pe.wait_ge(sc_used, b * NT + (i + AHEAD))
                    for g in range(NG):
                        c, h0 = g * G // HC, g * G % HC
                        mm = nc.tensor.matmul(ps_s[:, g, 0:G * S2], qT[:, c, i * P:(i + 1) * P],
                                              kbd[:, c, h0:h0 + G, :].rearrange("p h s -> p (h s)"), start=True, stop=True)
                    mm.then_inc(sc_ready, 1)

                def transposes(i):
                    u = i % 2
                    pe.wait_ge(exp_done, b * NT + (i + 1))
                    for g in range(NG):
                        pe.wait_ge(pT_copied, b * (NT * NG) + max(i * NG + g - 1 + AHEAD, AHEAD))
                        for h in range(G):
                            mm = nc.tensor.transpose(ps_t[0:S2, g % 2, h * P:(h + 1) * P], sc[:, u, g * G + h, :], ident[:, :])
                        mm.then_inc(pT_ready, 1)

                def context(i):
                    u = i % 2
                    pe.wait_ge(pT_copied, b * (NT * NG) + (i * NG + NG + AHEAD))
                    if i:
                        pe.wait_ge(cx_ready, b * NT + i)
                    for h in range(H):
                        mm = nc.tensor.matmul(ps_o[:, h * DH:(h + 1) * DH], pT[0:S2, u, h, :], v_sb[0:S2, h * DH:(h + 1) * DH],
                                              start=True, stop=True)
                    mm.then_inc(av_ready, 1)

                def out_t(i):
                    u = i % 2
                    pe.wait_ge(cx_ready, b * NT + (i + 1))
                    pe.wait_ge(y_done, b * NT + (i + AHEAD))
                    for c in range(KC):
                        mm = nc.tensor.transpose(ps_y[:, D + c * P:D + (c + 1) * P], cx[:, u, c * P:(c + 1) * P], ident[:, :])
                    mm.then_inc(cT_ready, 1)

                def out(i):
                    u = i % 2
                    pe.wait_ge(cT_copied, b * NT + (i + 1))
                    for k in range(KC):
                        mm = nc.tensor.matmul(ps_y[:, 0:D], cT[:, u, k, :], wo[:, k, :], start=(k == 0), stop=(k == KC - 1))
                    mm.then_inc(y_ready, 1)

                for i in range(NT + 2):
                    if i >= 2:
                        out_t(i - 2)
                    if i < NT:
                        scores(i)
                    if i >= 2:
                        out(i - 2)
                    if 1 <= i <= NT:
                        transposes(i - 1)
                        context(i - 1)


def ffn_norm(nc, a, x2, xr_s):
    x2f = x2.rearrange("(b i p) d -> b p i d", p=P, b=B)
    with ExitStack() as ctx:
        def sb(name, shape, dt=F32):
            return ctx.enter_context(nc.sbuf_tensor(name, shape, dt))

        def sem(name):
            return ctx.enter_context(nc.semaphore(name))

        ident = sb("e_ident", [P, P])
        nw = sb("e_nw", [P, KC])
        eps = sb("e_eps", [P, 1])
        xt = sb("e_x", [P, NT, D])
        st = sb("e_st", [P, NT, 6])
        mv = sb("e_mv", [P, NT, 2])
        m2 = sb("e_m2", [P, NT])
        sd = sb("e_sd", [P, NT])
        xrT = sb("e_xrT", [P, KC, T])
        spare = sb("e_spare", [P, 1])
        ps_t = ctx.enter_context(nc.psum_tensor("e_ps_t", [P, 2, HALF], F32))
        consts = sem("e_consts")
        x_in = sem("e_x_in")
        xr_out = sem("e_xr_out")
        chain = sem("e_chain")
        dev_in = sem("e_dev_in")
        sd_ready = sem("e_sd_ready")
        z_ready = sem("e_z_ready")
        tr_ready = sem("e_tr_ready")
        tr_used = sem("e_tr_used")
        block = ctx.enter_context(nc.Block())
        NG = KC * NT // 4
        CH = 7

        @block.sync
        def _(sp):
            sp.dma_start(ident[:, :], a["ident"]).then_inc(consts, 16)
            with nc.allow_non_contiguous_dma(reason="short per-channel vector"):
                sp.dma_start(nw[:, :], a["f_nw"].rearrange("(c p) -> p c", p=P)).then_inc(consts, 16)
            sp.dma_start(eps[:, :], a["eps"]).then_inc(consts, 16)
            sp.sem_inc(xr_out, DMA_AHEAD)
            with sp.Fori(0, B) as b:
                sp.wait_ge(tr_ready, b * NG + AHEAD)
                sp.dma_start(xt[:, :, :], x2f[b, :, :, :]).then_inc(x_in, 16)
                sp.wait_ge(tr_used, b * NG + NG)
                sp.dma_start(xr_s[:, bass.ds(b * T, T)].rearrange("(c p) n -> p c n", p=P), xrT[:, :, :]).then_inc(xr_out, 16)
            sp.wait_ge(xr_out, B * 16 + DMA_AHEAD)

        @block.vector
        def _(dve):
            dve.wait_ge(consts, 48)
            with dve.Fori(0, B) as b:
                steps = [0]

                def then(ins):
                    steps[0] += 1
                    ins.then_inc(chain, 1)
                    dve.wait_ge(chain, b * CH + steps[0])

                def stats():
                    for i in range(NT):
                        last = nc.vector.bn_stats(st[:, i, :], xt[:, i, :])
                    then(last)
                    nc.vector.memset(spare[:, :], 0.0)
                    for i in range(NT):
                        last = nc.vector.bn_aggr(mv[:, i, :], st[:, i, :])
                    return last

                dve.wait_ge(x_in, b * 16 + 16)
                stats().then_inc(dev_in, 1)
                dve.wait_ge(sd_ready, b * 2 + 1)
                then(nc.vector.reciprocal(sd[:, :], sd[:, :]))
                for i in range(NT):
                    last = nc.vector.tensor_scalar(xt[:, i, :], xt[:, i, :], mv[:, i, 0:1], sd[:, i:i + 1], ALU.subtract, ALU.mult)
                then(last)
                then(stats())
                then(nc.vector.tensor_tensor(m2[:, :], mv[:, :, 0], mv[:, :, 0], ALU.mult))
                nc.vector.tensor_tensor(m2[:, :], m2[:, :], mv[:, :, 1], ALU.add).then_inc(dev_in, 1)
                dve.wait_ge(sd_ready, b * 2 + 2)
                then(nc.vector.reciprocal(sd[:, :], sd[:, :]))
                assert steps[0] == CH, steps
                for i in range(NT):
                    last = nc.vector.tensor_scalar(xt[:, i, :], xt[:, i, :], sd[:, i:i + 1], None, ALU.mult)
                last.then_inc(z_ready, 1)
                for g in range(NG):
                    if g == 0:
                        dve.wait_ge(xr_out, b * 16 + DMA_AHEAD)
                    dve.wait_ge(tr_ready, b * NG + (g + 1 + AHEAD))
                    nc.vector.tensor_scalar(xrT[:, g // 2, (g % 2) * HALF:(g % 2 + 1) * HALF], ps_t[:, g % 2, :],
                                            nw[:, g // 2:g // 2 + 1], None, ALU.mult).then_inc(tr_used, 1)

        @block.scalar
        def _(act):
            act.wait_ge(consts, 48)
            with act.Fori(0, B) as b:
                act.wait_ge(dev_in, b * 2 + 1)
                nc.scalar.activation(sd[:, :], mv[:, :, 1], ACT.Sqrt, bias=eps[:, 0:1]).then_inc(sd_ready, 1)
                act.wait_ge(dev_in, b * 2 + 2)
                nc.scalar.activation(sd[:, :], m2[:, :], ACT.Sqrt, bias=eps[:, 0:1]).then_inc(sd_ready, 1)

        @block.tensor
        def _(pe):
            pe.wait_ge(consts, 48)
            pe.sem_inc(tr_ready, AHEAD)
            with pe.Fori(0, B) as b:
                pe.wait_ge(z_ready, b + 1)
                for g in range(NG):
                    c, i0 = g // 2, 4 * (g % 2)
                    if g >= 2:
                        pe.wait_ge(tr_used, b * NG + (g - 1))
                    for i in range(4):
                        mm = nc.tensor.transpose(ps_t[:, g % 2, i * P:(i + 1) * P], xt[:, i0 + i, c * P:(c + 1) * P], ident[:, :])
                    mm.then_inc(tr_ready, 1)


def experts(nc, a, x2, xr_s, out):
    NK = 64
    NC = 32
    FH = 8
    K = 16
    GS = 2 * FH
    NP0, NP1, NP2 = K, 7 * 8, 8
    NP = NP0 + NP1 + NP2
    LOW = -3e38
    with ExitStack() as ctx:
        def sb(name, shape, dt=F32):
            return ctx.enter_context(nc.sbuf_tensor(name, shape, dt))

        def sem(name):
            return ctx.enter_context(nc.semaphore(name))

        def pb(name, shape):
            return ctx.enter_context(nc.psum_tensor(name, shape, F32))

        ident = sb("f_ident", [P, P])
        km = sb("f_km", [P, KC, GS * NK])
        iota = sb("f_iota", [P, NC, P], BF16)
        iota16 = sb("f_iota16", [P, K], BF16)
        xs = sb("f_xs", [P, KC, P])
        xh = sb("f_xh", [P, KC, P])
        x2t = sb("f_x2", [P, D])
        y = sb("f_y", [P, D])
        sim = sb("f_sim", [P, GS, NK])
        top = sb("f_top", [P, FH, 2, K])
        topi = sb("f_topi", [P, GS, K], U32)
        topf = sb("f_topf", [P, FH, 2, K], BF16)
        cand = sb("f_cand", [P, FH, NP])
        val = sb("f_val", [P, FH, K])
        ci = sb("f_ci", [P, FH * K], U32)
        cg = sb("f_cg", [P, FH * K], U32)
        cf = sb("f_cf", [P, 8, FH * K])
        ab = sb("f_ab", [P, 2, FH * K], BF16)
        isel = sb("f_isel", [P, 2, FH * K])
        hi = sb("f_hi", [P, FH * K])
        pick = sb("f_pick", [P, 3, FH * K])
        pickT = sb("f_pickT", [P, 2, P], BF16)
        rowT = sb("f_rowT", [P, P // NC, P], BF16)
        wf = sb("f_wf", [P, P])
        wr = sb("f_wr", [P, P])
        wpart = sb("f_wpart", [P, 3, P], BF16)
        rowhot = sb("f_rowhot", [P, P, P], BF16)
        colhot = sb("f_colhot", [P, NC, P], BF16)
        eq = colhot[:, :, :].rearrange("p c n -> p (c n)").rearrange("p (s h k j) -> p s h k j", s=2, h=FH, k=K)
        colw = sb("f_colw", [P, 3, NC, P], BF16)
        gel = sb("f_gel", [P, NC, P])
        wd = sb("f_wd", [P, NC, P])
        spare = sb("f_spare", [P, 1])
        ps_s = pb("f_ps_s", [P, 2, HALF])
        ps_x = pb("f_ps_x", [P, HALF])
        ps_h = pb("f_ps_h", [P, 2, HALF])
        ps_w = pb("f_ps_w", [P, 2, HALF])
        ps_y = pb("f_ps_y", [P, HALF])

        consts = sem("f_consts")
        kw_in = sem("f_kw_in")
        km_ready = sem("f_km_ready")
        km_copied = sem("f_km_copied")
        xs_in = sem("f_xs_in")
        xh_in = sem("f_xh_in")
        x2_in = sem("f_x2_in")
        y_out = sem("f_y_out")
        sim_ready = sem("f_sim_ready")
        sim_copied = sem("f_sim_copied")
        chain = sem("f_chain")
        pick_ready = sem("f_pick_ready")
        pickT_ready = sem("f_pickT_ready")
        pickT_copied = sem("f_pickT_copied")
        hot_parts = sem("f_hot_parts")
        hot_ready = sem("f_hot_ready")
        h_ready = sem("f_h_ready")
        gel_done = sem("f_gel_done")
        w_ready = sem("f_w_ready")
        w_copied = sem("f_w_copied")
        gw_ready = sem("f_gw_ready")
        y_ready = sem("f_y_ready")
        y_done = sem("f_y_done")

        NH, NW, NG = NC // 4, P // 16, 4
        with ExitStack() as early:
            wqk = early.enter_context(nc.sbuf_tensor("g_wqT", [P, GS, D], F32))
            keysT = early.enter_context(nc.sbuf_tensor("g_keysT", [P, GS, NK], F32))
            with nc.Block() as block:
                @block.sync
                def _(sp):
                    sp.dma_start(wqk[:, :, :], a["f_wqT"].rearrange("(g p) n -> p g n", p=P)).then_inc(kw_in, 16)
                    sp.dma_start(keysT[:, :, :], a["f_keysT"]).then_inc(kw_in, 16)

                @block.tensor
                def _(pe):
                    pe.wait_ge(kw_in, 32)
                    for n in range(KC * 2):
                        c, hf = n // 2, n % 2
                        if n >= 2:
                            pe.wait_ge(km_copied, n - 1)
                        for g in range(8):
                            mm = nc.tensor.matmul(ps_s[:, n % 2, g * NK:(g + 1) * NK], wqk[:, hf * 8 + g, c * P:(c + 1) * P],
                                                  keysT[:, hf * 8 + g, :], start=True, stop=True)
                        mm.then_inc(km_ready, 1)

                @block.scalar
                def _(act):
                    for n in range(KC * 2):
                        c, hf = n // 2, n % 2
                        act.wait_ge(km_ready, n + 1)
                        nc.scalar.copy(km[:, c, hf * HALF:(hf + 1) * HALF], ps_s[:, n % 2, :]).then_inc(km_copied, 1)

        dn = sb("f_dn", [P, KC, NC * P])
        up = sb("f_up", [P, NC, D])
        block = ctx.enter_context(nc.Block())

        @block.sync
        def _(sp):
            for dst, src in ((ident[:, :], a["ident"]), (iota[:, :, :], a["f_iota"]), (iota16[:, :], a["f_iota16"]),
                             (dn[:, :, :], a["f_dnT"].rearrange("(c p) n -> p c n", p=P)), (up[:, :, :], a["f_up"])):
                sp.dma_start(dst, src).then_inc(consts, 16)

            def cols(t):
                return xr_s[:, bass.ds(t * P, P)].rearrange("(c p) n -> p c n", p=P)

            sp.dma_start(xs[:, :, :], cols(0)).then_inc(xs_in, 16)

            def tile(t, first=False, second=False, last=False):
                if not first:
                    sp.wait_ge(h_ready, t * NH)
                sp.dma_start(xh[:, :, :], cols(t)).then_inc(xh_in, 16)
                if not last:
                    sp.wait_ge(sim_ready, t + 1)
                    sp.dma_start(xs[:, :, :], cols(t + 1)).then_inc(xs_in, 16)
                if first:
                    sp.dma_start(x2t[:, :], x2[0:P, :]).then_inc(x2_in, 16)
                elif not second:
                    store(t - 2)

            def store(t):
                sp.wait_ge(y_done, t + 1)
                sp.dma_start(out[bass.ds(t * P, P), :], y[:, :]).then_inc(y_out, 16)
                if not isinstance(t, int) or t < TILES - 1:
                    sp.dma_start(x2t[:, :], x2[bass.ds(t * P + P, P), :]).then_inc(x2_in, 16)

            tile(0, first=True)
            tile(1, second=True)
            with sp.Fori(2, TILES - 1) as t:
                tile(t)
            tile(TILES - 1, last=True)
            store(TILES - 2)
            store(TILES - 1)
            sp.wait_ge(y_out, TILES * 16)

        @block.tensor
        def _(pe):
            def key_scores(t):
                pe.wait_ge(xs_in, t * 16 + 16)
                if not isinstance(t, int) or t > 0:
                    pe.wait_ge(sim_copied, t * 2)
                for hf in range(2):
                    for k in range(KC):
                        mm = nc.tensor.matmul(ps_s[:, hf, :], xs[:, k, :], km[:, k, hf * HALF:(hf + 1) * HALF],
                                              start=(k == 0), stop=(k == KC - 1))
                mm.then_inc(sim_ready, 1)

            def result(t):
                pe.wait_ge(gw_ready, t * NG + 1)
                if not isinstance(t, int) or t > 0:
                    pe.wait_ge(y_done, t)
                for c in range(NC):
                    if c % (NC // NG) == 0 and c > 0:
                        pe.wait_ge(gw_ready, t * NG + (c // (NC // NG) + 1))
                    mm = nc.tensor.matmul(ps_y[:, 0:D], wd[:, c, :], up[:, c, :], start=(c == 0), stop=(c == NC - 1))
                mm.then_inc(y_ready, 1)

            def tile(t, first=False, last=False):
                pe.wait_ge(xh_in, t * 16 + 16)
                for g in range(NH):
                    if g == NH // 2:
                        pe.wait_ge(pick_ready, t + 1)
                        for n in range(3):
                            mm = nc.tensor.transpose(ps_x[:, n * P:(n + 1) * P], pick[:, n, :], ident[:, :])
                        mm.then_inc(pickT_ready, 1)
                        if not last:
                            key_scores(t + 1)
                    if not (first and g < 2):
                        pe.wait_ge(gel_done, t * NH + (g - 1))
                    for j in range(4):
                        for k in range(KC):
                            mm = nc.tensor.matmul(ps_h[:, g % 2, j * P:(j + 1) * P], dn[:, k, (4 * g + j) * P:(4 * g + j + 1) * P],
                                                  xh[:, k, :], start=(k == 0), stop=(k == KC - 1))
                    mm.then_inc(h_ready, 1)
                if not first:
                    result(t - 1)
                pe.wait_ge(hot_ready, t * 4 + 4)
                for g in range(NW):
                    if not (first and g < 2):
                        pe.wait_ge(w_copied, t * NW + (g - 1))
                    for j in range(16):
                        tok = 16 * g + j
                        for n in range(3):
                            mm = nc.tensor.matmul(ps_w[:, g % 2, j * NC:(j + 1) * NC], rowhot[:, :, tok], colw[:, n, :, tok],
                                                  start=(n == 0), stop=(n == 2))
                    mm.then_inc(w_ready, 1)

            pe.wait_ge(consts, 5 * 16)
            key_scores(0)
            tile(0, first=True)
            with pe.Fori(1, TILES - 1) as t:
                tile(t)
            tile(TILES - 1, last=True)
            result(TILES - 1)

        @block.scalar
        def _(act):
            def copy_scores(t):
                act.wait_ge(sim_ready, t + 1)
                if not isinstance(t, int) or t > 0:
                    act.wait_ge(pick_ready, t)
                for hf in range(2):
                    nc.scalar.copy(sim[:, hf * FH:(hf + 1) * FH, :].rearrange("p g k -> p (g k)"), ps_s[:, hf, :]).then_inc(sim_copied, 1)

            def tile(t, first=False, last=False):
                for g in range(NH):
                    if g == NH // 2:
                        act.wait_ge(pickT_ready, t + 1)
                        nc.scalar.copy(pickT[:, :, :].rearrange("p a n -> p (a n)"), ps_x[:, 0:2 * P]).then_inc(pickT_copied, 1)
                        nc.scalar.copy(wf[:, :], ps_x[:, 2 * P:3 * P]).then_inc(pickT_copied, 1)
                        if not last:
                            copy_scores(t + 1)
                    if not first and g % 2 == 0:
                        act.wait_ge(gw_ready, t * NG - NG + (g // 2 + 1))
                    act.wait_ge(h_ready, t * NH + (g + 1))
                    nc.scalar.activation(gel[:, 4 * g:4 * g + 4, :].rearrange("p c n -> p (c n)"), ps_h[:, g % 2, :], ACT.Gelu).then_inc(gel_done, 1)
                for g in range(NW):
                    if g == 0 and not first:
                        act.wait_ge(y_ready, t)
                    act.wait_ge(w_ready, t * NW + (g + 1))
                    nc.scalar.copy(wd[:, :, 16 * g:16 * g + 16].rearrange("p c n -> p n c"),
                                   ps_w[:, g % 2, :].rearrange("p (n c) -> p n c", c=NC)).then_inc(w_copied, 1)

            copy_scores(0)
            tile(0, first=True)
            with act.Fori(1, TILES - 1) as t:
                tile(t)
            tile(TILES - 1, last=True)

        @block.vector
        def _(dve):
            CH = 24

            def wide(v, n):
                return v.unsqueeze(3).to_broadcast([P, v.shape[1], v.shape[2], n])

            def tile(t, first=False, second=False):
                steps = [0]

                def then(ins, carry=False):
                    steps[0] += 1
                    ins.then_inc(chain, 1)
                    dve.wait_ge(chain, t * CH + steps[0])
                    if carry:
                        nc.vector.memset(spare[:, :], 0.0)

                TT, TS, STT = nc.vector.tensor_tensor, nc.vector.tensor_scalar, nc.vector.scalar_tensor_tensor
                top2 = top[:, :, :, :].rearrange("p h s k -> p (h s) k")
                dve.wait_ge(sim_copied, t * 2 + 2)
                nc.vector.memset(spare[:, :], 0.0)
                for g in range(GS):
                    last = nc.vector.max(top2[:, g, 0:8], sim[:, g, :])
                then(last, carry=True)
                for g in range(GS):
                    nc.vector.max_index(topi[:, g, 0:8], top2[:, g, 0:8], sim[:, g, :])
                    last = nc.vector.match_replace(sim[:, g, :], top2[:, g, 0:8], sim[:, g, :], LOW)
                then(last, carry=True)
                for g in range(GS):
                    last = nc.vector.max(top2[:, g, 8:16], sim[:, g, :])
                then(last, carry=True)
                for g in range(GS):
                    last = nc.vector.max_index(topi[:, g, 8:16], top2[:, g, 8:16], sim[:, g, :])
                then(last)
                nc.vector.tensor_copy(topf[:, :, :, :].rearrange("p h s k -> p (h s) k"), topi[:, :, :])
                s1, s2 = top[:, :, 0, :], top[:, :, 1, :]
                TT(cand[:, :, 0:NP0], s1[:, :, 0:1].to_broadcast([P, FH, K]), s2, ALU.add)
                TT(cand[:, :, NP0:NP0 + NP1].rearrange("p h (a b) -> p h a b", b=8), wide(s1[:, :, 1:8], 8),
                   s2[:, :, 0:8].unsqueeze(2).to_broadcast([P, FH, 7, 8]), ALU.add)
                then(TT(cand[:, :, NP0 + NP1:NP], s1[:, :, 8:16], s2[:, :, 0:1].to_broadcast([P, FH, 8]), ALU.add), carry=True)
                civ = ci[:, :].rearrange("p (h k) -> p h k", k=K)
                for h in range(FH):
                    last = nc.vector.max(val[:, h, 0:8], cand[:, h, :])
                then(last, carry=True)
                for h in range(FH):
                    nc.vector.max_index(civ[:, h, 0:8], val[:, h, 0:8], cand[:, h, :])
                    last = nc.vector.match_replace(cand[:, h, :], val[:, h, 0:8], cand[:, h, :], LOW)
                then(last, carry=True)
                for h in range(FH):
                    last = nc.vector.max(val[:, h, 8:16], cand[:, h, :])
                then(last, carry=True)
                for h in range(FH):
                    last = nc.vector.max_index(civ[:, h, 8:16], val[:, h, 8:16], cand[:, h, :])
                then(last)
                c_f, g_f, e_f, g1, lo, g8, be = (cf[:, n, :] for n in range(7))
                nc.vector.tensor_copy(c_f, ci[:, :])
                then(TS(cg[:, :], ci[:, :], 3, None, ALU.logical_shift_right))
                then(nc.vector.tensor_copy(g_f, cg[:, :]))
                TS(e_f, c_f, -float(NP0 + NP1), 0.0, ALU.add, ALU.max)
                TS(g1, g_f, -1.0, 0.0, ALU.add, ALU.max)
                TS(g8, g_f, 1.0, 8.0, ALU.is_equal, ALU.mult)
                then(STT(out=lo, in0=g_f, scalar=-8.0, in1=c_f, op0=ALU.mult, op1=ALU.add))
                TT(ab[:, 0, :], g1, e_f, ALU.add)
                then(TT(be, lo, e_f, ALU.subtract))
                then(TT(ab[:, 1, :], be, g8, ALU.add))
                if not first:
                    dve.wait_ge(hot_ready, t * 4)
                for s in range(2):
                    r = ab[:, s, :].rearrange("p (h k) -> p h k", k=K)
                    last = TT(eq[:, s], wide(r, K), iota16[:, :].unsqueeze(1).to_broadcast([P, FH * K, K])
                              .rearrange("p (h k) j -> p h k j", k=K), ALU.is_equal)
                then(last)
                for s in range(2):
                    last = TT(eq[:, s], eq[:, s], topf[:, :, s, :].unsqueeze(2).to_broadcast([P, FH, K, K]), ALU.mult)
                then(last)
                eqv = colhot[:, :, :].rearrange("p c n -> p (c n)").rearrange("p (a j) -> p a j", j=K)
                then(TT(eqv[:, :, 0:8], eqv[:, :, 0:8], eqv[:, :, 8:16], ALU.add))
                then(TT(eqv[:, :, 0:4], eqv[:, :, 0:4], eqv[:, :, 4:8], ALU.add))
                then(nc.vector.tensor_reduce(isel[:, :, :].rearrange("p s n -> p (s n)"), eqv[:, :, 0:4], AX_X, ALU.add))
                then(TS(hi[:, :], isel[:, 1, :], float(NC), None, ALU.is_ge))
                STT(out=pick[:, 0, :], in0=hi[:, :], scalar=float(NK), in1=isel[:, 0, :], op0=ALU.mult, op1=ALU.add)
                STT(out=pick[:, 1, :], in0=hi[:, :], scalar=-float(NC), in1=isel[:, 1, :], op0=ALU.mult, op1=ALU.add)
                TS(pick[:, 2, :], val[:, :, :].rearrange("p h k -> p (h k)"), 0.0, None, ALU.max).then_inc(pick_ready, 1)
                if not (first or second):
                    total(t - 2)
                dve.wait_ge(pickT_copied, t * 2 + 2)
                if not first:
                    dve.wait_ge(w_ready, t * NW)
                then(nc.vector.tensor_copy(wpart[:, 0, :], wf[:, :]))
                TT(colhot[:, :, :], iota[:, 0:NC, :], pickT[:, 1:2, :].to_broadcast([P, NC, P]), ALU.is_equal).then_inc(hot_parts, 1)
                then(TT(wr[:, :], wf[:, :], wpart[:, 0, :], ALU.subtract))
                then(nc.vector.tensor_copy(wpart[:, 1, :], wr[:, :]))
                TT(wpart[:, 2, :], wr[:, :], wpart[:, 1, :], ALU.subtract).then_inc(hot_parts, 1)
                for n in range(P // NC):
                    last = TS(rowT[:, n, :], pickT[:, 0, :], -float(NC * n), None, ALU.add)
                then(last)
                for n in range(P // NC):
                    last = TT(rowhot[:, NC * n:NC * (n + 1), :], iota[:, :, :], rowT[:, n:n + 1, :].to_broadcast([P, NC, P]), ALU.is_equal)
                last.then_inc(hot_ready, 1)
                assert steps[0] == CH, steps

            def total(t):
                dve.wait_ge(x2_in, t * 16 + 16)
                if not isinstance(t, int) or t > 0:
                    dve.wait_ge(y_out, t * 16)
                dve.wait_ge(y_ready, t + 1)
                nc.vector.tensor_tensor(y[:, :], ps_y[:, 0:D], x2t[:, :], ALU.add).then_inc(y_done, 1)

            dve.wait_ge(consts, 5 * 16)
            tile(0, first=True)
            tile(1, second=True)
            with dve.Fori(2, TILES) as t:
                tile(t)
            total(TILES - 2)
            total(TILES - 1)

        @block.gpsimd
        def _(pool):
            def product(t):
                pool.wait_ge(gel_done, t * NH + NH)
                pool.wait_ge(w_copied, t * NW + NW)
                for n in range(NG):
                    cols = slice(n * (NC // NG), (n + 1) * (NC // NG))
                    nc.gpsimd.tensor_tensor(wd[:, cols, :], gel[:, cols, :], wd[:, cols, :], ALU.mult).then_inc(gw_ready, 1)

            def tile(t, first=False):
                if not first:
                    product(t - 1)
                for n in range(3):
                    if n < 2:
                        pool.wait_ge(hot_parts, t * 2 + (n + 1))
                    nc.gpsimd.tensor_tensor(colw[:, n], colhot[:, :, :], wpart[:, n:n + 1, :].to_broadcast([P, NC, P]),
                                            ALU.mult).then_inc(hot_ready, 1)

            tile(0, first=True)
            with pool.Fori(1, TILES) as t:
                tile(t)
            product(TILES - 1)


def build(nc, a, out):
    qu_s, qv_s, k_s = (nc.dram_tensor(n, [3, H * DH, N], BF16).ap() for n in ("qu_s", "qv_s", "k_s"))
    v_s = nc.dram_tensor("v_s", [N, 3 * D], BF16).ap()
    wp_s = nc.dram_tensor("wp_s", [3, H * DH, D], BF16).ap()
    ctx_s = nc.dram_tensor("ctx_s", [N, D], F32).ap()
    x1 = nc.dram_tensor("x1_s", [N, D], F32).ap()
    x2 = nc.dram_tensor("x2_s", [N, D], F32).ap()
    xr_s = nc.dram_tensor("xr_s", [D, N], F32).ap()
    project_qkv(nc, a["x"], a["attn_w"], a["attn_vecs"], a["attn_bv"], a["ident"], a["eps"], a["attn_wpos"], qu_s, qv_s, k_s, v_s, wp_s)
    self_attention(nc, a["trig"], a["ident"], qu_s, qv_s, k_s, v_s, wp_s, ctx_s)
    project_out(nc, a["x"], a["ident"], a["attn_woT"], a["attn_bo"], ctx_s, x1)
    cross_attention(nc, a, x1, x2)
    ffn_norm(nc, a, x2, xr_s)
    experts(nc, a, x2, xr_s, out.rearrange("b t d -> (b t) d"))


def kernel(**inputs):
    import concourse.bacc as _bacc
    from concourse.bass_utils import run_bass_kernel_spmd as _run

    def arr(name):
        return np.asarray(inputs[name])

    m = np.arange(0, D, 2).astype(np.float32)
    div = np.exp(m * np.float32(-math.log(10000.0) / D)).astype(np.float64)
    ang = div[:, None] * np.arange(T)[None, :]
    trig = np.stack([np.sin(ang), np.cos(ang), np.sin(ang)], axis=1).astype(np.float32)

    def rows(v):
        return np.broadcast_to(v[None, :], (P, v.shape[0]))

    wpos = arr("L0_attn_Wpos")
    laid = {
        "x": arr("x"),
        "ident": np.eye(P, dtype=np.float32),
        "eps": np.full((P, 1), 1e-5, np.float32),
        "trig": trig,
        "attn_w": np.stack([arr("L0_attn_Wq").T, arr("L0_attn_Wk").T, arr("L0_attn_Wv").T]),
        "attn_vecs": np.stack([arr("L0_attn_bq"), arr("L0_attn_bk"), arr("L0_attn_u_bias").reshape(-1),
                               arr("L0_attn_v_bias").reshape(-1), arr("L0_attn_ln_gamma"), arr("L0_attn_ln_beta")]),
        "attn_bv": rows(arr("L0_attn_bv")),
        "attn_wpos": np.concatenate([wpos[:, 0::2], wpos[:, 1::2]], axis=1),
        "attn_woT": arr("L0_attn_Wout").T,
        "attn_bo": rows(arr("L0_attn_bout")),
        "f_nw": arr("L0_ffn_norm_w"),
        "f_iota": np.broadcast_to(np.arange(32, dtype=np.float32).astype(mybir.dt.np(BF16))[None, :, None], (P, 32, P)),
        "f_iota16": np.broadcast_to(np.arange(16, dtype=np.float32).astype(mybir.dt.np(BF16))[None], (P, 16)),
        "f_wqT": arr("L0_ffn_wq").T,
        "f_keysT": arr("L0_ffn_keys").transpose(3, 0, 2, 1).reshape(P, 16, 64),
        "f_dnT": arr("L0_ffn_expert_down").reshape(64, 2, 32, D).transpose(3, 2, 1, 0).reshape(D, 32 * P),
        "f_up": arr("L0_ffn_expert_up").reshape(64, 2, 32, D).transpose(1, 0, 2, 3).reshape(P, 32, D),
        "ctxT": arr("ctx_1024").transpose(0, 2, 1),
        "mask": np.broadcast_to(arr("mask_BxS2_bk0")[None], (P, B, S2)),
        "eps2": np.broadcast_to(np.array([1e-5, 1e-6], np.float32)[None], (P, 2)),
        "x_diag": (np.arange(P)[:, None] // DH == np.arange(P // DH)[None, :]).astype(np.float32),
        "x_wqT": arr("L0_xattn_Wq").T,
        "x_wkvT": arr("L0_xattn_Wkv").T,
        "x_woT": arr("L0_xattn_Wo").T,
        "x_rows": np.broadcast_to(np.stack([arr("L0_xattn_bq"), arr("L0_xattn_bkv")[:D], arr("L0_xattn_bkv")[D:],
                                            arr("L0_xattn_bo")])[None], (P, 4, D)),
        "x_lnw": np.tile(np.stack([arr("L0_xattn_qn_w"), arr("L0_xattn_qn_b"), arr("L0_xattn_kn_w"),
                                   arr("L0_xattn_kn_b")], axis=1), (P // DH, 1)),
    }
    nc = _bacc.Bacc("TRN2", target_bir_lowering=False, num_devices=1)
    arrays, aps = {}, {}
    for name, v in laid.items():
        v = np.ascontiguousarray(v)
        arrays[f"in_{name}_dram"] = v
        aps[name] = nc.dram_tensor(f"in_{name}_dram", v.shape, mybir.dt.from_np(v.dtype), kind="ExternalInput").ap()
    out = nc.dram_tensor("out_0_dram", (B, T, D), F32, kind="ExternalOutput").ap()
    build(nc, aps, out)
    r = _run(nc, [arrays], core_ids=[0])
    return r.results[0]["out_0_dram"]
```

```python
from contextlib import ExitStack
import math

import numpy as np
import concourse.bass as bass
from concourse import mybir

ALU = mybir.AluOpType
ACT = mybir.ActivationFunctionType
AX_X = mybir.AxisListType.X
F32 = mybir.dt.float32
BF16 = mybir.dt.bfloat16
F32R = mybir.dt.float32r
U32 = mybir.dt.uint32

P = 128
B, T, D = 4, 1024, 256
N = B * T
S2 = 77
KC = D // P
H, DH = 16, 16
NT = T // P
TILES = N // P
HALF = 512
QT = T // 4
SCALE = 1.0 / math.sqrt(DH)

PARTS_Q = (0, 0, 0, 1, 1, 1, 2, 2)
PARTS_K = (0, 1, 2, 0, 1, 2, 0, 1)


AHEAD = 1
DMA_AHEAD = 16


def project_qkv(nc, x, wT, vecs, bv_rows, ident_in, eps_in, wpos, qu_s, qv_s, k_s, v_s, wp_s):
    xf = x.rearrange("b (i p) d -> b p i d", p=P)
    with ExitStack() as ctx:
        def sb(name, shape, dt=F32):
            return ctx.enter_context(nc.sbuf_tensor(name, shape, dt))

        def sem(name):
            return ctx.enter_context(nc.semaphore(name))

        SLOTS = 4
        ident = sb("a_ident", [P, P])
        w_sb = sb("a_w", [P, 3, KC, D])
        vec = sb("a_vec", [P, 7, KC])
        bias = sb("a_bias", [P, 3, KC])
        bv_b = sb("a_bv", [P, D])
        wp_f = sb("a_wp", [P, KC, D])
        wp_r = sb("a_wp_r", [P, KC, D])
        wp_parts = sb("a_wp_parts", [P, 3, KC, D], BF16)
        xt = sb("a_x", [P, NT, D])
        st = sb("a_st", [P, NT, 6])
        mv = sb("a_mv", [P, NT, 2])
        sd = sb("a_sd", [P, NT])
        eps = sb("a_eps", [P, 1])
        spare = sb("a_spare", [P, 1])
        xnT = sb("a_xnT", [P, KC, T])
        parts = sb("a_parts", [P, SLOTS, 3, HALF], BF16)
        resid = sb("a_resid", [P, SLOTS, HALF])
        v_sb = sb("a_v", [P, NT, D])
        v_parts = sb("a_v_parts", [P, NT, H, 3, DH], BF16)
        ps_t = ctx.enter_context(nc.psum_tensor("a_ps_t", [P, 2, HALF], F32))
        ps_p = ctx.enter_context(nc.psum_tensor("a_ps_p", [P, 2, HALF], F32))
        ps_v = ctx.enter_context(nc.psum_tensor("a_ps_v", [P, 2, HALF], F32))

        consts = sem("a_consts")
        x_in = sem("a_x_in")
        wp_out = sem("a_wp_out")
        parts_out = [sem(f"a_parts_out{u}") for u in range(SLOTS)]
        v_out = sem("a_v_out")
        wp_steps = sem("a_wp_steps")
        dve_steps = sem("a_dve_steps")
        var_ready = sem("a_var_ready")
        sd_ready = sem("a_sd_ready")
        z_ready = sem("a_z_ready")
        tr_ready = sem("a_tr_ready")
        tr_used = sem("a_tr_used")
        proj_ready = sem("a_proj_ready")
        high_ready = sem("a_high_ready")
        resid_ready = sem("a_resid_ready")
        mid_ready = sem("a_mid_ready")
        low_ready = sem("a_low_ready")
        vproj_ready = sem("a_vproj_ready")
        v_ready = sem("a_v_ready")
        v_high = sem("a_v_high")
        v_resid = sem("a_v_resid")
        v_mid = sem("a_v_mid")
        v_low = sem("a_v_low")
        unit_free = sem("a_unit_free")
        block = ctx.enter_context(nc.Block())

        UNITS = [(w, c, hf) for hf in range(2) for w in range(3) for c in range(KC)]
        NU = len(UNITS)
        NORM_AT = (4, 6, 8, 10)
        W_OF = (0, 0, 1)
        NCONST = 6 * 16

        def v_part(n):
            return v_parts[:, :, :, n, :].rearrange("p i h d -> p (i h) d")

        v_rows = v_sb[:, :, :].rearrange("p i (h d) -> p (i h) d", d=DH)

        @block.sync
        def _(sp):
            sp.dma_start(xt[:, :, :], xf[0, :, :, :]).then_inc(x_in, 16)
            sp.dma_start(ident[:, :], ident_in).then_inc(consts, 16)
            sp.dma_start(w_sb[:, :, :, :], wT.rearrange("w (c p) n -> p w c n", p=P)).then_inc(consts, 16)
            with nc.allow_non_contiguous_dma(reason="short per-channel vectors"):
                sp.dma_start(vec[:, 0:6, :], vecs.rearrange("v (c p) -> p v c", p=P)).then_inc(consts, 16)
            sp.dma_start(bv_b[:, :], bv_rows).then_inc(consts, 16)
            sp.dma_start(wp_f[:, :, :], wpos.rearrange("(c p) n -> p c n", p=P)).then_inc(consts, 16)
            sp.dma_start(eps[:, :], eps_in).then_inc(consts, 16)
            for s in (*parts_out, v_out):
                sp.sem_inc(s, DMA_AHEAD)
            sp.wait_ge(wp_steps, 5)
            for part in range(3):
                sp.dma_start(wp_s[part].rearrange("(c p) n -> p c n", p=P), wp_parts[:, part, :, :]).then_inc(wp_out, 16)

            def round(b, last=False):
                if not last:
                    sp.wait_ge(tr_ready, b * (2 * NT) + (2 * NT + AHEAD))
                    sp.dma_start(xt[:, :, :], xf[b + 1, :, :, :]).then_inc(x_in, 16)
                for n, (w, c, hf) in enumerate(UNITS):
                    sp.wait_ge(low_ready, b * NU + (n + 1))
                    dst = (qu_s, qv_s, k_s)[w]
                    for part in range(3):
                        sp.dma_start(dst[part, c * P:(c + 1) * P, bass.ds(b * T + hf * HALF, HALF)],
                                     parts[:, n % SLOTS, part, :]).then_inc(parts_out[n % SLOTS], 16)
                sp.wait_ge(v_low, b + (1 + AHEAD))
                sp.dma_start(v_s[bass.ds(b * T, T), :].rearrange("(i p) n -> p i n", p=P),
                             v_parts[:, :, :, :, :].rearrange("p i h n d -> p i (h n d)")).then_inc(v_out, 16)

            with sp.Fori(0, B - 1) as b:
                round(b)
            round(B - 1, last=True)
            sp.wait_ge(wp_out, 3 * 16)
            for u in range(SLOTS):
                sp.wait_ge(parts_out[u], B * (NU // SLOTS) * 3 * 16 + DMA_AHEAD)
            sp.wait_ge(v_out, B * 16 + DMA_AHEAD)

        @block.vector
        def _(dve):
            dve.wait_ge(consts, NCONST)
            nc.vector.tensor_copy(wp_parts[:, 0], wp_f[:, :, :]).then_inc(wp_steps, 1)
            dve.wait_ge(wp_steps, 1)
            nc.vector.tensor_tensor(wp_r[:, :, :], wp_f[:, :, :], wp_parts[:, 0], ALU.subtract).then_inc(wp_steps, 1)
            dve.wait_ge(wp_steps, 2)
            nc.vector.tensor_copy(wp_parts[:, 1], wp_r[:, :, :]).then_inc(wp_steps, 1)
            dve.wait_ge(wp_steps, 3)
            nc.vector.tensor_tensor(wp_parts[:, 2], wp_r[:, :, :], wp_parts[:, 1], ALU.subtract).then_inc(wp_steps, 1)
            nc.vector.tensor_tensor(bias[:, 0, :], vec[:, 0, :], vec[:, 2, :], ALU.add)
            nc.vector.tensor_tensor(bias[:, 1, :], vec[:, 0, :], vec[:, 3, :], ALU.add)
            nc.vector.tensor_copy(bias[:, 2, :], vec[:, 1, :]).then_inc(wp_steps, 1)
            def carry(spare):
                nc.vector.memset(spare, 0.0)

            def norm_piece(b, piece):
                rnd = piece // 2
                if piece % 2 == 0:
                    if rnd == 0:
                        dve.wait_ge(x_in, b * 16 + 16)
                    else:
                        dve.wait_ge(dve_steps, b * 5 + 3)
                    for i in range(NT):
                        last = nc.vector.bn_stats(st[:, i, :], xt[:, i, :])
                    last.then_inc(dve_steps, 1)
                    dve.wait_ge(dve_steps, b * 5 + (3 * rnd + 1))
                    carry(spare[:, :])
                    for i in range(NT):
                        last = nc.vector.bn_aggr(mv[:, i, :], st[:, i, :])
                    last.then_inc(var_ready, 1)
                else:
                    dve.wait_ge(sd_ready, b * 2 + (rnd + 1))
                    nc.vector.reciprocal(sd[:, :], sd[:, :]).then_inc(dve_steps, 1)
                    dve.wait_ge(dve_steps, b * 5 + (3 * rnd + 2))
                    for i in range(NT):
                        last = nc.vector.tensor_scalar(xt[:, i, :], xt[:, i, :], mv[:, i, 0:1], sd[:, i:i + 1],
                                                       ALU.subtract, ALU.mult)
                    last.then_inc(dve_steps if rnd == 0 else z_ready, 1)

            def round(b, last=False):
                for g in range(2 * NT // 4):
                    c, i0 = g // 2, 4 * (g % 2)
                    dve.wait_ge(tr_ready, b * (2 * NT) + (4 * g + 4 + AHEAD))
                    nc.vector.tensor_scalar(xnT[:, c, i0 * P:(i0 + 4) * P], ps_t[:, g % 2, :],
                                            vec[:, 4, c:c + 1], vec[:, 5, c:c + 1], ALU.mult, ALU.add).then_inc(tr_used, 1)
                for i in range(NT):
                    if i == 0:
                        dve.wait_ge(v_low, b + AHEAD)
                    dve.wait_ge(vproj_ready, b * NT + (i + 1))
                    nc.vector.tensor_tensor(v_sb[:, i, :], ps_v[:, i % 2, 0:D], bv_b[:, :], ALU.add).then_inc(v_ready, 1)

                def rest(n):
                    w, c, hf = UNITS[n]
                    dve.wait_ge(high_ready, b * NU + (n + 1))
                    nc.vector.scalar_tensor_tensor(out=resid[:, n % SLOTS, :], in0=ps_p[:, n % 2, :], scalar=bias[:, w, c:c + 1],
                                                   in1=parts[:, n % SLOTS, 0, :], op0=ALU.add, op1=ALU.subtract).then_inc(resid_ready, 1)

                def low(n):
                    dve.wait_ge(mid_ready, b * NU + (n + 1))
                    nc.vector.tensor_tensor(parts[:, n % SLOTS, 2, :], resid[:, n % SLOTS, :], parts[:, n % SLOTS, 1, :],
                                            ALU.subtract).then_inc(low_ready, 1)

                rest(0)
                for n in range(1, NU):
                    rest(n)
                    low(n - 1)
                    if not last and n in NORM_AT:
                        norm_piece(b + 1, NORM_AT.index(n))
                low(NU - 1)

            for piece in range(4):
                norm_piece(0, piece)
            with dve.Fori(0, B - 1) as b:
                round(b)
            round(B - 1, last=True)

        @block.scalar
        def _(act):
            act.wait_ge(wp_steps, 5)

            def deviation(b, rnd):
                act.wait_ge(var_ready, b * 2 + (rnd + 1))
                nc.scalar.activation(sd[:, :], mv[:, :, 1], ACT.Sqrt, bias=eps[:, 0:1]).then_inc(sd_ready, 1)

            def round(b, last=False):
                def high(n):
                    w, c, hf = UNITS[n]
                    act.wait_ge(parts_out[n % SLOTS], b * (NU // SLOTS * 48) + (n // SLOTS * 48 + DMA_AHEAD))
                    act.wait_ge(proj_ready, b * NU + (n + 1))
                    nc.scalar.activation(parts[:, n % SLOTS, 0, :], ps_p[:, n % 2, :], ACT.Identity,
                                         bias=bias[:, w, c:c + 1]).then_inc(high_ready, 1)

                def middle(n):
                    act.wait_ge(resid_ready, b * NU + (n + 1))
                    nc.scalar.copy(parts[:, n % SLOTS, 1, :], resid[:, n % SLOTS, :]).then_inc(mid_ready, 1)

                high(0)
                for n in range(1, NU + 1):
                    if n < NU:
                        high(n)
                    middle(n - 1)
                    if n == 3:
                        act.wait_ge(v_out, b * 16 + DMA_AHEAD)
                        act.wait_ge(v_ready, b * NT + NT)
                        nc.scalar.copy(v_part(0), v_rows).then_inc(v_high, 1)
                    if n == 8:
                        act.wait_ge(v_resid, b + 1)
                        nc.scalar.copy(v_part(1), v_rows).then_inc(v_mid, 1)
                    if not last and n in NORM_AT[0::2]:
                        deviation(b + 1, NORM_AT.index(n) // 2)

            for rnd in range(2):
                deviation(0, rnd)
            with act.Fori(0, B - 1) as b:
                round(b)
            round(B - 1, last=True)

        @block.gpsimd
        def _(pool):
            pool.sem_inc(v_low, AHEAD)
            with pool.Fori(0, B) as b:
                pool.wait_ge(v_high, b + 1)
                nc.gpsimd.tensor_tensor(v_rows, v_rows, v_part(0), ALU.subtract).then_inc(v_resid, 1)
                pool.wait_ge(v_mid, b + 1)
                nc.gpsimd.tensor_tensor(v_part(2), v_rows, v_part(1), ALU.subtract).then_inc(v_low, 1)

        @block.tensor
        def _(pe):
            pe.wait_ge(consts, NCONST)
            pe.sem_inc(tr_ready, AHEAD)
            with pe.Fori(0, B) as b:
                for g in range(2 * NT // 4):
                    c, i0 = g // 2, 4 * (g % 2)
                    if g == 0:
                        pe.wait_ge(z_ready, b + 1)
                    if g >= 2:
                        pe.wait_ge(tr_used, b * 4 + (g - 1))
                    for i in range(4):
                        nc.tensor.transpose(ps_t[:, g % 2, i * P:(i + 1) * P], xt[:, i0 + i, c * P:(c + 1) * P],
                                            ident[:, :]).then_inc(tr_ready, 1)
                pe.wait_ge(tr_used, b * 4 + 4)
                for i in range(NT):
                    if i >= 2:
                        pe.wait_ge(v_ready, b * NT + (i - 1))
                    for k in range(KC):
                        mm = nc.tensor.matmul(ps_v[:, i % 2, 0:D], xnT[:, k, i * P:(i + 1) * P], w_sb[:, 2, k, :],
                                              start=(k == 0), stop=(k == KC - 1))
                    mm.then_inc(vproj_ready, 1)
                for n, (w, c, hf) in enumerate(UNITS):
                    if n >= 2:
                        pe.wait_ge(resid_ready, b * NU + (n - 1))
                    for k in range(KC):
                        mm = nc.tensor.matmul(ps_p[:, n % 2, :], w_sb[:, W_OF[w], k, c * P:(c + 1) * P],
                                              xnT[:, k, hf * HALF:(hf + 1) * HALF], start=(k == 0), stop=(k == KC - 1))
                    mm.then_inc(proj_ready, 1)


def self_attention(nc, trig_in, ident_in, qu_s, qv_s, k_s, v_s, wp_s, ctx_s):
    with ExitStack() as ctx:
        def sb(name, shape, dt=F32):
            return ctx.enter_context(nc.sbuf_tensor(name, shape, dt))

        def pb(name, shape):
            return ctx.enter_context(nc.psum_tensor(name, shape, F32))

        def sem(name):
            return ctx.enter_context(nc.semaphore(name))

        ident = sb("b_ident", [P, P])
        trig = sb("b_trig", [P, 3, T])
        qu = sb("b_qu", [P, 2, T], BF16)
        ks = sb("b_ks", [P, 2, T], BF16)
        qv = sb("b_qv", [P, 2, T], BF16)
        wp = sb("b_wp", [P, 2, D], BF16)
        vh = sb("b_vh", [P, 2, NT, 3 * DH], BF16)
        r1 = sb("b_r1", [P, 2, QT])
        r2 = sb("b_r2", [P, 2, QT])
        uvf = sb("b_uvf", [P, 4, 2, QT])
        uv = sb("b_uv", [P, 2, 2, 2, T], F32R)
        trig_r = sb("b_trig_r", [P, 2, 2, T], F32R)
        nmax = sb("b_nmax", [P, 2])
        rmax = sb("b_rmax", [P, 2])
        probs = sb("b_probs", [P, 2, T])
        rsum = sb("b_rsum", [P, 2, NT])
        rinv = sb("b_rinv", [P, NT])
        pT = sb("b_pT", [P, 2, 3, NT, P], BF16)
        pr = sb("b_pr", [P, 2, HALF])
        ctx_sum = sb("b_ctx_sum", [P, NT, DH])
        ctx_sb = sb("b_ctx", [P, 2, NT, DH])
        zero = sb("b_zero", [P, 2])
        ps_a = pb("b_ps_a", [P, 2, QT])
        ps_s = pb("b_ps_s", [P, 2, 2, HALF])
        ps_t = pb("b_ps_t", [P, 2, HALF])
        ps_o = pb("b_ps_o", [P, HALF])

        consts = sem("b_consts")
        qv_in = [sem(f"b_qv_in{u}") for u in range(2)]
        qk_in = [sem(f"b_qk_in{u}") for u in range(2)]
        ctx_out = [sem(f"b_ctx_out{u}") for u in range(2)]
        sc_ready = sem("b_sc_ready")
        max_ready = sem("b_max_ready")
        nmax_ready = sem("b_nmax_ready")
        exp_done = sem("b_exp_done")
        tr_ready = sem("b_tr_ready")
        hi_done = sem("b_hi_done")
        rest_done = sem("b_rest_done")
        mid_done = sem("b_mid_done")
        lo_done = sem("b_lo_done")
        sum_ready = sem("b_sum_ready")
        av_done = sem("b_av_done")
        a_ready = sem("b_a_ready")
        rot_done = sem("b_rot_done")
        uv_ready = sem("b_uv_ready")
        uv_high = sem("b_uv_high")
        uv_low = sem("b_uv_low")
        trig_parts = sem("b_trig_parts")
        inv_ready = sem("b_inv_ready")
        ctx_ready = sem("b_ctx_ready")
        block = ctx.enter_context(nc.Block())

        TPH = B * NT
        NCONST = 2 * 16
        QV_DMAS, QK_DMAS = 16, 17


        @block.sync
        def _(sp):
            sp.dma_start(ident[:, :], ident_in).then_inc(consts, 16)
            sp.dma_start(trig[:, :, :], trig_in).then_inc(consts, 16)

            def load_qv(h, b, first):
                if not first:
                    sp.wait_ge(a_ready, (h * B + b) * 4 - 4)
                for n in range(8):
                    sp.dma_start(qv[n * DH:(n + 1) * DH, b % 2, :],
                                 qv_s[PARTS_K[n], bass.ds(h * DH, DH), b * T:(b + 1) * T]).then_inc(qv_in[b % 2], 16)
                    sp.dma_start(wp[n * DH:(n + 1) * DH, b % 2, :],
                                 wp_s[PARTS_Q[n], bass.ds(h * DH, DH), :]).then_inc(qv_in[b % 2], 16)

            def load_qk(h, b, first):
                if not first:
                    sp.wait_ge(av_done, (h * B + b) * NT - (NT - AHEAD))
                for n in range(8):
                    sp.dma_start(qu[n * DH:(n + 1) * DH, b % 2, :],
                                 qu_s[PARTS_Q[n], bass.ds(h * DH, DH), b * T:(b + 1) * T]).then_inc(qk_in[b % 2], 16)
                    sp.dma_start(ks[n * DH:(n + 1) * DH, b % 2, :],
                                 k_s[PARTS_K[n], bass.ds(h * DH, DH), b * T:(b + 1) * T]).then_inc(qk_in[b % 2], 16)
                sp.dma_start(vh[:, b % 2, :, :],
                             v_s[b * T:(b + 1) * T, bass.ds(h * (3 * DH), 3 * DH)].rearrange("(i p) d -> p i d", p=P)).then_inc(qk_in[b % 2], 16)

            for s in ctx_out:
                sp.sem_inc(s, DMA_AHEAD)
            load_qv(0, 0, True)
            load_qk(0, 0, True)
            load_qv(0, 1, True)
            load_qk(0, 1, True)

            def job(h, b, ahead):
                if ahead:
                    load_qv(h + (b + 2) // B, (b + 2) % B, False)
                    load_qk(h + (b + 2) // B, (b + 2) % B, False)

            with sp.Fori(0, H - 1) as h:
                for b in range(B):
                    job(h, b, True)
            for b in range(2):
                job(H - 1, b, True)
            for u in range(2):
                sp.wait_ge(ctx_out[u], H * (B // 2) * 16 + DMA_AHEAD)

        @block.tensor
        def _(pe):
            def sc_chunk(h, job_off, n):
                b = job_off % 2
                if n == 0:
                    pe.wait_ge(qv_in[b], h * (B // 2 * QV_DMAS * 16) + (job_off // 2 + 1) * (QV_DMAS * 16))
                pe.wait_ge(rot_done, (h * B + job_off) * 8 + 2 * n)
                for c in range(2):
                    mm = nc.tensor.matmul(ps_a[:, c, :], wp[:, b, c * P:(c + 1) * P], qv[:, b, n * QT:(n + 1) * QT],
                                          start=True, stop=True)
                mm.then_inc(a_ready, 1)

            def scores(h, s, hf):
                b, i = s // NT, s % NT
                slot = b % 2
                if hf == 0:
                    pe.wait_ge(exp_done, h * TPH + (s + 1))
                    if i == 0:
                        pe.wait_ge(qk_in[slot], h * (B // 2 * QK_DMAS * 16) + (b // 2 + 1) * (QK_DMAS * 16))
                    if i * P % QT == 0:
                        pe.wait_ge(uv_low, h * (B * 4) + (4 * b + i * P // QT + 1))
                q = slice(i * P, (i + 1) * P)
                k = slice(hf * HALF, (hf + 1) * HALF)
                for n, (w, pu, pt) in enumerate(((0, 0, 0), (0, 0, 1), (0, 1, 0), (1, 0, 0), (1, 0, 1), (1, 1, 0))):
                    nc.tensor.matmul(ps_s[:, s % 2, hf, :], uv[:, slot, pu, w, q], trig_r[:, pt, 1 - w, k],
                                     start=(n == 0), stop=False)
                mm = nc.tensor.matmul(ps_s[:, s % 2, hf, :], qu[:, slot, q], ks[:, slot, k], start=False, stop=True)
                if hf == 1:
                    mm.then_inc(sc_ready, 1)

            def transposes(h, s, g):
                if g == 0:
                    pe.wait_ge(exp_done, h * TPH + (s + 3))
                if s >= 1:
                    pe.wait_ge(rest_done, h * (2 * TPH) + (2 * s + g - 1))
                for j in range(4):
                    mm = nc.tensor.transpose(ps_t[:, g, j * P:(j + 1) * P], probs[:, s % 2, (4 * g + j) * P:(4 * g + j + 1) * P],
                                             ident[:, :])
                mm.then_inc(tr_ready, 1)

            def context(h, s):
                b, i = (s // NT) % B, s % NT
                pe.wait_ge(lo_done, h * (2 * TPH) + (2 * s + 2))
                if i == 0:
                    pe.wait_ge(ctx_ready, h * B + (s // NT + AHEAD))
                for j in range(NT):
                    for part in range(3):
                        w = (3 - part) * DH
                        mm = nc.tensor.matmul(ps_o[:, i * 3 * DH:i * 3 * DH + w], pT[:, s % 2, part, j, :], vh[:, b % 2, j, 0:w],
                                              start=(j == 0 and part == 0), stop=(j == NT - 1 and part == 2), skip_group_check=True)
                mm.then_inc(av_done, 1)

            def step(h, s, behind=3, ahead=True):
                hh, ss = (h + 1, s - TPH) if s >= TPH else (h, s)
                scores(hh, ss, 0)
                if behind >= 2:
                    transposes(h, s - 2, 1)
                scores(hh, ss, 1)
                if behind >= 3:
                    context(h, s - 3)
                if behind >= 1:
                    transposes(h, s - 1, 0)
                if ahead and 3 <= s % NT <= 6:
                    sc_chunk(h, s // NT + 1, s % NT - 3)

            pe.wait_ge(consts, NCONST)
            pe.wait_ge(trig_parts, 2)
            pe.sem_inc(av_done, AHEAD)
            for n in range(4):
                sc_chunk(0, 0, n)
            for s in range(3):
                step(0, s, behind=s)
            with pe.Fori(0, H - 1) as h:
                for s in range(3, TPH + 3):
                    step(h, s)
            for s in range(3, TPH):
                step(H - 1, s, ahead=(s < TPH - NT))
            transposes(H - 1, TPH - 2, 1)
            context(H - 1, TPH - 3)
            transposes(H - 1, TPH - 1, 0)
            transposes(H - 1, TPH - 1, 1)
            context(H - 1, TPH - 2)
            context(H - 1, TPH - 1)

        @block.scalar
        def _(act):
            act.wait_ge(consts, NCONST)
            nc.scalar.copy(zero[:, 0:1], ident[:, 0:1]).then_inc(exp_done, 1)
            nc.scalar.copy(zero[:, 1:2], ident[:, 1:2]).then_inc(exp_done, 1)

            def exp(h, s, first=False):
                b = s // NT
                act.wait_ge(nmax_ready, h * TPH + (s + 1))
                if s % NT == 0 and not first:
                    act.wait_ge(ctx_ready, h * B + (b - 1 + AHEAD))
                nc.scalar.activation(probs[:, s % 2, :], ps_s[:, s % 2, :, :].rearrange("p a n -> p (a n)"), ACT.Exp,
                                     bias=nmax[:, s % 2:s % 2 + 1], scale=SCALE,
                                     accum_out=rsum[:, b % 2, s % NT:s % NT + 1]).then_inc(exp_done, 1)

            def high(h, s, g):
                if g == 0 and s >= 2:
                    act.wait_ge(av_done, h * TPH + (s - 1 + AHEAD))
                act.wait_ge(tr_ready, h * (2 * TPH) + (2 * s + g + 1))
                nc.scalar.copy(pT[:, s % 2, 0, 4 * g:4 * g + 4, :].rearrange("p a n -> p (a n)"), ps_t[:, g, :]).then_inc(hi_done, 1)

            def middle(h, s, g):
                act.wait_ge(rest_done, h * (2 * TPH) + (2 * s + g + 1))
                nc.scalar.copy(pT[:, s % 2, 1, 4 * g:4 * g + 4, :].rearrange("p a n -> p (a n)"), pr[:, g, :]).then_inc(mid_done, 1)

            def store_ctx(h, b):
                act.wait_ge(ctx_ready, h * B + (b + 1 + AHEAD))
                act.dma_start(ctx_s[b * T:(b + 1) * T, bass.ds(h * DH, DH)].rearrange("(i p) d -> p i d", p=P),
                              ctx_sb[:, b % 2, :, :]).then_inc(ctx_out[b % 2], 16)

            def uv_highs(h, job_off, n):
                act.wait_ge(uv_ready, (h * B + job_off) * 8 + (2 * n + 2))
                nc.scalar.copy(uv[:, job_off % 2, 0, :, n * QT:(n + 1) * QT], uvf[:, n, :, :]).then_inc(uv_high, 1)

            def step(h, s, behind=2, ahead=True):
                hh, ss = (h + 1, s - TPH) if s >= TPH else (h, s)
                if behind >= 2:
                    high(h, s - 2, 1)
                    middle(h, s - 2, 1)
                if behind >= 1:
                    high(h, s - 1, 0)
                exp(hh, ss, first=(behind == 0))
                if behind >= 1:
                    middle(h, s - 1, 0)
                if ahead and s % NT >= 4:
                    uv_highs(h, s // NT + 1, s % NT - 4)

            for n in range(4):
                uv_highs(0, 0, n)
            for s in range(3):
                step(0, s, behind=s)
            with act.Fori(0, H - 1) as h:
                for s in range(3, TPH + 3):
                    step(h, s)
                    if s % NT == 4 and s > NT:
                        store_ctx(h, s // NT - 1)
                store_ctx(h, B - 1)
            for s in range(3, TPH):
                step(H - 1, s, ahead=(s < TPH - NT))
                if s % NT == 4 and s > NT:
                    store_ctx(H - 1, s // NT - 1)
            high(H - 1, TPH - 2, 1)
            middle(H - 1, TPH - 2, 1)
            for g in range(2):
                high(H - 1, TPH - 1, g)
                middle(H - 1, TPH - 1, g)
            store_ctx(H - 1, B - 1)

        @block.vector
        def _(dve):
            def row_max(h, s):
                dve.wait_ge(sc_ready, h * TPH + (s + 1))
                nc.vector.tensor_reduce(rmax[:, s % 2:s % 2 + 1], ps_s[:, s % 2, :, :].rearrange("p a n -> p (a n)"),
                                        AX_X, ALU.max).then_inc(max_ready, 1)
                dve.wait_ge(max_ready, h * TPH + (s + 1))
                nc.vector.tensor_scalar(nmax[:, s % 2:s % 2 + 1], rmax[:, s % 2:s % 2 + 1], -SCALE, None,
                                        ALU.mult).then_inc(nmax_ready, 1)

            def products(h, job_off, n):
                cols = slice(n * QT, (n + 1) * QT)
                dve.wait_ge(a_ready, (h * B + job_off) * 4 + (n + 1))
                dve.wait_ge(uv_ready, (h * B + job_off) * 8 + 2 * n)
                nc.vector.tensor_tensor(r1[:, :, :], ps_a[:, :, :], trig[:, 0:2, cols], ALU.mult).then_inc(rot_done, 1)
                nc.vector.tensor_tensor(r2[:, :, :], ps_a[:, :, :], trig[:, 1:3, cols], ALU.mult).then_inc(rot_done, 1)

            def normalise(h, b):
                dve.wait_ge(av_done, h * TPH + ((b + 1) * NT + AHEAD))
                nc.vector.reciprocal(rinv[:, :], rsum[:, b % 2, :]).then_inc(inv_ready, 1)
                dve.wait_ge(ctx_out[b % 2], h * (B // 2 * 16) + (b // 2 * 16 + DMA_AHEAD))
                nc.vector.tensor_reduce(ctx_sum[:, :, :], ps_o[:, 0:NT * 3 * DH].rearrange("p (i n d) -> p i d n", n=3, d=DH),
                                        AX_X, ALU.add).then_inc(sum_ready, 1)
                dve.wait_ge(inv_ready, h * B + (b + 1))
                dve.wait_ge(sum_ready, h * B + (b + 1))
                nc.vector.tensor_tensor(ctx_sb[:, b % 2, :, :], ctx_sum[:, :, :],
                                        rinv[:, :].unsqueeze(2).to_broadcast([P, NT, DH]), ALU.mult).then_inc(ctx_ready, 1)

            def rest(h, s, g):
                if s >= 1:
                    dve.wait_ge(lo_done, h * (2 * TPH) + (2 * s + g - 1))
                dve.wait_ge(hi_done, h * (2 * TPH) + (2 * s + g + 1))
                nc.vector.tensor_tensor(pr[:, g, :], ps_t[:, g, :], pT[:, s % 2, 0, 4 * g:4 * g + 4, :].rearrange("p a n -> p (a n)"),
                                        ALU.subtract).then_inc(rest_done, 1)

            def step(h, s, behind=2, ahead=True):
                hh, ss = (h + 1, s - TPH) if s >= TPH else (h, s)
                if behind >= 2:
                    rest(h, s - 2, 1)
                row_max(hh, ss)
                if behind >= 1:
                    rest(h, s - 1, 0)
                if s > NT and s % NT == 2:
                    normalise(h, s // NT - 1)
                if ahead and 3 <= s % NT <= 6:
                    products(h, s // NT + 1, s % NT - 3)
                if ahead and s % NT >= 5:
                    uv_lows(h, s // NT + 1, s % NT - 5)
                if s >= NT and s % NT == 0:
                    uv_lows(h, s // NT, 3)

            def uv_lows(h, job_off, n):
                dve.wait_ge(uv_high, (h * B + job_off) * 4 + (n + 1))
                cols = slice(n * QT, (n + 1) * QT)
                nc.vector.tensor_tensor(uv[:, job_off % 2, 1, :, cols], uvf[:, n, :, :], uv[:, job_off % 2, 0, :, cols].bitcast(F32),
                                        ALU.subtract).then_inc(uv_low, 1)

            dve.wait_ge(consts, NCONST)
            dve.sem_inc(ctx_ready, AHEAD)
            nc.vector.tensor_copy(trig_r[:, 0, :, :], trig[:, 0:2, :]).then_inc(trig_parts, 1)
            dve.wait_ge(trig_parts, 1)
            nc.vector.tensor_tensor(trig_r[:, 1, :, :], trig[:, 0:2, :], trig_r[:, 0, :, :].bitcast(F32), ALU.subtract).then_inc(trig_parts, 1)
            for n in range(4):
                products(0, 0, n)
            for n in range(4):
                uv_lows(0, 0, n)
            for s in range(3):
                step(0, s, behind=s)
            with dve.Fori(0, H - 1) as h:
                for s in range(3, TPH + 3):
                    step(h, s)
            for s in range(3, TPH):
                step(H - 1, s, ahead=(s < TPH - NT))
            rest(H - 1, TPH - 2, 1)
            rest(H - 1, TPH - 1, 0)
            rest(H - 1, TPH - 1, 1)
            normalise(H - 1, B - 1)

        @block.gpsimd
        def _(pool):
            def combine(h, job_off, n):
                if not (isinstance(h, int) and h == 0 and job_off == 0):
                    pool.wait_ge(uv_low, (h * B + job_off) * 4 + (n - 3))
                pool.wait_ge(rot_done, (h * B + job_off) * 8 + (2 * n + 1))
                nc.gpsimd.tensor_tensor(uvf[:, n, 0, :], r1[:, 0, :], r1[:, 1, :], ALU.add).then_inc(uv_ready, 1)
                pool.wait_ge(rot_done, (h * B + job_off) * 8 + (2 * n + 2))
                nc.gpsimd.tensor_tensor(uvf[:, n, 1, :], r2[:, 1, :], r2[:, 0, :], ALU.subtract).then_inc(uv_ready, 1)

            def low(h, s, g):
                pool.wait_ge(mid_done, h * (2 * TPH) + (2 * s + g + 1))
                cols = slice(4 * g, 4 * g + 4)
                nc.gpsimd.tensor_tensor(pT[:, s % 2, 2, cols, :].rearrange("p a n -> p (a n)"), pr[:, g, :],
                                        pT[:, s % 2, 1, cols, :].rearrange("p a n -> p (a n)"), ALU.subtract).then_inc(lo_done, 1)

            def step(h, s, behind=2, ahead=True):
                if behind >= 2:
                    low(h, s - 2, 1)
                if behind >= 1:
                    low(h, s - 1, 0)
                if ahead and 3 <= s % NT <= 6:
                    combine(h, s // NT + 1, s % NT - 3)

            for n in range(4):
                combine(0, 0, n)
            for s in range(3):
                step(0, s, behind=s)
            with pool.Fori(0, H - 1) as h:
                for s in range(3, TPH + 3):
                    step(h, s)
            for s in range(3, TPH):
                step(H - 1, s, ahead=(s < TPH - NT))
            low(H - 1, TPH - 2, 1)
            low(H - 1, TPH - 1, 0)
            low(H - 1, TPH - 1, 1)


def project_out(nc, x, ident_in, woT, bo_rows, ctx_s, x1):
    xf = x.rearrange("b t d -> (b t) d")
    with ExitStack() as ctx:
        def sb(name, shape, dt=F32):
            return ctx.enter_context(nc.sbuf_tensor(name, shape, dt))

        def sem(name):
            return ctx.enter_context(nc.semaphore(name))

        ident = sb("c_ident", [P, P])
        wo = sb("c_wo", [P, KC, D])
        bo = sb("c_bo", [P, D])
        NS = 4
        ct = sb("c_ct", [P, NS, D])
        xt = sb("c_xt", [P, NS, D])
        cT = sb("c_cT", [P, NS, KC, P])
        y = sb("c_y", [P, NS, D])
        ps_t = ctx.enter_context(nc.psum_tensor("c_ps_t", [P, NS, HALF], F32))
        ps_y = ctx.enter_context(nc.psum_tensor("c_ps_y", [P, NS, HALF], F32))
        consts = sem("c_consts")
        ctx_in = [sem(f"c_ctx_in{u}") for u in range(NS)]
        y_out = [sem(f"c_y_out{u}") for u in range(NS)]
        tr_ready = sem("c_tr_ready")
        tr_copied = sem("c_tr_copied")
        y_ready = sem("c_y_ready")
        xb_ready = sem("c_xb_ready")
        y_done = sem("c_y_done")
        block = ctx.enter_context(nc.Block())

        @block.sync
        def _(sp):
            sp.dma_start(ident[:, :], ident_in).then_inc(consts, 16)
            sp.dma_start(wo[:, :, :], woT.rearrange("(c p) n -> p c n", p=P)).then_inc(consts, 16)
            sp.dma_start(bo[:, :], bo_rows).then_inc(consts, 16)
            for u in range(NS):
                sp.sem_inc(y_out[u], DMA_AHEAD)

            def rows(r, u):
                return bass.ds(r * (NS * P) + u * P, P)

            def load(r, u):
                sp.dma_start(ct[:, u, :], ctx_s[rows(r, u), :]).then_inc(ctx_in[u], 16)
                sp.dma_start(xt[:, u, :], xf[rows(r, u), :]).then_inc(ctx_in[u], 16)

            def store(r, u):
                sp.wait_ge(y_done, r * NS + (u + 1))
                sp.dma_start(x1[rows(r, u), :], y[:, u, :]).then_inc(y_out[u], 16)

            for u in range(NS):
                load(0, u)
            with sp.Fori(1, TILES // NS) as r:
                for u in range(NS):
                    store(r - 1, u)
                    load(r, u)
            for u in range(NS):
                store(TILES // NS - 1, u)
            for u in range(NS):
                sp.wait_ge(y_out[u], TILES // NS * 16 + DMA_AHEAD)

        @block.tensor
        def _(pe):
            pe.wait_ge(consts, 48)
            with pe.Fori(0, TILES // NS) as r:
                for u in range(NS):
                    pe.wait_ge(ctx_in[u], r * 32 + 32)
                    for k in range(KC):
                        mm = nc.tensor.transpose(ps_t[:, u, k * P:(k + 1) * P], ct[:, u, k * P:(k + 1) * P], ident[:, :])
                    mm.then_inc(tr_ready, 1)
                for u in range(NS):
                    pe.wait_ge(tr_copied, r * NS + (u + 1))
                    for k in range(KC):
                        mm = nc.tensor.matmul(ps_y[:, u, 0:D], cT[:, u, k, :], wo[:, k, :], start=(k == 0), stop=(k == KC - 1))
                    mm.then_inc(y_ready, 1)

        @block.scalar
        def _(act):
            with act.Fori(0, TILES // NS) as r:
                for u in range(NS):
                    act.wait_ge(tr_ready, r * NS + (u + 1))
                    nc.scalar.copy(cT[:, u, :, :].rearrange("p k n -> p (k n)"), ps_t[:, u, 0:D]).then_inc(tr_copied, 1)

        @block.vector
        def _(dve):
            dve.wait_ge(consts, 48)
            with dve.Fori(0, TILES // NS) as r:
                for u in range(NS):
                    dve.wait_ge(ctx_in[u], r * 32 + 32)
                    nc.vector.tensor_tensor(xt[:, u, :], xt[:, u, :], bo[:, :], ALU.add).then_inc(xb_ready, 1)
                for u in range(NS):
                    dve.wait_ge(y_out[u], r * 16 + DMA_AHEAD)
                    dve.wait_ge(xb_ready, r * NS + (u + 1))
                    dve.wait_ge(y_ready, r * NS + (u + 1))
                    nc.vector.tensor_tensor(y[:, u, :], ps_y[:, u, 0:D], xt[:, u, :], ALU.add).then_inc(y_done, 1)


def cross_attention(nc, a, x1, x2, prefetch):
    x1f = x1.rearrange("(b i p) d -> b p i d", p=P, b=B)
    x2f = x2.rearrange("(b i p) d -> b i p d", p=P, b=B)
    with ExitStack() as ctx:
        def sb(name, shape, dt=F32):
            return ctx.enter_context(nc.sbuf_tensor(name, shape, dt))

        def sem(name):
            return ctx.enter_context(nc.semaphore(name))

        G = 4
        NG = H // G
        HC = H // KC
        ident = sb("d_ident", [P, P])
        wq = sb("d_wq", [P, KC, D])
        wkv = sb("d_wkv", [P, KC, 2 * D])
        wo = sb("d_wo", [P, KC, D])
        rows = sb("d_rows", [P, 4, D])
        lnw = sb("d_lnw", [P, 4])
        eps = sb("d_eps", [P, 2])
        yT = sb("d_yT", [P, 2, KC, S2])
        diag = sb("d_diag", [P, HC])
        mask8 = sb("d_mask8", [P, B, S2], mybir.dt.uint8)
        bias = sb("d_bias", [P, B, S2])
        kx = sb("d_kx", [P, D])
        k_sq = sb("d_k_sq", [P, D])
        k_st = sb("d_k_st", [P, 3, H])
        kbd = sb("d_kbd", [P, 2, KC, HC, S2], F32R)
        kT_r = sb("d_kT_r", [P, 2, KC, S2], F32R)
        qT_r = sb("d_qT_r", [P, 2, KC, T], F32R)
        kT = sb("d_kT", [P, KC, S2])
        v_sb = sb("d_v", [P, D])
        xt = sb("d_x", [P, 2, NT, D])
        z = sb("d_z", [P, NT, D])
        st = sb("d_st", [P, NT, 6])
        mv = sb("d_mv", [P, NT, 2])
        sd = sb("d_sd", [P, NT])
        xnT = sb("d_xnT", [P, KC, T])
        q = z
        q_st = sb("d_q_st", [P, 3, NT * H])
        qT = xnT
        sc = sb("d_sc", [P, 2, H, S2])
        pm = sb("d_pm", [P, 2, H])
        rs = sb("d_rs", [P, 2, H])
        ri = sb("d_ri", [P, 2, H])
        pT = sb("d_pT", [P, 2, H, P])
        q_sq = pT[:, 0, :, :].rearrange("p h n -> p (h n)")
        cx = sb("d_cx", [P, 2, D])
        cT = sb("d_cT", [P, 2, KC, P])
        xb = sb("d_xb", [P, 2, D])
        y = sb("d_y", [P, 2, D])
        spare = sb("d_spare", [P, 1])
        ps_s = ctx.enter_context(nc.psum_tensor("d_ps_s", [P, NG, HALF], F32))
        ps_t = ctx.enter_context(nc.psum_tensor("d_ps_t", [P, 2, HALF], F32))
        ps_o = ctx.enter_context(nc.psum_tensor("d_ps_o", [P, HALF], F32))
        ps_y = ctx.enter_context(nc.psum_tensor("d_ps_y", [P, HALF], F32))

        consts = sem("d_consts")
        x_in = [sem(f"d_x_in{u}") for u in range(2)]
        yT_in = [sem(f"d_yT_in{u}") for u in range(2)]
        y_out = [sem(f"d_y_out{u}") for u in range(2)]
        setup = sem("d_setup")
        chain = sem("d_chain")
        sd_ready = sem("d_sd_ready")
        dev_in = sem("d_dev_in")
        z_ready = sem("d_z_ready")
        tr_ready = sem("d_tr_ready")
        tr_copied = sem("d_tr_copied")
        mm_ready = sem("d_mm_ready")
        mm_used = sem("d_mm_used")
        kbd_ready = sem("d_kbd_ready")
        kT_ready = sem("d_kT_ready")
        kT_parts = sem("d_kT_parts")
        qT_high = sem("d_qT_high")
        qT_low = sem("d_qT_low")
        sc_ready = sem("d_sc_ready")
        sc_used = sem("d_sc_used")
        sm_max = sem("d_sm_max")
        sm_sum = sem("d_sm_sum")
        sm_inv = sem("d_sm_inv")
        xb_ready = sem("d_xb_ready")
        sub_ready = sem("d_sub_ready")
        exp_done = sem("d_exp_done")
        pT_copied = sem("d_pT_copied")
        pT_ready = sem("d_pT_ready")
        av_ready = sem("d_av_ready")
        cx_ready = sem("d_cx_ready")
        cT_ready = sem("d_cT_ready")
        cT_copied = sem("d_cT_copied")
        y_ready = sem("d_y_ready")
        y_done = sem("d_y_done")
        block = ctx.enter_context(nc.Block())

        NCONST = 9 * 16
        CH = 12
        TRB = 2 * NT // 4 * 2 + 1
        MMB = NT + 2
        HB = HC * DH

        @block.sync
        def _(sp):
            for dst, src in ((ident[:, :], a["ident"]), (wq[:, :, :], a["x_wqT"].rearrange("(c p) n -> p c n", p=P)),
                             (wkv[:, :, :], a["x_wkvT"].rearrange("(c p) n -> p c n", p=P)),
                             (wo[:, :, :], a["x_woT"].rearrange("(c p) n -> p c n", p=P)),
                             (rows[:, :, :], a["x_rows"]), (lnw[:, :], a["x_lnw"]), (eps[:, :], a["eps2"]),
                             (diag[:, :], a["x_diag"]),
                             (mask8[:, :, :], a["mask"])):
                sp.dma_start(dst, src).then_inc(consts, 16)
            for s in y_out:
                sp.sem_inc(s, DMA_AHEAD)

            def load(b, slot):
                sp.dma_start(yT[:, slot, :, :], a["ctxT"].rearrange("b (c p) s -> b p c s", p=P)[b, :, :, :]).then_inc(yT_in[slot], 16)
                sp.dma_start(xt[:, slot, :, :], x1f[b, :, :, :]).then_inc(x_in[slot], 16)

            def stores(b):
                for i in range(NT):
                    sp.wait_ge(y_done, b * NT + (i + 1 + AHEAD))
                    sp.dma_start(x2f[b, i, :, :], y[:, i % 2, :]).then_inc(y_out[i % 2], 16)

            for slot in range(2):
                load(slot, slot)
            prefetch(sp)
            with sp.Fori(0, B // 2 - 1) as r:
                for slot in range(2):
                    stores(r * 2 + slot)
                    load(r * 2 + (slot + 2), slot)
            for slot in range(2):
                stores(B - 2 + slot)
            for s in y_out:
                sp.wait_ge(s, TILES // 2 * 16 + DMA_AHEAD)

        @block.vector
        def _(dve):
            def bc(v, n, w):
                return v.unsqueeze(2).to_broadcast([P, n, w])

            dve.wait_ge(consts, NCONST)
            nc.vector.tensor_scalar(bias[:, :, :], mask8[:, :, :], 1.0, 1e30, ALU.subtract, ALU.mult).then_inc(setup, 1)
            dve.wait_ge(setup, 1)
            dve.sem_inc(y_done, AHEAD)
            dve.sem_inc(sc_used, AHEAD)
            def round(r, slot):
                b = r * 2 + slot
                steps = [0]

                def then(ins):
                    steps[0] += 1
                    ins.then_inc(chain, 1)
                    dve.wait_ge(chain, b * CH + steps[0])

                dve.wait_ge(x_in[slot], r * 16 + 16)
                for i in range(NT):
                    last = nc.vector.bn_stats(st[:, i, :], xt[:, slot, i, :])
                then(last)
                nc.vector.memset(spare[:, :], 0.0)
                for i in range(NT):
                    last = nc.vector.bn_aggr(mv[:, i, :], st[:, i, :])
                last.then_inc(dev_in, 1)
                dve.wait_ge(sd_ready, b * 3 + 1)
                then(nc.vector.reciprocal(sd[:, :], sd[:, :]))
                for i in range(NT):
                    last = nc.vector.tensor_scalar(z[:, i, :], xt[:, slot, i, :], mv[:, i, 0:1], sd[:, i:i + 1],
                                                   ALU.subtract, ALU.mult)
                last.then_inc(z_ready, 1)

                def head_norm(v, sq, stat, n, p, dev):
                    v3 = v[0:p].rearrange("p (h d) -> p h d", d=DH)
                    q3 = sq[0:p].rearrange("p (h d) -> p h d", d=DH)
                    wide = [p, n, DH]
                    then(nc.vector.tensor_reduce(stat[0:p, 0, :], v3, AX_X, ALU.add))
                    then(nc.vector.tensor_scalar(stat[0:p, 0, :], stat[0:p, 0, :], 1.0 / DH, None, ALU.mult))
                    then(nc.vector.tensor_tensor(v3, v3, stat[0:p, 0, :].unsqueeze(2).to_broadcast(wide), ALU.subtract))
                    then(nc.vector.tensor_tensor(q3, v3, v3, ALU.mult))
                    nc.vector.tensor_reduce(stat[0:p, 1, :], q3, AX_X, ALU.add).then_inc(dev_in, 1)
                    dve.wait_ge(sd_ready, b * 3 + dev)
                    then(nc.vector.reciprocal(stat[0:p, 2, :], stat[0:p, 2, :]))
                    return nc.vector.tensor_tensor(v3, v3, stat[0:p, 2, :].unsqueeze(2).to_broadcast(wide), ALU.mult)

                dve.wait_ge(mm_ready, b * MMB + 1)
                nc.vector.tensor_tensor(kx[0:S2, :], ps_y[0:S2, 0:D], rows[0:S2, 1, :], ALU.add).then_inc(mm_used, 1)
                dve.wait_ge(mm_ready, b * MMB + 2)
                nc.vector.tensor_tensor(v_sb[0:S2, :], ps_o[0:S2, 0:D], rows[0:S2, 2, :], ALU.add).then_inc(mm_used, 1)
                dve.wait_ge(mm_used, b * MMB + 2)
                head_norm(kx[:, :], k_sq[:, :], k_st, H, S2, 2).then_inc(z_ready, 1)
                for g in range(2 * NT // 4):
                    dve.wait_ge(tr_ready, b * TRB + (g + 1))
                    nc.vector.tensor_copy(xnT[:, g // 2, (g % 2) * HALF:(g % 2 + 1) * HALF], ps_t[:, g % 2, :]).then_inc(tr_copied, 1)
                dve.wait_ge(tr_ready, b * TRB + 5)
                nc.vector.tensor_scalar(kT[:, :, :], ps_t[:, 0, 0:KC * S2].rearrange("p (c s) -> p c s", c=KC),
                                        lnw[:, 2:3], lnw[:, 3:4], ALU.mult, ALU.add).then_inc(kT_ready, 1)
                dve.wait_ge(kT_ready, b + 1)
                nc.vector.tensor_copy(kT_r[:, 0], kT[:, :, :]).then_inc(kT_parts, 1)
                dve.wait_ge(kT_parts, b * 2 + 1)
                nc.vector.tensor_tensor(kT_r[:, 1], kT[:, :, :], kT_r[:, 0].bitcast(F32), ALU.subtract).then_inc(kT_parts, 1)
                for c in range(KC):
                    last = nc.vector.tensor_tensor(kbd[:, 0, c, :, :], kT_r[:, 0, c:c + 1, :].bitcast(F32).to_broadcast([P, HC, S2]),
                                                   bc(diag[:, :], HC, S2), ALU.mult)
                last.then_inc(kbd_ready, 1)
                for i in range(NT):
                    dve.wait_ge(mm_ready, b * MMB + (i + 3))
                    bank = ps_y if i % 2 == 0 else ps_o
                    nc.vector.tensor_tensor(q[:, i, :], bank[:, 0:D], rows[:, 0, :], ALU.add).then_inc(mm_used, 1)
                dve.wait_ge(mm_used, b * MMB + MMB)
                head_norm(q[:, :, :].rearrange("p i n -> p (i n)"), q_sq,
                          q_st, NT * H, P, 3).then_inc(z_ready, 1)
                for g in range(2 * NT // 4):
                    dve.wait_ge(tr_ready, b * TRB + (g + 6))
                    nc.vector.tensor_scalar(qT[:, g // 2, (g % 2) * HALF:(g % 2 + 1) * HALF], ps_t[:, (g + 1) % 2, :],
                                            lnw[:, 0:1], lnw[:, 1:2], ALU.mult, ALU.add).then_inc(tr_copied, 1)
                assert steps[0] == CH, steps

                def soft_a(i):
                    u = i % 2
                    dve.wait_ge(sc_ready, b * NT + (i + 1))
                    for g in range(NG):
                        last = nc.vector.tensor_tensor(sc[:, u, g * G:(g + 1) * G, :],
                                                       ps_s[:, g, 0:G * S2].rearrange("p (h s) -> p h s", s=S2),
                                                       bias[:, bass.ds(b, 1), :].to_broadcast([P, G, S2]), ALU.add)
                    last.then_inc(sc_used, 1)
                    dve.wait_ge(sc_used, b * NT + (i + 1 + AHEAD))
                    nc.vector.tensor_reduce(pm[:, u, :], sc[:, u, :, :], AX_X, ALU.max).then_inc(sm_max, 1)
                    dve.wait_ge(sm_max, b * NT + (i + 1))
                    nc.vector.tensor_tensor(sc[:, u, :, :], sc[:, u, :, :], bc(pm[:, u, :], H, S2), ALU.subtract).then_inc(sub_ready, 1)

                def soft_b(i):
                    u = i % 2
                    dve.wait_ge(exp_done, b * NT + (i + 1))
                    nc.vector.tensor_reduce(rs[:, u, :], sc[:, u, :, :], AX_X, ALU.add).then_inc(sm_sum, 1)
                    dve.wait_ge(sm_sum, b * NT + (i + 1))
                    nc.vector.reciprocal(ri[:, u, :], rs[:, u, :]).then_inc(sm_inv, 1)

                def context(i):
                    u = i % 2
                    dve.wait_ge(sm_inv, b * NT + (i + 1))
                    dve.wait_ge(av_ready, b * NT + (i + 1))
                    nc.vector.tensor_tensor(cx[:, u, :].rearrange("p (h d) -> p h d", d=DH),
                                            ps_o[:, 0:D].rearrange("p (h d) -> p h d", d=DH), bc(ri[:, u, :], H, DH),
                                            ALU.mult).then_inc(cx_ready, 1)

                def result(i):
                    u = i % 2
                    dve.wait_ge(y_out[u], b * (NT // 2 * 16) + (i // 2 * 16 + DMA_AHEAD))
                    nc.vector.tensor_tensor(xb[:, u, :], xt[:, slot, i, :], rows[:, 3, :], ALU.add).then_inc(xb_ready, 1)
                    dve.wait_ge(xb_ready, b * NT + (i + 1))
                    dve.wait_ge(y_ready, b * NT + (i + 1))
                    nc.vector.tensor_tensor(y[:, u, :], ps_y[:, 0:D], xb[:, u, :], ALU.add).then_inc(y_done, 1)

                for i in range(NT + 2):
                    if i < NT:
                        soft_a(i)
                    if 1 <= i <= NT:
                        soft_b(i - 1)
                        context(i - 1)
                    if i >= 2:
                        result(i - 2)

            with dve.Fori(0, B // 2) as r:
                for slot in range(2):
                    round(r, slot)

        @block.scalar
        def _(act):
            act.wait_ge(consts, NCONST)
            act.sem_inc(pT_copied, AHEAD)
            with act.Fori(0, B) as b:
                act.wait_ge(dev_in, b * 3 + 1)
                nc.scalar.activation(sd[:, :], mv[:, :, 1], ACT.Sqrt, bias=eps[:, 0:1]).then_inc(sd_ready, 1)
                act.wait_ge(dev_in, b * 3 + 2)
                nc.scalar.activation(k_st[0:S2, 2, :], k_st[0:S2, 1, :], ACT.Sqrt, bias=eps[0:S2, 1:2], scale=1.0 / DH).then_inc(sd_ready, 1)
                act.wait_ge(dev_in, b * 3 + 3)
                nc.scalar.activation(q_st[:, 2, :], q_st[:, 1, :], ACT.Sqrt, bias=eps[:, 1:2], scale=1.0 / DH).then_inc(sd_ready, 1)

                for g in range(2 * NT // 4):
                    act.wait_ge(tr_copied, b * 8 + (g + 5))
                    nc.scalar.copy(qT_r[:, 0, g // 2, (g % 2) * HALF:(g % 2 + 1) * HALF],
                                   qT[:, g // 2, (g % 2) * HALF:(g % 2 + 1) * HALF]).then_inc(qT_high, 1)

                def exp(i):
                    u = i % 2
                    act.wait_ge(sub_ready, b * NT + (i + 1))
                    nc.scalar.activation(sc[:, u, :, :], sc[:, u, :, :], ACT.Exp, scale=SCALE).then_inc(exp_done, 1)

                def copy_pT(i, groups):
                    u = i % 2
                    for g in groups:
                        act.wait_ge(pT_ready, b * (NT * NG) + (i * NG + g + 1))
                        nc.scalar.copy(pT[0:S2, u, g * G:(g + 1) * G, :].rearrange("p g n -> p (g n)"),
                                       ps_t[0:S2, g % 2, :]).then_inc(pT_copied, 1)

                def copy_cT(i):
                    u = i % 2
                    act.wait_ge(cT_ready, b * NT + (i + 1))
                    nc.scalar.copy(cT[:, u, :, :].rearrange("p c n -> p (c n)"), ps_y[:, D:2 * D]).then_inc(cT_copied, 1)

                for i in range(NT + 2):
                    if 1 <= i <= NT:
                        copy_pT(i - 1, range(NG // 2))
                    if i >= 2:
                        copy_cT(i - 2)
                    if 1 <= i <= NT:
                        copy_pT(i - 1, range(NG // 2, NG))
                    if i < NT:
                        exp(i)

        @block.gpsimd
        def _(pool):
            pool.wait_ge(consts, NCONST)
            with pool.Fori(0, B) as b:
                pool.wait_ge(kT_parts, b * 2 + 2)
                for c in range(KC):
                    last = nc.gpsimd.tensor_tensor(kbd[:, 1, c, :, :], kT_r[:, 1, c:c + 1, :].bitcast(F32).to_broadcast([P, HC, S2]),
                                                   diag[:, :].unsqueeze(2).to_broadcast([P, HC, S2]), ALU.mult)
                last.then_inc(kbd_ready, 1)
                for g in range(2 * NT // 4):
                    pool.wait_ge(qT_high, b * 4 + (g + 1))
                    cols = slice((g % 2) * HALF, (g % 2 + 1) * HALF)
                    nc.gpsimd.tensor_tensor(qT_r[:, 1, g // 2, cols], qT[:, g // 2, cols], qT_r[:, 0, g // 2, cols].bitcast(F32),
                                            ALU.subtract).then_inc(qT_low, 1)

        @block.tensor
        def _(pe):
            pe.wait_ge(consts, NCONST)
            def round(r, slot):
                b = r * 2 + slot
                pe.wait_ge(y_done, b * NT + AHEAD)
                pe.wait_ge(yT_in[slot], r * 16 + 16)
                for w, bank in ((0, ps_y), (1, ps_o)):
                    for k in range(KC):
                        mm = nc.tensor.matmul(bank[0:S2, 0:D], yT[:, slot, k, :], wkv[:, k, w * D:(w + 1) * D],
                                              start=(k == 0), stop=(k == KC - 1))
                    mm.then_inc(mm_ready, 1)
                pe.wait_ge(z_ready, b * 3 + 1)
                for g in range(2 * NT // 4):
                    c, i0 = g // 2, 4 * (g % 2)
                    if g >= 2:
                        pe.wait_ge(tr_copied, b * 8 + (g - 1))
                    for i in range(4):
                        mm = nc.tensor.transpose(ps_t[:, g % 2, i * P:(i + 1) * P], z[:, i0 + i, c * P:(c + 1) * P], ident[:, :])
                    mm.then_inc(tr_ready, 1)
                pe.wait_ge(z_ready, b * 3 + 2)
                pe.wait_ge(tr_copied, b * 8 + 4)
                for c in range(KC):
                    mm = nc.tensor.transpose(ps_t[:, 0, c * S2:(c + 1) * S2], kx[0:S2, c * P:(c + 1) * P], ident[0:S2, 0:S2])
                mm.then_inc(tr_ready, 1)
                for i in range(NT):
                    pe.wait_ge(mm_used, b * MMB + (i + 1))
                    bank = ps_y if i % 2 == 0 else ps_o
                    for k in range(KC):
                        mm = nc.tensor.matmul(bank[:, 0:D], xnT[:, k, i * P:(i + 1) * P], wq[:, k, :], start=(k == 0), stop=(k == KC - 1))
                    mm.then_inc(mm_ready, 1)
                pe.wait_ge(z_ready, b * 3 + 3)
                pe.wait_ge(kT_ready, b + 1)
                for g in range(2 * NT // 4):
                    c, i0 = g // 2, 4 * (g % 2)
                    if g >= 2:
                        pe.wait_ge(tr_copied, b * 8 + (4 + g - 1))
                    for i in range(4):
                        mm = nc.tensor.transpose(ps_t[:, (g + 1) % 2, i * P:(i + 1) * P], q[:, i0 + i, c * P:(c + 1) * P], ident[:, :])
                    mm.then_inc(tr_ready, 1)
                pe.wait_ge(qT_low, b * 4 + 4)
                pe.wait_ge(kbd_ready, b * 2 + 2)

                def scores(i):
                    pe.wait_ge(sc_used, b * NT + (i + AHEAD))
                    for g in range(NG):
                        c, h0 = g * G // HC, g * G % HC
                        for n, (pq, pk) in enumerate(((0, 0), (0, 1), (1, 0))):
                            mm = nc.tensor.matmul(ps_s[:, g, 0:G * S2], qT_r[:, pq, c, i * P:(i + 1) * P],
                                                  kbd[:, pk, c, h0:h0 + G, :].rearrange("p h s -> p (h s)"),
                                                  start=(n == 0), stop=(n == 2))
                    mm.then_inc(sc_ready, 1)

                def transposes(i, groups):
                    u = i % 2
                    pe.wait_ge(exp_done, b * NT + (i + 1))
                    for g in groups:
                        pe.wait_ge(pT_copied, b * (NT * NG) + max(i * NG + g - 1 + AHEAD, AHEAD))
                        for h in range(G):
                            mm = nc.tensor.transpose(ps_t[0:S2, g % 2, h * P:(h + 1) * P], sc[:, u, g * G + h, :], ident[:, :])
                        mm.then_inc(pT_ready, 1)

                def context(i):
                    u = i % 2
                    pe.wait_ge(pT_copied, b * (NT * NG) + (i * NG + NG + AHEAD))
                    if i:
                        pe.wait_ge(cx_ready, b * NT + i)
                    for h in range(H):
                        mm = nc.tensor.matmul(ps_o[:, h * DH:(h + 1) * DH], pT[0:S2, u, h, :], v_sb[0:S2, h * DH:(h + 1) * DH],
                                              start=True, stop=True)
                    mm.then_inc(av_ready, 1)

                def out_t(i):
                    u = i % 2
                    pe.wait_ge(cx_ready, b * NT + (i + 1))
                    pe.wait_ge(y_done, b * NT + (i + AHEAD))
                    for c in range(KC):
                        mm = nc.tensor.transpose(ps_y[:, D + c * P:D + (c + 1) * P], cx[:, u, c * P:(c + 1) * P], ident[:, :])
                    mm.then_inc(cT_ready, 1)

                def out(i):
                    u = i % 2
                    pe.wait_ge(cT_copied, b * NT + (i + 1))
                    for k in range(KC):
                        mm = nc.tensor.matmul(ps_y[:, 0:D], cT[:, u, k, :], wo[:, k, :], start=(k == 0), stop=(k == KC - 1))
                    mm.then_inc(y_ready, 1)

                for i in range(NT + 2):
                    if i < NT:
                        scores(i)
                    if 1 <= i <= NT:
                        transposes(i - 1, range(NG // 2))
                    if i >= 2:
                        out_t(i - 2)
                    if 1 <= i <= NT:
                        transposes(i - 1, range(NG // 2, NG))
                    if i >= 2:
                        out(i - 2)
                    if 1 <= i <= NT:
                        context(i - 1)

            with pe.Fori(0, B // 2) as r:
                for slot in range(2):
                    round(r, slot)

TABLES = 4


def ffn_norm(nc, a, x2, xr_s, wqk, keysT, km, tables_in):
    GS, NK = keysT.shape[1], keysT.shape[2]
    x2f = x2.rearrange("(b i p) d -> b p i d", p=P, b=B)
    with ExitStack() as ctx:
        def sb(name, shape, dt=F32):
            return ctx.enter_context(nc.sbuf_tensor(name, shape, dt))

        def sem(name):
            return ctx.enter_context(nc.semaphore(name))

        ident = sb("e_ident", [P, P])
        nw = sb("e_nw", [P, KC])
        eps = sb("e_eps", [P, 1])
        xt = sb("e_x", [P, 2, NT, D])
        st = sb("e_st", [P, NT, 6])
        mv = sb("e_mv", [P, NT, 2])
        m2 = sb("e_m2", [P, NT])
        sd = sb("e_sd", [P, NT])
        xrT = sb("e_xrT", [P, KC, T])
        spare = sb("e_spare", [P, 1])
        ps_t = ctx.enter_context(nc.psum_tensor("e_ps_t", [P, 2, HALF], F32))
        ps_k = ctx.enter_context(nc.psum_tensor("e_ps_k", [P, 2, HALF], F32))
        consts = sem("e_consts")
        km_ready = sem("e_km_ready")
        km_copied = sem("e_km_copied")
        x_in = [sem(f"e_x_in{u}") for u in range(2)]
        xr_out = sem("e_xr_out")
        chain = sem("e_chain")
        dev_in = sem("e_dev_in")
        sd_ready = sem("e_sd_ready")
        z_ready = sem("e_z_ready")
        tr_ready = sem("e_tr_ready")
        tr_used = sem("e_tr_used")
        block = ctx.enter_context(nc.Block())
        NG = KC * NT // 4
        CH = 7

        @block.sync
        def _(sp):
            sp.dma_start(ident[:, :], a["ident"]).then_inc(consts, 16)
            with nc.allow_non_contiguous_dma(reason="short per-channel vector"):
                sp.dma_start(nw[:, :], a["f_nw"].rearrange("(c p) -> p c", p=P)).then_inc(consts, 16)
            sp.dma_start(eps[:, :], a["eps"]).then_inc(consts, 16)
            sp.sem_inc(xr_out, DMA_AHEAD)

            def load(b, slot):
                sp.dma_start(xt[:, slot, :, :], x2f[b, :, :, :]).then_inc(x_in[slot], 16)

            def store(b):
                sp.wait_ge(tr_used, b * NG + NG)
                sp.dma_start(xr_s[:, bass.ds(b * T, T)].rearrange("(c p) n -> p c n", p=P), xrT[:, :, :]).then_inc(xr_out, 16)

            for slot in range(2):
                load(slot, slot)
            with sp.Fori(0, B // 2 - 1) as r:
                for slot in range(2):
                    store(r * 2 + slot)
                    load(r * 2 + (slot + 2), slot)
            for slot in range(2):
                store(B - 2 + slot)
            sp.wait_ge(xr_out, B * 16 + DMA_AHEAD)

        @block.vector
        def _(dve):
            dve.wait_ge(consts, 48)
            def round(r, slot):
                b = r * 2 + slot
                steps = [0]

                def then(ins):
                    steps[0] += 1
                    ins.then_inc(chain, 1)
                    dve.wait_ge(chain, b * CH + steps[0])

                def stats():
                    for i in range(NT):
                        last = nc.vector.bn_stats(st[:, i, :], xt[:, slot, i, :])
                    then(last)
                    nc.vector.memset(spare[:, :], 0.0)
                    for i in range(NT):
                        last = nc.vector.bn_aggr(mv[:, i, :], st[:, i, :])
                    return last

                dve.wait_ge(x_in[slot], r * 16 + 16)
                stats().then_inc(dev_in, 1)
                dve.wait_ge(sd_ready, b * 2 + 1)
                then(nc.vector.reciprocal(sd[:, :], sd[:, :]))
                for i in range(NT):
                    last = nc.vector.tensor_scalar(xt[:, slot, i, :], xt[:, slot, i, :], mv[:, i, 0:1], sd[:, i:i + 1], ALU.subtract, ALU.mult)
                then(last)
                then(stats())
                then(nc.vector.tensor_tensor(m2[:, :], mv[:, :, 0], mv[:, :, 0], ALU.mult))
                nc.vector.tensor_tensor(m2[:, :], m2[:, :], mv[:, :, 1], ALU.add).then_inc(dev_in, 1)
                dve.wait_ge(sd_ready, b * 2 + 2)
                then(nc.vector.reciprocal(sd[:, :], sd[:, :]))
                assert steps[0] == CH, steps
                for i in range(NT):
                    last = nc.vector.tensor_scalar(xt[:, slot, i, :], xt[:, slot, i, :], sd[:, i:i + 1], None, ALU.mult)
                last.then_inc(z_ready, 1)
                for g in range(NG):
                    if g == 0:
                        dve.wait_ge(xr_out, b * 16 + DMA_AHEAD)
                    dve.wait_ge(tr_ready, b * NG + (g + 1))
                    nc.vector.tensor_scalar(xrT[:, g // 2, (g % 2) * HALF:(g % 2 + 1) * HALF], ps_t[:, g % 2, :],
                                            nw[:, g // 2:g // 2 + 1], None, ALU.mult).then_inc(tr_used, 1)

            with dve.Fori(0, B // 2) as r:
                for slot in range(2):
                    round(r, slot)

        @block.scalar
        def _(act):
            act.wait_ge(consts, 48)
            for n in range(KC * 2):
                c, hf = n // 2, n % 2
                act.wait_ge(km_ready, n + 1)
                nc.scalar.copy(km[:, c, hf * HALF:(hf + 1) * HALF], ps_k[:, n % 2, :]).then_inc(km_copied, 1)
            with act.Fori(0, B) as b:
                act.wait_ge(dev_in, b * 2 + 1)
                nc.scalar.activation(sd[:, :], mv[:, :, 1], ACT.Sqrt, bias=eps[:, 0:1]).then_inc(sd_ready, 1)
                act.wait_ge(dev_in, b * 2 + 2)
                nc.scalar.activation(sd[:, :], m2[:, :], ACT.Sqrt, bias=eps[:, 0:1]).then_inc(sd_ready, 1)

        @block.tensor
        def _(pe):
            pe.wait_ge(consts, 48)
            pe.wait_ge(tables_in, TABLES * 16)
            for n in range(KC * 2):
                c, hf = n // 2, n % 2
                if n >= 2:
                    pe.wait_ge(km_copied, n - 1)
                for g in range(GS // 2):
                    mm = nc.tensor.matmul(ps_k[:, n % 2, g * NK:(g + 1) * NK], wqk[:, hf * (GS // 2) + g, c * P:(c + 1) * P],
                                          keysT[:, hf * (GS // 2) + g, :], start=True, stop=True)
                mm.then_inc(km_ready, 1)

            def round(r, slot):
                b = r * 2 + slot
                pe.wait_ge(z_ready, b + 1)
                for g in range(NG):
                    c, i0 = g // 2, 4 * (g % 2)
                    if g >= 2:
                        pe.wait_ge(tr_used, b * NG + (g - 1))
                    for i in range(4):
                        mm = nc.tensor.transpose(ps_t[:, g % 2, i * P:(i + 1) * P], xt[:, slot, i0 + i, c * P:(c + 1) * P], ident[:, :])
                    mm.then_inc(tr_ready, 1)

            with pe.Fori(0, B // 2) as r:
                for slot in range(2):
                    round(r, slot)


def experts(nc, a, x2, xr_s, out, km, dn, up):
    NK = 64
    NC = 32
    FH = 8
    K = 16
    GS = 2 * FH
    NP0, NP1, NP2 = K, 7 * 8, 8
    NP = NP0 + NP1 + NP2
    LOW = -3e38
    with ExitStack() as ctx:
        def sb(name, shape, dt=F32):
            return ctx.enter_context(nc.sbuf_tensor(name, shape, dt))

        def sem(name):
            return ctx.enter_context(nc.semaphore(name))

        def pb(name, shape):
            return ctx.enter_context(nc.psum_tensor(name, shape, F32))

        ident = sb("f_ident", [P, P])
        iota = sb("f_iota", [P, NC, P], BF16)
        iota16 = sb("f_iota16", [P, K], BF16)
        xs = sb("f_xs", [P, KC, P])
        xh = sb("f_xh", [P, KC, P])
        x2t = sb("f_x2", [P, D])
        y = sb("f_y", [P, D])
        sim = sb("f_sim", [P, GS, NK])
        top = sb("f_top", [P, FH, 2, K])
        topi = sb("f_topi", [P, GS, K], U32)
        topf = sb("f_topf", [P, FH, 2, K], BF16)
        cand = sb("f_cand", [P, FH, NP])
        val = sb("f_val", [P, FH, K])
        ci = sb("f_ci", [P, FH * K], U32)
        cg = sb("f_cg", [P, FH * K], U32)
        cf = sb("f_cf", [P, 8, FH * K])
        ab = sb("f_ab", [P, 2, FH * K], BF16)
        isel = sb("f_isel", [P, 2, FH * K])
        hi = sb("f_hi", [P, FH * K])
        pick = sb("f_pick", [P, 3, FH * K])
        pickT = sb("f_pickT", [P, 2, P], BF16)
        rowT = sb("f_rowT", [P, P // NC, P], BF16)
        wf = sb("f_wf", [P, P])
        wr = sb("f_wr", [P, P])
        wpart = sb("f_wpart", [P, 3, P], BF16)
        rowhot = sb("f_rowhot", [P, P, P], BF16)
        colhot = sb("f_colhot", [P, NC, P], BF16)
        eq = colhot[:, :, :].rearrange("p c n -> p (c n)").rearrange("p (s h k j) -> p s h k j", s=2, h=FH, k=K)
        colw = sb("f_colw", [P, 3, NC, P], BF16)
        gel = sb("f_gel", [P, NC, P])
        wd = sb("f_wd", [P, NC, P])
        spare = sb("f_spare", [P, 1])
        ps_s = pb("f_ps_s", [P, 2, HALF])
        ps_x = pb("f_ps_x", [P, HALF])
        ps_h = pb("f_ps_h", [P, 2, HALF])
        ps_w = pb("f_ps_w", [P, 2, HALF])
        ps_y = pb("f_ps_y", [P, HALF])

        consts = sem("f_consts")
        xs_in = sem("f_xs_in")
        xh_in = sem("f_xh_in")
        x2_in = sem("f_x2_in")
        y_out = sem("f_y_out")
        sim_ready = sem("f_sim_ready")
        sim_copied = sem("f_sim_copied")
        chain = sem("f_chain")
        pick_ready = sem("f_pick_ready")
        pickT_ready = sem("f_pickT_ready")
        pickT_copied = sem("f_pickT_copied")
        hot_parts = sem("f_hot_parts")
        hot_ready = sem("f_hot_ready")
        h_ready = sem("f_h_ready")
        gel_done = sem("f_gel_done")
        w_ready = sem("f_w_ready")
        w_copied = sem("f_w_copied")
        gw_ready = sem("f_gw_ready")
        y_ready = sem("f_y_ready")
        y_done = sem("f_y_done")

        NH, NW, NG = NC // 4, P // 16, 4
        block = ctx.enter_context(nc.Block())

        @block.sync
        def _(sp):
            for dst, src in ((ident[:, :], a["ident"]), (iota[:, :, :], a["f_iota"]), (iota16[:, :], a["f_iota16"])):
                sp.dma_start(dst, src).then_inc(consts, 16)

            def cols(t):
                return xr_s[:, bass.ds(t * P, P)].rearrange("(c p) n -> p c n", p=P)

            sp.dma_start(xs[:, :, :], cols(0)).then_inc(xs_in, 16)

            def tile(t, first=False, second=False, last=False):
                if not first:
                    sp.wait_ge(h_ready, t * NH)
                sp.dma_start(xh[:, :, :], cols(t)).then_inc(xh_in, 16)
                if not last:
                    sp.wait_ge(sim_ready, t + 1)
                    sp.dma_start(xs[:, :, :], cols(t + 1)).then_inc(xs_in, 16)
                if first:
                    sp.dma_start(x2t[:, :], x2[0:P, :]).then_inc(x2_in, 16)
                elif not second:
                    store(t - 2)

            def store(t):
                sp.wait_ge(y_done, t + 1)
                sp.dma_start(out[bass.ds(t * P, P), :], y[:, :]).then_inc(y_out, 16)
                if not isinstance(t, int) or t < TILES - 1:
                    sp.dma_start(x2t[:, :], x2[bass.ds(t * P + P, P), :]).then_inc(x2_in, 16)

            tile(0, first=True)
            tile(1, second=True)
            with sp.Fori(2, TILES - 1) as t:
                tile(t)
            tile(TILES - 1, last=True)
            store(TILES - 2)
            store(TILES - 1)
            sp.wait_ge(y_out, TILES * 16)

        @block.tensor
        def _(pe):
            def key_scores(t):
                pe.wait_ge(xs_in, t * 16 + 16)
                if not isinstance(t, int) or t > 0:
                    pe.wait_ge(sim_copied, t * 2)
                for hf in range(2):
                    for k in range(KC):
                        mm = nc.tensor.matmul(ps_s[:, hf, :], xs[:, k, :], km[:, k, hf * HALF:(hf + 1) * HALF],
                                              start=(k == 0), stop=(k == KC - 1))
                mm.then_inc(sim_ready, 1)

            def result(t):
                pe.wait_ge(gw_ready, t * NG + 1)
                if not isinstance(t, int) or t > 0:
                    pe.wait_ge(y_done, t)
                for c in range(NC):
                    if c % (NC // NG) == 0 and c > 0:
                        pe.wait_ge(gw_ready, t * NG + (c // (NC // NG) + 1))
                    mm = nc.tensor.matmul(ps_y[:, 0:D], wd[:, c, :], up[:, c, :], start=(c == 0), stop=(c == NC - 1))
                mm.then_inc(y_ready, 1)

            def tile(t, first=False, last=False):
                pe.wait_ge(xh_in, t * 16 + 16)
                for g in range(NH):
                    if g == NH // 2:
                        pe.wait_ge(pick_ready, t + 1)
                        for n in range(3):
                            mm = nc.tensor.transpose(ps_x[:, n * P:(n + 1) * P], pick[:, n, :], ident[:, :])
                        mm.then_inc(pickT_ready, 1)
                        if not last:
                            key_scores(t + 1)
                    if not (first and g < 2):
                        pe.wait_ge(gel_done, t * NH + (g - 1))
                    for j in range(4):
                        for k in range(KC):
                            mm = nc.tensor.matmul(ps_h[:, g % 2, j * P:(j + 1) * P], dn[:, k, (4 * g + j) * P:(4 * g + j + 1) * P],
                                                  xh[:, k, :], start=(k == 0), stop=(k == KC - 1))
                    mm.then_inc(h_ready, 1)
                if not first:
                    result(t - 1)
                pe.wait_ge(hot_ready, t * 4 + 4)
                for g in range(NW):
                    if not (first and g < 2):
                        pe.wait_ge(w_copied, t * NW + (g - 1))
                    for j in range(16):
                        tok = 16 * g + j
                        for n in range(3):
                            mm = nc.tensor.matmul(ps_w[:, g % 2, j * NC:(j + 1) * NC], rowhot[:, :, tok], colw[:, n, :, tok],
                                                  start=(n == 0), stop=(n == 2))
                    mm.then_inc(w_ready, 1)

            pe.wait_ge(consts, 3 * 16)
            key_scores(0)
            tile(0, first=True)
            with pe.Fori(1, TILES - 1) as t:
                tile(t)
            tile(TILES - 1, last=True)
            result(TILES - 1)

        @block.scalar
        def _(act):
            def copy_scores(t):
                act.wait_ge(sim_ready, t + 1)
                if not isinstance(t, int) or t > 0:
                    act.wait_ge(pick_ready, t)
                for hf in range(2):
                    nc.scalar.copy(sim[:, hf * FH:(hf + 1) * FH, :].rearrange("p g k -> p (g k)"), ps_s[:, hf, :]).then_inc(sim_copied, 1)

            def tile(t, first=False, last=False):
                for g in range(NH):
                    if g == NH // 2:
                        act.wait_ge(pickT_ready, t + 1)
                        nc.scalar.copy(pickT[:, :, :].rearrange("p a n -> p (a n)"), ps_x[:, 0:2 * P]).then_inc(pickT_copied, 1)
                        nc.scalar.copy(wf[:, :], ps_x[:, 2 * P:3 * P]).then_inc(pickT_copied, 1)
                        if not last:
                            copy_scores(t + 1)
                    if not first and g % 2 == 0:
                        act.wait_ge(gw_ready, t * NG - NG + (g // 2 + 1))
                    act.wait_ge(h_ready, t * NH + (g + 1))
                    nc.scalar.activation(gel[:, 4 * g:4 * g + 4, :].rearrange("p c n -> p (c n)"), ps_h[:, g % 2, :], ACT.Gelu).then_inc(gel_done, 1)
                for g in range(NW):
                    if g == 0 and not first:
                        act.wait_ge(y_ready, t)
                    act.wait_ge(w_ready, t * NW + (g + 1))
                    nc.scalar.copy(wd[:, :, 16 * g:16 * g + 16].rearrange("p c n -> p n c"),
                                   ps_w[:, g % 2, :].rearrange("p (n c) -> p n c", c=NC)).then_inc(w_copied, 1)

            copy_scores(0)
            tile(0, first=True)
            with act.Fori(1, TILES - 1) as t:
                tile(t)
            tile(TILES - 1, last=True)

        @block.vector
        def _(dve):
            CH = 24

            def wide(v, n):
                return v.unsqueeze(3).to_broadcast([P, v.shape[1], v.shape[2], n])

            def tile(t, first=False, second=False):
                steps = [0]

                def then(ins, carry=False):
                    steps[0] += 1
                    ins.then_inc(chain, 1)
                    dve.wait_ge(chain, t * CH + steps[0])
                    if carry:
                        nc.vector.memset(spare[:, :], 0.0)

                TT, TS, STT = nc.vector.tensor_tensor, nc.vector.tensor_scalar, nc.vector.scalar_tensor_tensor
                top2 = top[:, :, :, :].rearrange("p h s k -> p (h s) k")
                dve.wait_ge(sim_copied, t * 2 + 2)
                nc.vector.memset(spare[:, :], 0.0)
                for g in range(GS):
                    last = nc.vector.max(top2[:, g, 0:8], sim[:, g, :])
                then(last, carry=True)
                for g in range(GS):
                    nc.vector.max_index(topi[:, g, 0:8], top2[:, g, 0:8], sim[:, g, :])
                    last = nc.vector.match_replace(sim[:, g, :], top2[:, g, 0:8], sim[:, g, :], LOW)
                then(last, carry=True)
                for g in range(GS):
                    last = nc.vector.max(top2[:, g, 8:16], sim[:, g, :])
                then(last, carry=True)
                for g in range(GS):
                    last = nc.vector.max_index(topi[:, g, 8:16], top2[:, g, 8:16], sim[:, g, :])
                then(last)
                nc.vector.tensor_copy(topf[:, :, :, :].rearrange("p h s k -> p (h s) k"), topi[:, :, :])
                s1, s2 = top[:, :, 0, :], top[:, :, 1, :]
                TT(cand[:, :, 0:NP0], s1[:, :, 0:1].to_broadcast([P, FH, K]), s2, ALU.add)
                TT(cand[:, :, NP0:NP0 + NP1].rearrange("p h (a b) -> p h a b", b=8), wide(s1[:, :, 1:8], 8),
                   s2[:, :, 0:8].unsqueeze(2).to_broadcast([P, FH, 7, 8]), ALU.add)
                then(TT(cand[:, :, NP0 + NP1:NP], s1[:, :, 8:16], s2[:, :, 0:1].to_broadcast([P, FH, 8]), ALU.add), carry=True)
                civ = ci[:, :].rearrange("p (h k) -> p h k", k=K)
                for h in range(FH):
                    last = nc.vector.max(val[:, h, 0:8], cand[:, h, :])
                then(last, carry=True)
                for h in range(FH):
                    nc.vector.max_index(civ[:, h, 0:8], val[:, h, 0:8], cand[:, h, :])
                    last = nc.vector.match_replace(cand[:, h, :], val[:, h, 0:8], cand[:, h, :], LOW)
                then(last, carry=True)
                for h in range(FH):
                    last = nc.vector.max(val[:, h, 8:16], cand[:, h, :])
                then(last, carry=True)
                for h in range(FH):
                    last = nc.vector.max_index(civ[:, h, 8:16], val[:, h, 8:16], cand[:, h, :])
                then(last)
                c_f, g_f, e_f, g1, lo, g8, be = (cf[:, n, :] for n in range(7))
                nc.vector.tensor_copy(c_f, ci[:, :])
                then(TS(cg[:, :], ci[:, :], 3, None, ALU.logical_shift_right))
                then(nc.vector.tensor_copy(g_f, cg[:, :]))
                TS(e_f, c_f, -float(NP0 + NP1), 0.0, ALU.add, ALU.max)
                TS(g1, g_f, -1.0, 0.0, ALU.add, ALU.max)
                TS(g8, g_f, 1.0, 8.0, ALU.is_equal, ALU.mult)
                then(STT(out=lo, in0=g_f, scalar=-8.0, in1=c_f, op0=ALU.mult, op1=ALU.add))
                TT(ab[:, 0, :], g1, e_f, ALU.add)
                then(TT(be, lo, e_f, ALU.subtract))
                then(TT(ab[:, 1, :], be, g8, ALU.add))
                if not first:
                    dve.wait_ge(hot_ready, t * 4)
                for s in range(2):
                    r = ab[:, s, :].rearrange("p (h k) -> p h k", k=K)
                    last = TT(eq[:, s], wide(r, K), iota16[:, :].unsqueeze(1).to_broadcast([P, FH * K, K])
                              .rearrange("p (h k) j -> p h k j", k=K), ALU.is_equal)
                then(last)
                for s in range(2):
                    last = TT(eq[:, s], eq[:, s], topf[:, :, s, :].unsqueeze(2).to_broadcast([P, FH, K, K]), ALU.mult)
                then(last)
                eqv = colhot[:, :, :].rearrange("p c n -> p (c n)").rearrange("p (a j) -> p a j", j=K)
                then(TT(eqv[:, :, 0:8], eqv[:, :, 0:8], eqv[:, :, 8:16], ALU.add))
                then(TT(eqv[:, :, 0:4], eqv[:, :, 0:4], eqv[:, :, 4:8], ALU.add))
                then(nc.vector.tensor_reduce(isel[:, :, :].rearrange("p s n -> p (s n)"), eqv[:, :, 0:4], AX_X, ALU.add))
                then(TS(hi[:, :], isel[:, 1, :], float(NC), None, ALU.is_ge))
                STT(out=pick[:, 0, :], in0=hi[:, :], scalar=float(NK), in1=isel[:, 0, :], op0=ALU.mult, op1=ALU.add)
                STT(out=pick[:, 1, :], in0=hi[:, :], scalar=-float(NC), in1=isel[:, 1, :], op0=ALU.mult, op1=ALU.add)
                TS(pick[:, 2, :], val[:, :, :].rearrange("p h k -> p (h k)"), 0.0, None, ALU.max).then_inc(pick_ready, 1)
                if not (first or second):
                    total(t - 2)
                dve.wait_ge(pickT_copied, t * 2 + 2)
                if not first:
                    dve.wait_ge(w_ready, t * NW)
                then(nc.vector.tensor_copy(wpart[:, 0, :], wf[:, :]))
                TT(colhot[:, :, :], iota[:, 0:NC, :], pickT[:, 1:2, :].to_broadcast([P, NC, P]), ALU.is_equal).then_inc(hot_parts, 1)
                then(TT(wr[:, :], wf[:, :], wpart[:, 0, :], ALU.subtract))
                then(nc.vector.tensor_copy(wpart[:, 1, :], wr[:, :]))
                TT(wpart[:, 2, :], wr[:, :], wpart[:, 1, :], ALU.subtract).then_inc(hot_parts, 1)
                for n in range(P // NC):
                    last = TS(rowT[:, n, :], pickT[:, 0, :], -float(NC * n), None, ALU.add)
                then(last)
                for n in range(P // NC):
                    last = TT(rowhot[:, NC * n:NC * (n + 1), :], iota[:, :, :], rowT[:, n:n + 1, :].to_broadcast([P, NC, P]), ALU.is_equal)
                last.then_inc(hot_ready, 1)
                assert steps[0] == CH, steps

            def total(t):
                dve.wait_ge(x2_in, t * 16 + 16)
                if not isinstance(t, int) or t > 0:
                    dve.wait_ge(y_out, t * 16)
                dve.wait_ge(y_ready, t + 1)
                nc.vector.tensor_tensor(y[:, :], ps_y[:, 0:D], x2t[:, :], ALU.add).then_inc(y_done, 1)

            dve.wait_ge(consts, 3 * 16)
            tile(0, first=True)
            tile(1, second=True)
            with dve.Fori(2, TILES) as t:
                tile(t)
            total(TILES - 2)
            total(TILES - 1)

        @block.gpsimd
        def _(pool):
            def product(t):
                pool.wait_ge(gel_done, t * NH + NH)
                pool.wait_ge(w_copied, t * NW + NW)
                for n in range(NG):
                    cols = slice(n * (NC // NG), (n + 1) * (NC // NG))
                    nc.gpsimd.tensor_tensor(wd[:, cols, :], gel[:, cols, :], wd[:, cols, :], ALU.mult).then_inc(gw_ready, 1)

            def tile(t, first=False):
                if not first:
                    product(t - 1)
                for n in range(3):
                    if n < 2:
                        pool.wait_ge(hot_parts, t * 2 + (n + 1))
                    nc.gpsimd.tensor_tensor(colw[:, n], colhot[:, :, :], wpart[:, n:n + 1, :].to_broadcast([P, NC, P]),
                                            ALU.mult).then_inc(hot_ready, 1)

            tile(0, first=True)
            with pool.Fori(1, TILES) as t:
                tile(t)
            product(TILES - 1)


def build(nc, a, out):
    qu_s, qv_s, k_s = (nc.dram_tensor(n, [3, H * DH, N], BF16).ap() for n in ("qu_s", "qv_s", "k_s"))
    v_s = nc.dram_tensor("v_s", [N, 3 * D], BF16).ap()
    wp_s = nc.dram_tensor("wp_s", [3, H * DH, D], BF16).ap()
    ctx_s = nc.dram_tensor("ctx_s", [N, D], F32).ap()
    x1 = nc.dram_tensor("x1_s", [N, D], F32).ap()
    x2 = nc.dram_tensor("x2_s", [N, D], F32).ap()
    xr_s = nc.dram_tensor("xr_s", [D, N], F32).ap()
    project_qkv(nc, a["x"], a["attn_w"], a["attn_vecs"], a["attn_bv"], a["ident"], a["eps"], a["attn_wpos"], qu_s, qv_s, k_s, v_s, wp_s)
    self_attention(nc, a["trig"], a["ident"], qu_s, qv_s, k_s, v_s, wp_s, ctx_s)
    project_out(nc, a["x"], a["ident"], a["attn_woT"], a["attn_bo"], ctx_s, x1)
    with ExitStack() as held:
        dn = held.enter_context(nc.sbuf_tensor("g_dn", [P, KC, 32 * P], F32))
        up = held.enter_context(nc.sbuf_tensor("g_up", [P, 32, D], F32))
        km = held.enter_context(nc.sbuf_tensor("g_km", [P, KC, 16 * 64], F32))
        tables_in = held.enter_context(nc.semaphore("g_tables_in"))
        with ExitStack() as early:
            wqk = early.enter_context(nc.sbuf_tensor("g_wqT", [P, 16, D], F32))
            keysT = early.enter_context(nc.sbuf_tensor("g_keysT", [P, 16, 64], F32))

            def prefetch(sp):
                for dst, src in ((wqk[:, :, :], a["f_wqT"].rearrange("(g p) n -> p g n", p=P)), (keysT[:, :, :], a["f_keysT"]),
                                 (dn[:, :, :], a["f_dnT"].rearrange("(c p) n -> p c n", p=P)), (up[:, :, :], a["f_up"])):
                    sp.dma_start(dst, src).then_inc(tables_in, 16)

            cross_attention(nc, a, x1, x2, prefetch)
            ffn_norm(nc, a, x2, xr_s, wqk, keysT, km, tables_in)
        experts(nc, a, x2, xr_s, out.rearrange("b t d -> (b t) d"), km, dn, up)


def kernel(**inputs):
    import concourse.bacc as _bacc
    from concourse.bass_utils import run_bass_kernel_spmd as _run

    def arr(name):
        return np.asarray(inputs[name])

    m = np.arange(0, D, 2).astype(np.float32)
    div = np.exp(m * np.float32(-math.log(10000.0) / D)).astype(np.float64)
    ang = div[:, None] * np.arange(T)[None, :]
    trig = np.stack([np.sin(ang), np.cos(ang), np.sin(ang)], axis=1).astype(np.float32)

    def rows(v):
        return np.broadcast_to(v[None, :], (P, v.shape[0]))

    wpos = arr("L0_attn_Wpos")
    laid = {
        "x": arr("x"),
        "ident": np.eye(P, dtype=np.float32),
        "eps": np.full((P, 1), 1e-5, np.float32),
        "trig": trig,
        "attn_w": np.stack([arr("L0_attn_Wq").T, arr("L0_attn_Wk").T, arr("L0_attn_Wv").T]),
        "attn_vecs": np.stack([arr("L0_attn_bq"), arr("L0_attn_bk"), arr("L0_attn_u_bias").reshape(-1),
                               arr("L0_attn_v_bias").reshape(-1), arr("L0_attn_ln_gamma"), arr("L0_attn_ln_beta")]),
        "attn_bv": rows(arr("L0_attn_bv")),
        "attn_wpos": np.concatenate([wpos[:, 0::2], wpos[:, 1::2]], axis=1),
        "attn_woT": arr("L0_attn_Wout").T,
        "attn_bo": rows(arr("L0_attn_bout")),
        "f_nw": arr("L0_ffn_norm_w"),
        "f_iota": np.broadcast_to(np.arange(32, dtype=np.float32).astype(mybir.dt.np(BF16))[None, :, None], (P, 32, P)),
        "f_iota16": np.broadcast_to(np.arange(16, dtype=np.float32).astype(mybir.dt.np(BF16))[None], (P, 16)),
        "f_wqT": arr("L0_ffn_wq").T,
        "f_keysT": arr("L0_ffn_keys").transpose(3, 0, 2, 1).reshape(P, 16, 64),
        "f_dnT": arr("L0_ffn_expert_down").reshape(64, 2, 32, D).transpose(3, 2, 1, 0).reshape(D, 32 * P),
        "f_up": arr("L0_ffn_expert_up").reshape(64, 2, 32, D).transpose(1, 0, 2, 3).reshape(P, 32, D),
        "ctxT": arr("ctx_1024").transpose(0, 2, 1),
        "mask": np.broadcast_to(arr("mask_BxS2_bk0")[None], (P, B, S2)),
        "eps2": np.broadcast_to(np.array([1e-5, 1e-6], np.float32)[None], (P, 2)),
        "x_diag": (np.arange(P)[:, None] // DH == np.arange(P // DH)[None, :]).astype(np.float32),
        "x_wqT": arr("L0_xattn_Wq").T,
        "x_wkvT": arr("L0_xattn_Wkv").T,
        "x_woT": arr("L0_xattn_Wo").T,
        "x_rows": np.broadcast_to(np.stack([arr("L0_xattn_bq"), arr("L0_xattn_bkv")[:D], arr("L0_xattn_bkv")[D:],
                                            arr("L0_xattn_bo")])[None], (P, 4, D)),
        "x_lnw": np.tile(np.stack([arr("L0_xattn_qn_w"), arr("L0_xattn_qn_b"), arr("L0_xattn_kn_w"),
                                   arr("L0_xattn_kn_b")], axis=1), (P // DH, 1)),
    }
    nc = _bacc.Bacc("TRN2", target_bir_lowering=False, num_devices=1)
    arrays, aps = {}, {}
    for name, v in laid.items():
        v = np.ascontiguousarray(v)
        arrays[f"in_{name}_dram"] = v
        aps[name] = nc.dram_tensor(f"in_{name}_dram", v.shape, mybir.dt.from_np(v.dtype), kind="ExternalInput").ap()
    out = nc.dram_tensor("out_0_dram", (B, T, D), F32, kind="ExternalOutput").ap()
    build(nc, aps, out)
    r = _run(nc, [arrays], core_ids=[0])
    return r.results[0]["out_0_dram"]
```
